# Optimizing a Trainium2 kernel written in Bass

```python
import numpy as np
import jax
import jax.numpy as jnp

def _softmax(x, axis=-1):
    return jax.nn.softmax(x, axis=axis)

def _gelu(x):
    return jax.nn.gelu(x, approximate=True)

def _silu(x):
    return jax.nn.silu(x)

def _sigmoid(x):
    return jax.nn.sigmoid(x)

def _layernorm(x, axis=-1, eps=1e-05):
    m = jnp.mean(x, axis=axis, keepdims=True)
    v = jnp.var(x, axis=axis, keepdims=True)
    return (x - m) / jnp.sqrt(v + eps)

def _scatter_add(tgt, idx, src, axis=0):
    return tgt.at[idx].add(src)

def _segment_sum(src, seg, n):
    return jax.ops.segment_sum(src, seg, n)
kernel_name = 'mk_gnn_resnorm_d2_gnn_r8_bdb2ae'

def setup_inputs(seed: int=0):
    np.random.seed(seed)
    _w = jnp.asarray

    def _rec_inputs():
        import jax
        import jax.numpy as jnp
        _gk = jax.random.key(seed)
        x = -0.0002117 + 1 * jax.random.normal(jax.random.fold_in(_gk, 1), (1250, 512), jnp.float32)
        _s = jax.random.randint(jax.random.fold_in(_gk, 2), (10000,), 0, 1250, jnp.int32)
        _d = jax.random.randint(jax.random.fold_in(_gk, 3), (10000,), 0, 1250, jnp.int32)
        _loop = jnp.arange(1250, dtype=jnp.int32)
        src = jnp.concatenate([_s, _d, _loop])
        dst = jnp.concatenate([_d, _s, _loop])
        _o = jnp.argsort(dst, stable=True)
        src = src[_o]
        dst = dst[_o]
        edge_attr_128 = 0.000283511 + 1.00007 * jax.random.normal(jax.random.fold_in(_gk, 11), (21250, 128), jnp.float32)
        edge_attr_64 = -5.3897e-05 + 0.999841 * jax.random.normal(jax.random.fold_in(_gk, 12), (21250, 64), jnp.float32)
        return (x, src, dst, edge_attr_128, edge_attr_64)
    x, src, dst, edge_attr_128, edge_attr_64 = _rec_inputs()

    def _L0_gnn_setup():
        import jax, jax.numpy as jnp
        import numpy as np
        N, E, H, ED = (6250, 50000, 512, 64)
        BN_EPS = 1e-05

        def _bn(h, g, b):
            mu = jnp.mean(h, axis=0)
            var = jnp.mean(jnp.square(h - mu), axis=0)
            return (h - mu) * jax.lax.rsqrt(var + BN_EPS) * g + b
        key = jax.random.key(seed)
        ks = jax.random.split(key, 8)
        s = lambda d: 1.0 / np.sqrt(d)
        return {'x': jax.random.normal(ks[0], (N, H), jnp.float32), 'edge_attr': jax.random.normal(ks[1], (E, ED), jnp.float32), 'edge_index': jax.random.randint(ks[2], (2, E), 0, N, jnp.int32), 'W_e': jax.random.normal(ks[3], (ED, H), jnp.float32) * s(ED), 'b_e': jnp.zeros((H,), jnp.float32), 'W1': jax.random.normal(ks[4], (H, 2 * H), jnp.float32) * s(H), 'b1': jnp.zeros((2 * H,), jnp.float32), 'g1': jnp.ones((2 * H,), jnp.float32), 'beta1': jnp.zeros((2 * H,), jnp.float32), 'W2': jax.random.normal(ks[5], (2 * H, H), jnp.float32) * s(2 * H), 'b2': jnp.zeros((H,), jnp.float32), 'g2': jnp.ones((H,), jnp.float32), 'beta2': jnp.zeros((H,), jnp.float32), 'eps': jnp.zeros((), jnp.float32)}
    _L0_gnn_all = _L0_gnn_setup()
    _L0_gnn_in = {k: v for k, v in _L0_gnn_all.items() if k in ('W_e', 'b_e', 'W1', 'b1', 'g1', 'beta1', 'W2', 'b2', 'g2', 'beta2', 'eps')}
    del _L0_gnn_all

    def _L1_gnn_setup():
        import jax, jax.numpy as jnp
        import numpy as np
        N, E = (1250, 18750)
        HD, ED = (512, 128)
        BN_EPS = 1e-05
        key = jax.random.key(seed)
        ks = jax.random.split(key, 16)
        s = 0.02
        return {'h': jax.random.normal(ks[0], (N, HD), jnp.float32), 'edge_index': jax.random.randint(ks[1], (2, E), 0, N, jnp.int32), 'edge_attr': jax.random.normal(ks[2], (E, ED), jnp.float32), 'W1': jax.random.normal(ks[3], (HD, HD + ED), jnp.float32) * s, 'b1': jnp.zeros((HD,), jnp.float32), 'W2': jax.random.normal(ks[4], (HD, HD), jnp.float32) * s, 'b2': jnp.zeros((HD,), jnp.float32), 'W_ih': jax.random.normal(ks[5], (3 * HD, HD), jnp.float32) * s, 'W_hh': jax.random.normal(ks[6], (3 * HD, HD), jnp.float32) * s, 'b_ih': jnp.zeros((3 * HD,), jnp.float32), 'b_hh': jnp.zeros((3 * HD,), jnp.float32), 'gamma': jnp.ones((HD,), jnp.float32), 'beta': jnp.zeros((HD,), jnp.float32), 'run_mean': jnp.zeros((HD,), jnp.float32), 'run_var': jnp.ones((HD,), jnp.float32)}
    _L1_gnn_all = _L1_gnn_setup()
    _L1_gnn_in = {k: v for k, v in _L1_gnn_all.items() if k in ('W1', 'b1', 'W2', 'b2', 'W_ih', 'W_hh', 'b_ih', 'b_hh', 'gamma', 'beta', 'run_mean', 'run_var')}
    del _L1_gnn_all
    return {'x': x, 'src': src, 'dst': dst, 'edge_attr_128': edge_attr_128, 'edge_attr_64': edge_attr_64, 'L0_gnn_W_e': _L0_gnn_in['W_e'], 'L0_gnn_b_e': _L0_gnn_in['b_e'], 'L0_gnn_W1': _L0_gnn_in['W1'], 'L0_gnn_b1': _L0_gnn_in['b1'], 'L0_gnn_g1': _L0_gnn_in['g1'], 'L0_gnn_beta1': _L0_gnn_in['beta1'], 'L0_gnn_W2': _L0_gnn_in['W2'], 'L0_gnn_b2': _L0_gnn_in['b2'], 'L0_gnn_g2': _L0_gnn_in['g2'], 'L0_gnn_beta2': _L0_gnn_in['beta2'], 'L0_gnn_eps': _L0_gnn_in['eps'], 'L1_gnn_W1': _L1_gnn_in['W1'], 'L1_gnn_b1': _L1_gnn_in['b1'], 'L1_gnn_W2': _L1_gnn_in['W2'], 'L1_gnn_b2': _L1_gnn_in['b2'], 'L1_gnn_W_ih': _L1_gnn_in['W_ih'], 'L1_gnn_W_hh': _L1_gnn_in['W_hh'], 'L1_gnn_b_ih': _L1_gnn_in['b_ih'], 'L1_gnn_b_hh': _L1_gnn_in['b_hh'], 'L1_gnn_gamma': _L1_gnn_in['gamma'], 'L1_gnn_beta': _L1_gnn_in['beta'], 'L1_gnn_run_mean': _L1_gnn_in['run_mean'], 'L1_gnn_run_var': _L1_gnn_in['run_var']}

def reference(x, src, dst, edge_attr_128, edge_attr_64, L0_gnn_W_e, L0_gnn_b_e, L0_gnn_W1, L0_gnn_b1, L0_gnn_g1, L0_gnn_beta1, L0_gnn_W2, L0_gnn_b2, L0_gnn_g2, L0_gnn_beta2, L0_gnn_eps, L1_gnn_W1, L1_gnn_b1, L1_gnn_W2, L1_gnn_b2, L1_gnn_W_ih, L1_gnn_W_hh, L1_gnn_b_ih, L1_gnn_b_hh, L1_gnn_gamma, L1_gnn_beta, L1_gnn_run_mean, L1_gnn_run_var):
    import jax
    import jax.numpy as jnp

    def _L0_gnn_ref(x, edge_attr, edge_index, W_e, b_e, W1, b1, g1, beta1, W2, b2, g2, beta2, eps):
        import jax, jax.numpy as jnp
        import numpy as np
        N, E, H, ED = (6250, 50000, 512, 64)
        BN_EPS = 1e-05

        def _bn(h, g, b):
            mu = jnp.mean(h, axis=0)
            var = jnp.mean(jnp.square(h - mu), axis=0)
            return (h - mu) * jax.lax.rsqrt(var + BN_EPS) * g + b
        src, dst = (edge_index[0], edge_index[1])
        msg = jax.nn.relu(x[src] + edge_attr @ W_e + b_e)
        aggr = jax.ops.segment_sum(msg, dst, num_segments=x.shape[0])
        h = (1.0 + eps) * x + aggr
        h = jax.nn.silu(_bn(h @ W1 + b1, g1, beta1))
        h = h @ W2 + b2
        return jax.nn.silu(_bn(h, g2, beta2))

    def _L1_gnn_ref(h, edge_index, edge_attr, W1, b1, W2, b2, W_ih, W_hh, b_ih, b_hh, gamma, beta, run_mean, run_var):
        import jax, jax.numpy as jnp
        import numpy as np
        N, E = (1250, 18750)
        HD, ED = (512, 128)
        BN_EPS = 1e-05
        src, dst = (edge_index[0], edge_index[1])
        m_in = jnp.concatenate([h[src], edge_attr], axis=1)
        m = jax.nn.relu(m_in @ W1.T + b1) @ W2.T + b2
        agg = jax.ops.segment_sum(m, dst, num_segments=h.shape[0])
        gi = agg @ W_ih.T + b_ih
        gh = h @ W_hh.T + b_hh
        i_r, i_z, i_n = jnp.split(gi, 3, axis=1)
        h_r, h_z, h_n = jnp.split(gh, 3, axis=1)
        r = jax.nn.sigmoid(i_r + h_r)
        z = jax.nn.sigmoid(i_z + h_z)
        n = jnp.tanh(i_n + r * h_n)
        h_new = (1.0 - z) * n + z * h
        bn = gamma * (h_new - run_mean) * jax.lax.rsqrt(run_var + BN_EPS) + beta
        return h + bn
    edge_index = jnp.stack([src, dst])
    x = _layernorm(x + _L0_gnn_ref(x, edge_attr_64, edge_index, L0_gnn_W_e, L0_gnn_b_e, L0_gnn_W1, L0_gnn_b1, L0_gnn_g1, L0_gnn_beta1, L0_gnn_W2, L0_gnn_b2, L0_gnn_g2, L0_gnn_beta2, L0_gnn_eps), axis=-1)
    x = _layernorm(x + _L1_gnn_ref(x, edge_index, edge_attr_128, L1_gnn_W1, L1_gnn_b1, L1_gnn_W2, L1_gnn_b2, L1_gnn_W_ih, L1_gnn_W_hh, L1_gnn_b_ih, L1_gnn_b_hh, L1_gnn_gamma, L1_gnn_beta, L1_gnn_run_mean, L1_gnn_run_var), axis=-1)
    return x

_drawn_inputs = setup_inputs


def setup_inputs(seed=0):
    import zlib

    import numpy as np

    out = dict(_drawn_inputs(seed))
    spreads = {'L0_gnn_b_e': (0.0, 0.1),
     'L0_gnn_b1': (0.0, 0.8),
     'L0_gnn_g1': (1.0, 0.2),
     'L0_gnn_beta1': (0.0, 0.1),
     'L0_gnn_b2': (0.0, 0.8),
     'L0_gnn_g2': (1.0, 0.2),
     'L0_gnn_beta2': (0.0, 0.1),
     'L1_gnn_b1': (0.0, 0.1),
     'L1_gnn_b2': (0.0, 0.1),
     'L1_gnn_b_ih': (0.0, 0.456),
     'L1_gnn_b_hh': (0.0, 0.613),
     'L1_gnn_gamma': (1.0, 0.2),
     'L1_gnn_beta': (0.0, 0.1),
     'L1_gnn_run_mean': (0.0, 0.1),
     'L1_gnn_run_var': (1.0, 0.575)}
    factors = {}
    for name, (base, spread) in spreads.items():
        noise = np.random.default_rng([zlib.crc32(name.encode()), seed]).standard_normal(out[name].shape)
        drawn = base * np.exp(spread * noise) if base else spread * noise
        out[name] = jnp.asarray(drawn.astype(out[name].dtype))
    for name, factor in factors.items():
        out[name] = (out[name] * factor).astype(out[name].dtype)
    return out
```

```python
from contextlib import ExitStack

import concourse.bass as bass
from concourse import mybir

F32 = mybir.dt.float32
F32R = mybir.dt.float32r
I32 = mybir.dt.int32
ALU = mybir.AluOpType
ACT = mybir.ActivationFunctionType

P = 128
N, E, D = 1250, 21250, 512
ED0, ED1 = 64, 128
H0 = 2 * D
EPS = 1e-5
KD = D // P
KH = H0 // P

GROUP = 12
TILES = -(-E // (P * 2 * GROUP)) * 2 * GROUP
GROUPS = TILES // GROUP
STEP = 2 * GROUP
STEPS = TILES // STEP
CHUNK = 4
ROWS = (-(-N // P) + 1) * P
BLOCKS = -(-N // P)

GATH, EPS_BANKS, MSG, HOT, RING = 6, 4, 4, 4, 3
LAG = 3

NODE_CHUNKS = [(0, 418), (418, 416), (834, 416)]
COLS = {}
for _name, _k in (("b1", KH), ("g1", KH), ("beta1", KH), ("b2", KD), ("g2", KD), ("beta2", KD),
                  ("b_ih", 3 * KD), ("b_hh", 3 * KD), ("gamma", KD), ("beta", KD),
                  ("run_mean", KD), ("run_var", KD), ("eps", 1)):
    COLS[_name] = (sum(w for _, w in COLS.values()), _k)
NCOLS = sum(w for _, w in COLS.values())

KB = 1024


def rows_in(block):
    return min(P, N - block * P)


def gnn_program(nc, x, src, dst, attr0, attr1, W_e, b_e, W1, W2, V1h, V1e, v_b1, V2, v_b2, Wg, cols, out):
    with ExitStack() as ctx:
        base = -(-nc.sbuf_base // 64) * 64
        A0 = base + 10 * KB + KB // 2
        B0 = A0 + 64 * KB

        def at(name, shape, dt, offset):
            return nc.alloc_sbuf_tensor_at(name, shape, dt, offset=offset)

        def sem(name):
            return ctx.enter_context(nc.semaphore(name))

        def psum(name, shape):
            return ctx.enter_context(nc.psum_tensor(name, shape, F32))

        small = [base]

        def keep(name, width, dt=F32, parts=P):
            t = at(name, [parts, width], dt, small[0])
            small[0] += -(-width * 4 // 64) * 64
            assert small[0] <= A0, name
            return t

        src_sb = keep("src_sb", TILES, I32)
        dst_i = keep("dst_i", TILES, I32)
        dst_f = keep("dst_f", TILES)
        in_window = keep("in_window", TILES)
        dst_left = keep("dst_left", TILES)
        iota_f = keep("iota_f", P)
        ident = keep("ident", P)
        ones = keep("ones", P)
        ones_r = keep("ones_r", 2, F32R)
        col = keep("col", NCOLS)
        stats = keep("stats", 2 * 18)
        moments = keep("moments", 2 * 4)
        minus_half = keep("minus_half", KD)
        one_eps = keep("one_eps", 1)
        gate_bias = keep("gate_bias", 2 * KD)
        bn_scale = keep("bn_scale", KD)
        bn_bias = keep("bn_bias", KD)
        base_sb = keep("base_sb", GROUPS)
        left_n = keep("left_n", 4)
        any_left = keep("any_left", 1, I32)
        idx_now = keep("idx_now", STEP, I32)
        lf_idx = keep("lf_idx", 1, I32)
        lf_dst = keep("lf_dst", 1)
        v_b2_hi = keep("v_b2_hi", D, F32R, 1)
        v_b2_lo = keep("v_b2_lo", D, F32R, 1)

        def vec(name, k=0):
            return col[:, COLS[name][0] + k:COLS[name][0] + k + 1]

        W1_hi = at("W1_hi", [P, KD, H0], F32R, A0)
        W1_lo = at("W1_lo", [P, KD, H0], F32R, A0 + 16 * KB)
        W2_hi = at("W2_hi", [P, KH, D], F32R, A0 + 32 * KB)
        W2_lo = at("W2_lo", [P, KH, D], F32R, A0 + 48 * KB)
        W12_raw = at("W12_raw", [P, KD * H0], F32, B0 + 68 * KB)
        x_in = at("x_in", [P, BLOCKS, D], F32, B0 + 84 * KB)
        xb = at("xb", [P, BLOCKS, D], F32, B0 + 104 * KB)
        zero_rows = at("zero_rows", [P, D + 2], F32, B0 + 124 * KB)
        be_bc = at("be_bc", [P, D], F32, B0 + 127 * KB)
        iota_i = at("iota_i", [P, P], I32, B0 + 130 * KB)

        gath = [at("gath0", [P, GATH, D], F32, B0), at("gath1", [P, GATH, D], F32, B0 + 80 * KB)]
        attr = [at("attr0_sb", [P, RING, CHUNK * P], F32, B0 + 38 * KB),
                at("attr1_sb", [P, RING, CHUNK * P], F32, B0 + 92 * KB)]
        attr_hl = at("attr_hl", [P, RING, CHUNK * P], F32R, B0 + 44 * KB)
        E0, E1 = B0 + 20 * KB, A0 + 40 * KB
        msg_hi = [at("msg_hi0", [P, MSG, D], F32R, E0), at("msg_hi1", [P, MSG, D], F32R, E1)]
        msg_lo = [at("msg_lo0", [P, MSG, D], F32R, E0 + 8 * KB), at("msg_lo1", [P, MSG, D], F32R, E1 + 8 * KB)]
        hot = [at("hot0", [P, HOT, P], F32R, B0 + 36 * KB), at("hot1", [P, HOT, P], F32R, E1 + 16 * KB)]
        hot_d = [at("hot_d0", [P, CHUNK, P], F32, B0 + 66 * KB), at("hot_d1", [P, CHUNK, P], F32, E1 + 18 * KB)]
        sums = [at("sums0", [P, 2, D + 4], F32, B0 + 50 * KB), at("sums1", [P, 2, D + 4], F32, E1 + 20 * KB)]
        lf_msg = [at("lf_msg0", [P, D], F32, B0 + 64 * KB), at("lf_msg1", [P, D], F32, B0 + 98 * KB)]
        lf_hot = [h[:, 0, :] for h in hot_d]
        We_raw = at("We_raw", [P, D], F32, B0 + 55 * KB)
        We_hi = at("We_hi", [P, D], F32R, B0 + 57 * KB)
        We_lo = at("We_lo", [P, D], F32R, B0 + 59 * KB)
        V1e_sb = at("V1e_sb", [P, D], F32, A0 + 28 * KB)

        h_hi = at("h_hi", [P, KD, N], F32R, B0)
        h_lo = at("h_lo", [P, KD, N], F32R, B0 + 20 * KB)
        stage0 = at("stage0", [P, 4, D], F32, B0 + 40 * KB)
        s_hi = at("s_hi", [P, KH, N], F32R, B0 + 40 * KB)
        s_lo = at("s_lo", [P, KH, N], F32R, B0 + 80 * KB)
        pre = at("pre", [P, 2, N], F32, B0 + 120 * KB)
        y_t = at("y_t", [P, KD, N], F32, B0)

        rows = at("rows", [P, BLOCKS, D], F32, A0)
        V1h_raw = at("V1h_raw", [P, KD, D], F32, A0 + 20 * KB)
        V1h_hi = at("V1h_hi", [P, KD, D], F32R, B0 + 20 * KB)
        V1h_lo = at("V1h_lo", [P, KD, D], F32R, B0 + 28 * KB)
        x1_hi = at("x1_hi", [P, KD, N], F32R, B0 + 40 * KB)
        x1_lo = at("x1_lo", [P, KD, N], F32R, B0 + 60 * KB)
        table_sb = at("table_sb", [P, 2, D], F32, B0 + 120 * KB)
        vb1_bc = at("vb1_bc", [P, D], F32, B0 + 36 * KB)
        lnx = at("lnx", [P, 2, D], F32, B0 + 126 * KB)

        stage1 = at("stage1", [P, 2, D + 2], F32, A0 + 20 * KB)
        V2_raw = at("V2_raw", [P, KD, D], F32, A0 + 20 * KB)
        V2_hi = at("V2_hi", [P, KD, D], F32R, B0 + 100 * KB)
        V2_lo = at("V2_lo", [P, KD, D], F32R, B0 + 108 * KB)
        r_hi = at("r_hi", [P, KD, N], F32R, B0 + 80 * KB)
        r_lo = at("r_lo", [P, KD, N], F32R, B0 + 20 * KB)
        deg_r = at("deg_r", [2, N], F32R, B0 + 128 * KB)
        v_b2_raw = at("v_b2_raw", [1, D], F32, B0 + 38 * KB)
        m_hi = at("m_hi", [P, KD, N], F32R, A0 + 32 * KB)
        m_lo = at("m_lo", [P, KD, N], F32R, A0 + 52 * KB)
        Wg_raw = at("Wg_raw", [P, 2 * KD * 3 * P], F32, A0 + 20 * KB)
        Wg_hi = [at("Wg_hi0", [P, 2, KD, 3, P], F32R, B0 + 8 * KB), at("Wg_hi1", [P, 2, KD, 3, P], F32R, B0 + 20 * KB)]
        Wg_lo = [at("Wg_lo0", [P, 2, KD, 3, P], F32R, B0 + 116 * KB), at("Wg_lo1", [P, 2, KD, 3, P], F32R, B0 + 80 * KB)]
        g_r = at("g_r", [P, 2, 418], F32, B0 + 32 * KB)
        g_z = at("g_z", [P, 2, 418], F32, B0 + 36 * KB)
        g_n = at("g_n", [P, 418], F32, B0 + 112 * KB)
        g_d = at("g_d", [P, 418], F32, B0 + 114 * KB)
        bn_t = at("bn_t", [P, KD, N], F32, B0 + 92 * KB)
        fin = at("fin", [P, 2, D], F32, A0 + 20 * KB)
        assert B0 + 128 * KB + 4 * N <= nc.sbuf_usable_end

        xb_dram = nc.dram_tensor("xb_dram", [BLOCKS * P, D], F32).ap()
        table_dram = nc.dram_tensor("table_dram", [N, D], F32).ap()
        sum_dram = [nc.dram_tensor("sum0_dram", [ROWS, D], F32).ap(),
                    nc.dram_tensor("sum1_dram", [ROWS, D + 2], F32).ap()]
        tables = [xb_dram, table_dram]

        bank = [psum(f"bank{b}", [P, 512]) for b in range(8)]
        e_bank = bank[0:EPS_BANKS]
        sum_bank = bank[4:6]
        degree_bank = bank[6:8]
        misc = bank[6]
        lf_bank = bank[7]

        idx_in, cols_in, be_in, x_in_done, we_in, w1_in, w2_in = map(
            sem, ("idx_in", "cols_in", "be_in", "x_in_done", "we_in", "w1_in", "w2_in"))
        pool_consts, ident_ready, dst_ready, window_ready, base_ready = map(
            sem, ("pool_consts", "ident_ready", "dst_ready", "window_ready", "base_ready"))
        left_ready, left_counted, flag_ready = map(sem, ("left_ready", "left_counted", "flag_ready"))
        eps_ready, xb_ready, start_ready, zero_ready, xb_out = map(
            sem, ("eps_ready", "xb_ready", "start_ready", "zero_ready", "xb_out"))
        start_out = [sem("start_out0"), sem("start_out1")]
        we_split, w1_split, w2_split = map(sem, ("we_split", "w1_split", "w2_split"))
        stage_in = [[sem(f"stage_in0_{i}") for i in range(4)], [sem(f"stage_in1_{i}") for i in range(2)]]
        turned, turned_high, turned_low = ([sem(f"{n}{L}") for L in range(2)] for n in ("turned", "turned_high", "turned_low"))
        mlp_mm, mlp_out, silu_done, s_split = map(sem, ("mlp_mm", "mlp_out", "silu_done", "s_split"))
        var_ready, rstd_ready, bn_ready = map(sem, ("var_ready", "rstd_ready", "bn_ready"))
        rows_in_done, v1h_in, v1e_in, vb1_in, vb2_in, v2_in, wg_in = map(
            sem, ("rows_in_done", "v1h_in", "v1e_in", "vb1_in", "vb2_in", "v2_in", "wg_in"))
        v1h_split, vb2_split, v2_split, wg_split = map(sem, ("v1h_split", "vb2_split", "v2_split", "wg_split"))
        back_turned, back_added, x1_ready, x1_turned, x1_high, x1_low = map(
            sem, ("back_turned", "back_added", "x1_ready", "x1_turned", "x1_high", "x1_low"))
        table_mm, table_ready = map(sem, ("table_mm", "table_ready"))
        table_out = [sem(f"table_out{i}") for i in range(2)]
        m_mm, m_high, m_low = map(sem, ("m_mm", "m_high", "m_low"))
        gate_mm, r_done, z_done, n_in, n_done, gru_done = map(
            sem, ("gate_mm", "r_done", "z_done", "n_in", "n_done", "gru_done"))
        fin_turned, fin_added, fin_ready = map(sem, ("fin_turned", "fin_added", "fin_ready"))
        fin_out = [sem(f"fin_out{i}") for i in range(2)]
        gate_bias_ready = sem("gate_bias_ready")
        dve_step = sem("dve_step")
        (idx_copied, idx_read, edge_mm, added, relued, low, hot_diff, hot_ready, summed, sum_out, accumulated,
         attr_high, attr_split) = ([sem(f"{n}{L}") for L in range(2)] for n in (
             "idx_copied", "idx_read", "edge_mm", "added", "relued", "low", "hot_diff", "hot_ready", "summed",
             "sum_out", "accumulated", "attr_high", "attr_split"))
        gathered = [[sem(f"gathered{L}_{i}") for i in range(GATH)] for L in range(2)]
        attr_in = [[sem(f"attr_in{L}_{i}") for i in range(RING)] for L in range(2)]
        lf_free, lf_idx_ready, lf_gathered, lf_attr_in, lf_mm, lf_msg_steps, lf_hot_ready, lf_summed, lf_copied, lf_added = (
            [sem(f"{n}{L}") for L in range(2)] for n in (
                "lf_free", "lf_idx_ready", "lf_gathered", "lf_attr_in", "lf_mm", "lf_msg_steps", "lf_hot_ready",
                "lf_summed", "lf_copied", "lf_added"))

        attr_dram, attr_parts = [attr0, attr1], [ED0, ED1]
        width = [D, D + 2]
        CPS = STEP // CHUNK
        left_value = any_left[0:1, 0:1]
        LF_ALL = 16 * TILES * BLOCKS

        def feature_major(b):
            return b[:, :].rearrange("p (k n) -> p k n", k=KD)

        block = ctx.enter_context(nc.Block())

        @block.sync
        def _(sp):
            def load_attr(L, it, first):
                rows_of = attr_parts[L]
                for c in range(CPS):
                    if not first or c >= RING:
                        if L == 0:
                            sp.wait_ge(attr_split[0], it * CPS + c - RING + 1)
                        else:
                            sp.wait_ge(edge_mm[1], it * STEP + (c - RING + 1) * CHUNK)
                    for h in range(P // rows_of):
                        sp.dma_start(attr[L][h * rows_of:(h + 1) * rows_of, c % RING, :],
                                     attr_dram[L][:, bass.ds(it * (STEP * P) + c * CHUNK * P, CHUNK * P)]
                                     ).then_inc(attr_in[L][c % RING], 16)

            def load_leftover_attr(L):
                sp.wait_ge(flag_ready, 1)
                left = sp.value_load(left_value, min_val=0, max_val=1)
                with sp.If(left > 0):
                    with sp.Fori(0, TILES) as t:
                        sp.wait_ge(lf_free[L], t + 1)
                        sp.dma_start(attr[L][0:attr_parts[L], 0, 0:P],
                                     attr_dram[L][:, bass.ds(t * P, P)]).then_inc(lf_attr_in[L], 16)
                    sp.wait_ge(lf_added[L], LF_ALL)

            def load_sums(L, stage, slots):
                sp.wait_ge(accumulated[L], 16 * GROUPS)
                for b in range(BLOCKS):
                    if b >= slots:
                        sp.wait_ge(turned[L], b - slots + 1)
                    sp.dma_start(stage[:, b % slots, :], sum_dram[L][b * P:(b + 1) * P, :]
                                 ).then_inc(stage_in[L][b % slots], 16)

            by_block = x.rearrange("(t p) d -> p t d", p=P)
            sp.dma_start(dst_i[:, :], dst).then_inc(idx_in, 16)
            sp.dma_start(src_sb[:, :], src).then_inc(idx_in, 16)
            sp.dma_start(col[:, :], cols).then_inc(cols_in, 16)
            sp.dma_start(be_bc[:, :], b_e.partition_broadcast(P)).then_inc(be_in, 16)
            sp.dma_start(x_in[:, :, :], by_block).then_inc(x_in_done, 16)
            sp.dma_start(We_raw[0:ED0, :], W_e).then_inc(we_in, 16)
            sp.dma_start(We_raw[ED0:P, :], W_e).then_inc(we_in, 16)
            sp.dma_start(W12_raw[:, :].rearrange("p (k n) -> p k n", k=KD),
                         W1.rearrange("(k p) n -> p k n", p=P)).then_inc(w1_in, 16)
            sp.wait_ge(xb_ready, 1)
            sp.dma_start(xb_dram.rearrange("(t p) d -> p t d", p=P), xb[:, :, :]).then_inc(xb_out, 16)
            load_attr(0, 0, True)
            sp.wait_ge(start_ready, 1)
            sp.dma_start(sum_dram[0][0:BLOCKS * P, :].rearrange("(t p) d -> p t d", p=P),
                         x_in[:, :, :]).then_inc(start_out[0], 16)
            sp.wait_ge(zero_ready, 1)
            sp.dma_start(sum_dram[0][BLOCKS * P:ROWS, :], zero_rows[:, 0:D]).then_inc(start_out[0], 16)
            sp.wait_ge(w1_split, 1)
            sp.dma_start(W12_raw[:, :].rearrange("p (k n) -> p k n", k=KH),
                         W2.rearrange("(k p) n -> p k n", p=P)).then_inc(w2_in, 16)
            with sp.Fori(1, STEPS) as it:
                load_attr(0, it, False)
            for b in range(ROWS // P):
                sp.dma_start(sum_dram[1][b * P:(b + 1) * P, :], zero_rows[:, :]).then_inc(start_out[1], 16)
            load_leftover_attr(0)
            sp.wait_ge(start_out[1], 16 * (ROWS // P))
            load_sums(0, stage0, 4)
            sp.wait_ge(mlp_mm, KH * 3)
            sp.dma_start(V1h_raw[:, :, :], V1h.rearrange("(k p) n -> p k n", p=P)).then_inc(v1h_in, 16)
            sp.dma_start(rows[:, :, :], by_block).then_inc(rows_in_done, 16)
            sp.dma_start(V1e_sb[:, :], V1e).then_inc(v1e_in, 16)
            sp.dma_start(vb1_bc[:, :], v_b1.partition_broadcast(P)).then_inc(vb1_in, 16)
            sp.dma_start(v_b2_raw[:, :], v_b2).then_inc(vb2_in, 16)
            sp.wait_ge(mlp_mm, (KH + KD) * 3)
            load_attr_first = load_attr
            for b in range(BLOCKS):
                sp.wait_ge(table_ready, b + 1)
                sp.dma_start(table_dram[b * P:b * P + rows_in(b), :], table_sb[0:rows_in(b), b % 2, :]
                             ).then_inc(table_out[b % 2], 16)
            load_attr_first(1, 0, True)
            sp.wait_ge(v1h_split, 1)
            sp.dma_start(V2_raw[:, :, :], V2.rearrange("(k p) n -> p k n", p=P)).then_inc(v2_in, 16)
            with sp.Fori(1, STEPS) as it:
                load_attr(1, it, False)
            load_leftover_attr(1)
            sp.wait_ge(v2_split, 1)
            load_sums(1, stage1, 2)
            sp.wait_ge(turned[1], BLOCKS)
            for m in range(KD):
                if m:
                    sp.wait_ge(wg_split, m)
                sp.dma_start(Wg_raw[:, :], Wg[m]).then_inc(wg_in, 16)
            for b in range(BLOCKS):
                sp.wait_ge(fin_ready, b + 1)
                sp.dma_start(out[b * P:b * P + rows_in(b), :], fin[0:rows_in(b), b % 2, :]).then_inc(fin_out[b % 2], 16)
            for i in range(2):
                sp.wait_ge(fin_out[i], 16 * (BLOCKS // 2))

        @block.gpsimd
        def _(pool):
            def in_register(name, value):
                if isinstance(value, int):
                    return value
                pool.reg_mov(counts[name], pool.to_reg(value))
                return counts[name]

            counts = {name: pool.alloc_register(f"count_{name}") for name in ("one", "other")}

            def accumulate(L, g, slot, very_first):
                first_node = pool.value_load(dst_i[0:1, bass.ds((g - 1) * GROUP, 1)], min_val=0, max_val=ROWS - P)
                summed_there = in_register("one", g)
                landed = in_register("other", 16 * (g - 1))
                pool.wait_ge(start_out[L], 16 * (2, ROWS // P)[L])
                pool.wait_ge(sum_out[L], summed_there)
                if not very_first:
                    pool.wait_ge(accumulated[L], landed)
                pool.dma_start(sum_dram[L][bass.ds(first_node, P), :], sums[L][:, slot, 0:width[L]],
                               accum_op=ALU.add).then_inc(accumulated[L], 16)

            def wait_table(L):
                if L == 0:
                    pool.wait_ge(xb_out, 16)
                else:
                    for i in range(2):
                        pool.wait_ge(table_out[i], 16 * (BLOCKS // 2))

            def gather_step(L, it, first):
                for j in range(STEP):
                    i, half = it * STEP + j, j // GROUP
                    if j % GROUP == 0:
                        if not first:
                            pool.wait_ge(idx_read[L], i - GROUP)
                        nc.gpsimd.tensor_copy(idx_now[:, half * GROUP:(half + 1) * GROUP],
                                              src_sb[:, bass.ds(i, GROUP)]).then_inc(idx_copied[L], 1)
                    copied, used = in_register("one", it * 2 + half + 1), in_register("other", i - GATH + 1)
                    wait_table(L)
                    if j % GROUP == 0:
                        pool.wait_ge(idx_copied[L], copied)
                    if not first or j >= GATH:
                        pool.wait_ge(added[L], used)
                    pool.indirect_dma_start(gath[L][:, j % GATH, :], None, tables[L],
                                            bass.IndirectOffsetOnAxis(ap=idx_now[:, j:j + 1], axis=0),
                                            engine_sem=idx_read[L]).then_inc(gathered[L][j % GATH], 16)
                    if j % GROUP == GROUP - 2 and (not first or half):
                        accumulate(L, it * 2 + half, 1 - half, first)

            def gather_leftover(L):
                pool.wait_ge(flag_ready, 1)
                left = pool.value_load(left_value, min_val=0, max_val=1)
                with pool.If(left > 0):
                    with pool.Fori(0, TILES) as t:
                        pool.wait_ge(lf_free[L], t + 1)
                        nc.gpsimd.tensor_copy(lf_idx[:, :], src_sb[:, bass.ds(t, 1)]).then_inc(lf_idx_ready[L], 1)
                        copied = in_register("one", t + 1)
                        wait_table(L)
                        pool.wait_ge(lf_idx_ready[L], copied)
                        pool.indirect_dma_start(gath[L][:, 0, :], None, tables[L],
                                                bass.IndirectOffsetOnAxis(ap=lf_idx[:, :], axis=0)
                                                ).then_inc(lf_gathered[L], 16)
                        for b in range(BLOCKS):
                            copied = in_register("one", t * BLOCKS + b + 1)
                            pool.wait_ge(start_out[L], 16 * (2, ROWS // P)[L])
                            pool.wait_ge(lf_copied[L], copied)
                            pool.dma_start(sum_dram[L][b * P:(b + 1) * P, :], sums[L][:, 0, 0:width[L]],
                                           accum_op=ALU.add).then_inc(lf_added[L], 16)
                            pool.wait_ge(lf_added[L], t * (16 * BLOCKS) + 16 * (b + 1))

            def rstd(n, slot):
                pool.wait_ge(var_ready, n)
                nc.gpsimd.tensor_tensor(moments[:, slot * 4 + 2:slot * 4 + 3], moments[:, slot * 4 + 1:slot * 4 + 2],
                                        minus_half[:, 0:1], ALU.pow).then_inc(rstd_ready, 1)

            nc.gpsimd.iota(iota_i[:, :], [[1, P]], base=0, channel_multiplier=0).then_inc(pool_consts, 1)
            nc.gpsimd.memset(minus_half[:, :], -0.5).then_inc(pool_consts, 1)
            nc.gpsimd.memset(ones[:, :], 1.0).then_inc(pool_consts, 1)
            nc.gpsimd.memset(ident[:, :], 0.0).then_inc(pool_consts, 1)
            pool.wait_ge(pool_consts, 4)
            nc.gpsimd.affine_select(out=ident[:, :], in_=ident[:, :], compare_op=ALU.not_equal, fill=1.0, base=0,
                                    pattern=[[-1, P]], channel_multiplier=1).then_inc(ident_ready, 1)
            pool.wait_ge(idx_in, 32)
            n = 0
            for L in range(2):
                wait_table(L)
                gather_step(L, 0, True)
                with pool.Fori(1, STEPS) as it:
                    gather_step(L, it, False)
                accumulate(L, GROUPS, 1, False)
                gather_leftover(L)
                if L == 0:
                    for c in range(KH + KD):
                        n += 1
                        rstd(n, c % 2)
                else:
                    n += 1
                    pool.wait_ge(var_ready, n)
                    nc.gpsimd.tensor_tensor(bn_scale[:, :], bn_scale[:, :], minus_half[:, :],
                                            ALU.pow).then_inc(rstd_ready, 1)
                for b in range(BLOCKS):
                    n += 1
                    rstd(n, b % 2)

        @block.tensor
        def _(pe):
            def product(acc, terms, start=True):
                passes = [(a, b) for a_hi, a_lo, b_hi, b_lo in terms for a, b in ((a_hi, b_hi), (a_hi, b_lo), (a_lo, b_hi))]
                for i, (a, b) in enumerate(passes):
                    mm = nc.tensor.matmul(acc, a, b, start=start and i == 0, stop=i == len(passes) - 1)
                return mm

            def edge_product(L, it, j, first):
                c, ks = j // CHUNK, slice(j % CHUNK * P, (j % CHUNK + 1) * P)
                if j % CHUNK == 0:
                    if L == 0:
                        pe.wait_ge(attr_split[0], it * CPS + c + 1)
                    else:
                        pe.wait_ge(attr_in[1][c % RING], it * (CPS // RING * 16) + (c // RING + 1) * 16)
                if not first or j >= EPS_BANKS:
                    pe.wait_ge(low[L], it * STEP + j - EPS_BANKS + 1)
                acc = e_bank[j % EPS_BANKS][:, :]
                if L == 0:
                    nc.tensor.matmul(acc, attr_hl[:, c % RING, ks], We_hi[:, :], start=True, stop=False)
                    nc.tensor.matmul(acc, attr_hl[:, c % RING, ks], We_lo[:, :], start=False,
                                     stop=True).then_inc(edge_mm[0], 1)
                else:
                    nc.tensor.matmul(acc, attr[1][:, c % RING, ks], V1e_sb[:, :], start=True,
                                     stop=True).then_inc(edge_mm[1], 1)

            def sum_product(L, it, j, first):
                start, stop, half = j % GROUP == 0, j % GROUP == GROUP - 1, j // GROUP % 2
                pe.wait_ge(low[L], it * STEP + j + 1)
                pe.wait_ge(hot_ready[L], it * STEP + j + 1)
                if start and not first:
                    pe.wait_ge(sum_out[L], it * 2 + j // GROUP - 1)
                acc, h = sum_bank[half][:, :], hot[L][:, j % HOT, :]
                nc.tensor.matmul(acc, h, msg_hi[L][:, j % MSG, :], start=start, stop=False)
                mm = nc.tensor.matmul(acc, h, msg_lo[L][:, j % MSG, :], start=False, stop=stop)
                if L == 1:
                    mm = nc.tensor.matmul(degree_bank[half][:, 0:2], h, ones_r[:, :], start=start, stop=stop)
                mm.then_inc(summed[L], 1)

            def edges(L):
                for j in range(STEP):
                    if j >= LAG:
                        sum_product(L, 0, j - LAG, True)
                    edge_product(L, 0, j, True)
                with pe.Fori(1, STEPS) as it:
                    for j in range(STEP):
                        sum_product(L, it, j - LAG, False)
                        edge_product(L, it, j, False)
                for j in range(STEP - LAG, STEP):
                    sum_product(L, STEPS - 1, j, False)

            def leftover(L):
                pe.wait_ge(flag_ready, 1)
                left = pe.value_load(left_value, min_val=0, max_val=1)
                with pe.If(left > 0):
                    K, W = attr_parts[L], (We_raw, V1e_sb)[L]
                    with pe.Fori(0, TILES) as t:
                        pe.wait_ge(lf_attr_in[L], t * 16 + 16)
                        pe.wait_ge(lf_free[L], t + 1)
                        nc.tensor.matmul(lf_bank[:, :], attr[L][0:K, 0, 0:P], W[0:K, :], start=True,
                                         stop=True).then_inc(lf_mm[L], 1)
                        for b in range(BLOCKS):
                            pe.wait_ge(lf_hot_ready[L], t * BLOCKS + b + 1)
                            mm = nc.tensor.matmul(sum_bank[0][:, :], lf_hot[L], lf_msg[L][:, :], start=True, stop=True)
                            if L == 1:
                                mm = nc.tensor.matmul(misc[:, 0:2], lf_hot[L], ones[:, 0:2], start=True, stop=True)
                            mm.then_inc(lf_summed[L], 1)
                    pe.wait_ge(lf_added[L], LF_ALL)

            def turn_sums(L, stage, slots):
                for b in range(BLOCKS):
                    pe.wait_ge(stage_in[L][b % slots], 16 * (b // slots + 1))
                    if b >= 2:
                        pe.wait_ge(turned_low[L], b - 1)
                    for k in range(KD):
                        tr = nc.tensor.transpose(bank[b % 2][:, k * P:(k + 1) * P], stage[:, b % slots, k * P:(k + 1) * P],
                                                 ident[:, :])
                    if L == 1:
                        tr = nc.tensor.transpose(bank[2 + b % 2][0:2, 0:P], stage[:, b % slots, D:D + 2], ident[:, :])
                    tr.then_inc(turned[L], 1)

            pe.wait_ge(pool_consts, 4)
            pe.wait_ge(dst_ready, 1)
            nc.tensor.matmul(misc[:, 0:GROUPS], ones[0:1, :], dst_f[0:1, 0:TILES:GROUP], start=True,
                             stop=True).then_inc(base_ready, 1)
            pe.wait_ge(left_ready, 1)
            nc.tensor.matmul(misc[0:1, 16:17], left_n[:, 0:1], ones[:, 0:1], start=True, stop=True).then_inc(left_counted, 1)
            pe.wait_ge(we_split, 1)
            edges(0)
            leftover(0)
            pe.wait_ge(ident_ready, 1)
            turn_sums(0, stage0, 4)

            pe.wait_ge(turned_low[0], BLOCKS)
            pe.wait_ge(w1_split, 1)
            n = 0
            for W_hi, W_lo, X_hi, X_lo, K, M in ((W1_hi, W1_lo, h_hi, h_lo, KD, KH), (W2_hi, W2_lo, s_hi, s_lo, KH, KD)):
                if K == KH:
                    pe.wait_ge(s_split, KH)
                    pe.wait_ge(w2_split, 1)
                for m in range(M):
                    ms = slice(m * P, (m + 1) * P)
                    for a, w in NODE_CHUNKS:
                        if n >= 6:
                            pe.wait_ge(mlp_out, n - 5)
                        product(bank[2 + n % 6][:, 0:w],
                                [(W_hi[:, k, ms], W_lo[:, k, ms], X_hi[:, k, a:a + w], X_lo[:, k, a:a + w]) for k in range(K)]
                                ).then_inc(mlp_mm, 1)
                        n += 1

            pe.wait_ge(silu_done, KH + KD)
            pe.wait_ge(mlp_out, 3 * (KH + KD))
            for t in range(BLOCKS + 3):
                if t < BLOCKS:
                    r = rows_in(t)
                    if t >= 2:
                        pe.wait_ge(back_added, t - 1)
                    for k in range(KD):
                        tr = nc.tensor.transpose(bank[t % 2][0:r, k * P:(k + 1) * P], y_t[:, k, t * P:t * P + r], ident[:, :])
                    tr.then_inc(back_turned, 1)
                b = t - 2
                if 0 <= b < BLOCKS:
                    r = rows_in(b)
                    pe.wait_ge(x1_ready, b + 1)
                    if b >= 2:
                        pe.wait_ge(x1_low, b - 1)
                    for k in range(KD):
                        tr = nc.tensor.transpose(bank[2 + b % 2][:, k * P:k * P + r], rows[0:r, b, k * P:(k + 1) * P],
                                                 ident[0:r, 0:r])
                    tr.then_inc(x1_turned, 1)
                b = t - 3
                if b >= 0:
                    r = rows_in(b)
                    pe.wait_ge(x1_low, b + 1)
                    if b == 0:
                        pe.wait_ge(v1h_split, 1)
                    if b >= 2:
                        pe.wait_ge(table_ready, b - 1)
                    product(bank[4 + b % 2][0:r, :],
                            [(x1_hi[:, k, b * P:b * P + r], x1_lo[:, k, b * P:b * P + r], V1h_hi[:, k, :], V1h_lo[:, k, :])
                             for k in range(KD)]).then_inc(table_mm, 1)
            pe.wait_ge(table_ready, BLOCKS)
            pe.wait_ge(v1e_in, 16)
            edges(1)
            leftover(1)
            turn_sums(1, stage1, 2)

            pe.wait_ge(turned_low[1], BLOCKS)
            pe.wait_ge(v2_split, 1)
            pe.wait_ge(vb2_split, 1)
            n = 0
            for m in range(KD):
                ms = slice(m * P, (m + 1) * P)
                for a, w in NODE_CHUNKS:
                    if n >= 4:
                        pe.wait_ge(m_low, n - 3)
                    acc = bank[4 + n % 4][:, 0:w]
                    nc.tensor.matmul(acc, v_b2_hi[0:1, ms], deg_r[0:1, a:a + w], start=True, stop=False)
                    nc.tensor.matmul(acc, v_b2_lo[0:1, ms], deg_r[0:1, a:a + w], start=False, stop=False)
                    product(acc, [(V2_hi[:, k, ms], V2_lo[:, k, ms], r_hi[:, k, a:a + w], r_lo[:, k, a:a + w])
                                  for k in range(KD)], start=False).then_inc(m_mm, 1)
                    n += 1

            pe.wait_ge(m_low, n)
            n = 0
            for m in range(KD):
                pe.wait_ge(wg_split, m + 1)
                for a, w in NODE_CHUNKS:
                    def gate(source, g):
                        X_hi, X_lo = ((m_hi, m_lo), (x1_hi, x1_lo))[source]
                        return [(Wg_hi[m % 2][:, source, k, g, :], Wg_lo[m % 2][:, source, k, g, :],
                                 X_hi[:, k, a:a + w], X_lo[:, k, a:a + w]) for k in range(KD)]
                    if n >= 2:
                        pe.wait_ge(z_done, n - 1)
                        pe.wait_ge(n_in, n - 1)
                    four = bank[4 * (n % 2):4 * (n % 2) + 4]
                    product(four[0][:, 0:w], gate(0, 0) + gate(1, 0)).then_inc(gate_mm, 1)
                    product(four[1][:, 0:w], gate(1, 2)).then_inc(gate_mm, 1)
                    product(four[2][:, 0:w], gate(0, 2)).then_inc(gate_mm, 1)
                    product(four[3][:, 0:w], gate(0, 1) + gate(1, 1)).then_inc(gate_mm, 1)
                    n += 1
            pe.wait_ge(gru_done, n)
            for b in range(BLOCKS):
                r = rows_in(b)
                if b >= 2:
                    pe.wait_ge(fin_added, b - 1)
                for k in range(KD):
                    tr = nc.tensor.transpose(bank[b % 2][0:r, k * P:(k + 1) * P], bn_t[:, k, b * P:b * P + r], ident[:, :])
                tr.then_inc(fin_turned, 1)

        @block.scalar
        def _(act):
            def copy(to, of):
                return nc.scalar.activation(to, of, ACT.Copy)

            def window_out(L, g, slot, first):
                act.wait_ge(summed[L], g * GROUP)
                if not first:
                    act.wait_ge(accumulated[L], 16 * (g - 2))
                if L == 1:
                    copy(sums[1][:, slot, D:D + 2], degree_bank[slot][:, 0:2])
                copy(sums[L][:, slot, 0:D], sum_bank[slot][:, :]).then_inc(sum_out[L], 1)

            def message_step(L, it, first):
                for j in range(STEP):
                    i, c = it * STEP + j, j // CHUNK
                    if L == 0 and j % CHUNK == 0:
                        act.wait_ge(attr_in[0][c % RING], it * (CPS // RING * 32) + (c // RING + 1) * 32)
                        if not first or c >= RING:
                            act.wait_ge(edge_mm[0], it * STEP + (c - RING + 1) * CHUNK)
                        copy(attr_hl[:, c % RING, :], attr[0][:, c % RING, :]).then_inc(attr_high[0], 1)
                    if not first or j >= HOT:
                        act.wait_ge(hot_ready[L], i - HOT + 1)
                    nc.scalar.activation(hot_d[L][:, j % HOT, :], iota_f[:, :], ACT.Abs,
                                         bias=in_window[:, bass.ds(i, 1)]).then_inc(hot_diff[L], 1)
                    act.wait_ge(hot_diff[L], i + 1)
                    if not first or j >= HOT:
                        act.wait_ge(summed[L], i - HOT + 1)
                    nc.scalar.activation(hot[L][:, j % HOT, :], hot_d[L][:, j % HOT, :], ACT.Relu, bias=1.0,
                                         scale=-1.0).then_inc(hot_ready[L], 1)
                    act.wait_ge(added[L], i + 1)
                    nc.scalar.activation(msg_hi[L][:, j % MSG, :], e_bank[j % EPS_BANKS][:, :],
                                         ACT.Relu).then_inc(relued[L], 1)
                    if j % GROUP == LAG + 1 and (not first or j > GROUP):
                        window_out(L, it * 2 + j // GROUP, 1 - j // GROUP, first)

            def edges(L):
                message_step(L, 0, True)
                with act.Fori(1, STEPS) as it:
                    message_step(L, it, False)
                window_out(L, GROUPS, 1, False)
                act.wait_ge(flag_ready, 1)
                left = act.value_load(left_value, min_val=0, max_val=1)
                with act.If(left > 0):
                    act.wait_ge(lf_added[L], LF_ALL)

            def high_of_turned(L, hi):
                for b in range(BLOCKS):
                    r = rows_in(b)
                    act.wait_ge(turned[L], b + 1)
                    if L == 1:
                        copy(deg_r[:, b * P:b * P + r], bank[2 + b % 2][0:2, 0:r])
                    copy(hi[:, :, b * P:b * P + r], feature_major(bank[b % 2])[:, :, 0:r]).then_inc(turned_high[L], 1)

            act.wait_ge(eps_ready, 1)
            act.wait_ge(xb_ready, 1)
            nc.scalar.activation(x_in[:, :, :], x_in[:, :, :], ACT.Identity, scale=one_eps[:, :]).then_inc(start_ready, 1)
            act.wait_ge(window_ready, 1)
            edges(0)
            high_of_turned(0, h_hi)

            def silu(c):
                act.wait_ge(bn_ready, c + 1)
                to = pre[:, c % 2, :] if c < KH else y_t[:, c - KH, :]
                at4 = 4 * (c % 2)
                nc.scalar.activation(to, pre[:, c % 2, :], ACT.Silu, scale=moments[:, at4 + 2:at4 + 3],
                                     bias=moments[:, at4 + 3:at4 + 4]).then_inc(silu_done, 1)

            n = 0
            for c in range(KH + KD):
                if c == KH:
                    silu(c - 1)
                for q, (a, w) in enumerate(NODE_CHUNKS):
                    act.wait_ge(mlp_mm, n + 1)
                    if c >= 2 and q == 0:
                        act.wait_ge(s_split, min(c - 1, KH))
                        act.wait_ge(silu_done, c - 1)
                    nc.scalar.activation(pre[:, c % 2, a:a + w], bank[2 + n % 6][:, 0:w], ACT.Identity,
                                         bias=vec("b1", c) if c < KH else vec("b2", c - KH)).then_inc(mlp_out, 1)
                    n += 1
                    if q == 0 and c not in (0, KH):
                        silu(c - 1)
            silu(KH + KD - 1)
            for b in range(BLOCKS):
                r = rows_in(b)
                act.wait_ge(x1_turned, b + 1)
                copy(x1_hi[:, :, b * P:b * P + r], feature_major(bank[2 + b % 2])[:, :, 0:r]).then_inc(x1_high, 1)
            edges(1)
            high_of_turned(1, r_hi)
            n = 0
            for m in range(KD):
                for a, w in NODE_CHUNKS:
                    act.wait_ge(m_mm, n + 1)
                    copy(m_hi[:, m, a:a + w], bank[4 + n % 4][:, 0:w]).then_inc(m_high, 1)
                    n += 1
            act.wait_ge(gate_bias_ready, 1)
            n = 0
            for m in range(KD):
                for a, w in NODE_CHUNKS:
                    four = bank[4 * (n % 2):4 * (n % 2) + 4]
                    act.wait_ge(gate_mm, 4 * n + 1)
                    if n >= 2:
                        act.wait_ge(gru_done, n - 1)
                    nc.scalar.activation(g_r[:, n % 2, 0:w], four[0][:, 0:w], ACT.Sigmoid,
                                         bias=gate_bias[:, m:m + 1]).then_inc(r_done, 1)
                    act.wait_ge(n_in, n + 1)
                    if n:
                        act.wait_ge(gru_done, n)
                    nc.scalar.activation(g_n[:, 0:w], g_r[:, n % 2, 0:w], ACT.Tanh,
                                         bias=vec("b_ih", 2 * KD + m)).then_inc(n_done, 1)
                    act.wait_ge(gate_mm, 4 * n + 4)
                    nc.scalar.activation(g_z[:, n % 2, 0:w], four[3][:, 0:w], ACT.Sigmoid,
                                         bias=gate_bias[:, KD + m:KD + m + 1]).then_inc(z_done, 1)
                    n += 1

        @block.vector
        def _(dve):
            steps = [0]

            def link(ins):
                steps[0] += 1
                ins.then_inc(dve_step, 1)
                dve.wait_ge(dve_step, steps[0])

            def low_part(to, value, high):
                return nc.vector.tensor_tensor(to, value, high.bitcast(F32), ALU.subtract)

            def split(hi, lo, raw):
                link(nc.vector.tensor_copy(hi, raw))
                return low_part(lo, raw, hi)

            dve.wait_ge(cols_in, 16)
            nc.vector.tensor_scalar(one_eps[:, :], vec("eps"), 1.0, None, ALU.add).then_inc(eps_ready, 1)
            dve.wait_ge(idx_in, 32)
            nc.vector.tensor_copy(dst_f[:, :], dst_i[:, :]).then_inc(dst_ready, 1)
            dve.wait_ge(pool_consts, 4)
            nc.vector.tensor_copy(iota_f[:, :], iota_i[:, :])
            nc.vector.tensor_copy(ones_r[:, :], ones[:, 0:2])
            dve.wait_ge(base_ready, 1)
            link(nc.vector.tensor_copy(base_sb[:, :], misc[:, 0:GROUPS]))
            for g in range(GROUPS):
                gs = slice(g * GROUP, (g + 1) * GROUP)
                i = nc.vector.tensor_scalar(in_window[:, gs], dst_f[:, gs], -1.0, base_sb[:, g:g + 1], ALU.mult, ALU.add)
            link(i)
            link(nc.vector.tensor_scalar(dst_left[:, :], in_window[:, :], 0.0, None, ALU.is_gt))
            link(nc.vector.scalar_tensor_tensor(dst_left[:, :], in_window[:, :], float(1 - P), dst_left[:, :],
                                                ALU.is_lt, ALU.add))
            link(nc.vector.scalar_tensor_tensor(dst_left[:, :], dst_f[:, :], 0.0, dst_left[:, :], ALU.is_ge, ALU.mult))
            link(nc.vector.tensor_reduce(left_n[:, 0:1], dst_left[:, :], mybir.AxisListType.X, ALU.add))
            link(nc.vector.scalar_tensor_tensor(dst_left[:, :], dst_f[:, :], 1.0, dst_left[:, :], ALU.add, ALU.mult))
            link(nc.vector.tensor_scalar(dst_left[:, :], dst_left[:, :], -1.0, None, ALU.add))
            nc.vector.nop().then_inc(window_ready, 1)
            nc.vector.nop().then_inc(left_ready, 1)
            dve.wait_ge(left_counted, 1)
            nc.vector.tensor_scalar(any_left[0:1, :], misc[0:1, 16:17], 0.0, None, ALU.is_gt).then_inc(flag_ready, 1)
            dve.wait_ge(we_in, 32)
            split(We_hi[:, :], We_lo[:, :], We_raw[:, :]).then_inc(we_split, 1)
            dve.wait_ge(be_in, 16)
            dve.wait_ge(x_in_done, 16)
            nc.vector.tensor_tensor(xb[:, :, :], x_in[:, :, :], be_bc[:, :].unsqueeze(1).broadcast_to([P, BLOCKS, D]),
                                    ALU.add).then_inc(xb_ready, 1)
            nc.vector.memset(zero_rows[:, :], 0.0).then_inc(zero_ready, 1)
            dve.wait_ge(w1_in, 16)
            for k in range(KD):
                raw = W12_raw[:, k * H0:(k + 1) * H0]
                i = split(W1_hi[:, k, :], W1_lo[:, k, :], raw)
            i.then_inc(w1_split, 1)

            def message_low(L, i, j):
                dve.wait_ge(relued[L], i + 1)
                nc.vector.scalar_tensor_tensor(msg_lo[L][:, j % MSG, :], e_bank[j % EPS_BANKS][:, :], 0.0,
                                               msg_hi[L][:, j % MSG, :].bitcast(F32), ALU.max,
                                               ALU.subtract).then_inc(low[L], 1)

            def message_step(L, it, first):
                for j in range(STEP):
                    i, c = it * STEP + j, j // CHUNK
                    if L == 0 and j % CHUNK == 0:
                        dve.wait_ge(attr_high[0], it * CPS + c + 1)
                        low_part(attr_hl[ED0:P, c % RING, :], attr[0][ED0:P, c % RING, :],
                                 attr_hl[ED0:P, c % RING, :]).then_inc(attr_split[0], 1)
                    dve.wait_ge(gathered[L][j % GATH], it * (STEP // GATH * 16) + (j // GATH + 1) * 16)
                    dve.wait_ge(edge_mm[L], i + 1)
                    acc = e_bank[j % EPS_BANKS][:, :]
                    nc.vector.tensor_tensor(acc, acc, gath[L][:, j % GATH, :], ALU.add).then_inc(added[L], 1)
                    if not first or j:
                        message_low(L, i - 1, j - 1)

            def edges(L):
                message_step(L, 0, True)
                if L == 0:
                    dve.wait_ge(w2_in, 16)
                    for k in range(KH):
                        i = split(W2_hi[:, k, :], W2_lo[:, k, :], W12_raw[:, k * D:(k + 1) * D])
                    i.then_inc(w2_split, 1)
                else:
                    dve.wait_ge(v2_in, 16)
                    i = split(V2_hi[:, :, :], V2_lo[:, :, :], V2_raw[:, :, :])
                    i.then_inc(v2_split, 1)
                    dve.wait_ge(vb2_in, 16)
                    split(v_b2_hi[:, :], v_b2_lo[:, :], v_b2_raw[:, :]).then_inc(vb2_split, 1)
                with dve.Fori(1, STEPS) as it:
                    message_step(L, it, False)
                message_low(L, TILES - 1, STEP - 1)
                leftover(L)

            def leftover(L):
                dve.wait_ge(flag_ready, 1)
                left = dve.value_load(left_value, min_val=0, max_val=1)
                with dve.If(left > 0):
                    dve.wait_ge(accumulated[L], 16 * GROUPS)
                    nc.vector.nop().then_inc(lf_free[L], 1)
                    with dve.Fori(0, TILES) as t:
                        dve.wait_ge(lf_gathered[L], t * 16 + 16)
                        dve.wait_ge(lf_mm[L], t + 1)
                        nc.vector.tensor_copy(lf_dst[:, :], dst_left[:, bass.ds(t, 1)]).then_inc(lf_msg_steps[L], 1)
                        nc.vector.tensor_tensor(lf_msg[L][:, :], lf_bank[:, :], gath[L][:, 0, :],
                                                ALU.add).then_inc(lf_msg_steps[L], 1)
                        dve.wait_ge(lf_msg_steps[L], t * 3 + 2)
                        nc.vector.tensor_scalar(lf_msg[L][:, :], lf_msg[L][:, :], 0.0, None,
                                                ALU.max).then_inc(lf_msg_steps[L], 1)
                        dve.wait_ge(lf_msg_steps[L], t * 3 + 3)
                        for b in range(BLOCKS):
                            nc.vector.tensor_scalar(lf_hot[L], iota_f[:, :], float(b * P), lf_dst[:, 0:1], ALU.add,
                                                    ALU.is_equal).then_inc(lf_hot_ready[L], 1)
                            dve.wait_ge(lf_summed[L], t * BLOCKS + b + 1)
                            if b:
                                dve.wait_ge(lf_added[L], t * (16 * BLOCKS) + 16 * b)
                            if L == 1:
                                nc.vector.tensor_copy(sums[1][:, 0, D:D + 2], misc[:, 0:2])
                            nc.vector.tensor_copy(sums[L][:, 0, 0:D], sum_bank[0][:, :]).then_inc(lf_copied[L], 1)
                        dve.wait_ge(lf_added[L], t * (16 * BLOCKS) + 16 * BLOCKS)
                        nc.vector.nop().then_inc(lf_free[L], 1)

            def low_of_turned(L, hi, lo):
                for b in range(BLOCKS):
                    r = rows_in(b)
                    dve.wait_ge(turned_high[L], b + 1)
                    low_part(lo[:, :, b * P:b * P + r], feature_major(bank[b % 2])[:, :, 0:r],
                             hi[:, :, b * P:b * P + r]).then_inc(turned_low[L], 1)

            def variance(slot, parts, value):
                n = len(value)
                for q, v in enumerate(value):
                    i = nc.vector.bn_stats(stats[0:parts, slot * 18 + q * 6:slot * 18 + q * 6 + 6], v)
                link(i)
                link(nc.vector.bn_aggr(moments[0:parts, slot * 4:slot * 4 + 2], stats[0:parts, slot * 18:slot * 18 + 6 * n]))
                at4 = slot * 4 + 1
                nc.vector.tensor_scalar(moments[0:parts, at4:at4 + 1], moments[0:parts, at4:at4 + 1], EPS, None,
                                        ALU.add).then_inc(var_ready, 1)

            edges(0)
            low_of_turned(0, h_hi, h_lo)

            rstds = [0]

            def rstd_now():
                rstds[0] += 1
                dve.wait_ge(rstd_ready, rstds[0])

            def split_hidden(c):
                dve.wait_ge(silu_done, c + 1)
                split(s_hi[:, c, :], s_lo[:, c, :], pre[:, c % 2, :]).then_inc(s_split, 1)

            for c in range(KH + KD):
                dve.wait_ge(mlp_out, 3 * c + 3)
                variance(c % 2, P, [pre[:, c % 2, a:a + w] for a, w in NODE_CHUNKS])
                rstd_now()
                at4 = 4 * (c % 2)
                g, beta = (vec("g1", c), vec("beta1", c)) if c < KH else (vec("g2", c - KH), vec("beta2", c - KH))
                link(nc.vector.tensor_tensor(moments[:, at4 + 2:at4 + 3], moments[:, at4 + 2:at4 + 3], g, ALU.mult))
                link(nc.vector.tensor_tensor(moments[:, at4 + 3:at4 + 4], moments[:, at4:at4 + 1], moments[:, at4 + 2:at4 + 3],
                                             ALU.mult))
                nc.vector.tensor_tensor(moments[:, at4 + 3:at4 + 4], beta, moments[:, at4 + 3:at4 + 4],
                                        ALU.subtract).then_inc(bn_ready, 1)
                if c < KH:
                    split_hidden(c)
                if c == KH:
                    dve.wait_ge(v1h_in, 16)
                    split(V1h_hi[:, :, :], V1h_lo[:, :, :], V1h_raw[:, :, :]).then_inc(v1h_split, 1)

            def normalize(to, parts, slot):
                rstd_now()
                return nc.vector.tensor_scalar(to, lnx[0:parts, slot, :], moments[0:parts, slot * 4:slot * 4 + 1],
                                               moments[0:parts, slot * 4 + 2:slot * 4 + 3], ALU.subtract, ALU.mult)

            dve.wait_ge(rows_in_done, 16)
            dve.wait_ge(vb1_in, 16)
            for t in range(BLOCKS + 3):
                if t < BLOCKS:
                    r = rows_in(t)
                    dve.wait_ge(back_turned, t + 1)
                    if t >= 2:
                        dve.wait_ge(x1_ready, t - 1)
                    i = nc.vector.tensor_tensor(lnx[0:r, t % 2, :], bank[t % 2][0:r, :], rows[0:r, t, :], ALU.add)
                    i.then_inc(back_added, 1)
                    dve.wait_ge(back_added, t + 1)
                    variance(t % 2, r, [lnx[0:r, t % 2, :]])
                b = t - 1
                if 0 <= b < BLOCKS:
                    r = rows_in(b)
                    normalize(rows[0:r, b, :], r, b % 2).then_inc(x1_ready, 1)
                b = t - 2
                if 0 <= b < BLOCKS:
                    r = rows_in(b)
                    dve.wait_ge(x1_high, b + 1)
                    low_part(x1_lo[:, :, b * P:b * P + r], feature_major(bank[2 + b % 2])[:, :, 0:r],
                             x1_hi[:, :, b * P:b * P + r]).then_inc(x1_low, 1)
                b = t - 3
                if b >= 0:
                    r = rows_in(b)
                    dve.wait_ge(table_mm, b + 1)
                    if b >= 2:
                        dve.wait_ge(table_out[b % 2], 16 * (b // 2))
                    nc.vector.tensor_tensor(table_sb[0:r, b % 2, :], bank[4 + b % 2][0:r, :], vb1_bc[0:r, :],
                                            ALU.add).then_inc(table_ready, 1)
            edges(1)
            low_of_turned(1, r_hi, r_lo)

            def split_gates(m):
                dve.wait_ge(wg_in, 16 * (m + 1))
                flat = (t[:, :, :, :, :].rearrange("p a k g n -> p (a k g n)") for t in (Wg_hi[m % 2], Wg_lo[m % 2]))
                split(*flat, Wg_raw[:, :]).then_inc(wg_split, 1)

            n = 0
            for m in range(KD):
                for a, w in NODE_CHUNKS:
                    dve.wait_ge(m_high, n + 1)
                    low_part(m_lo[:, m, a:a + w], bank[4 + n % 4][:, 0:w], m_hi[:, m, a:a + w]).then_inc(m_low, 1)
                    n += 1
                    if n == 6:
                        split_gates(0)
            at_ih, at_hh = COLS["b_ih"][0], COLS["b_hh"][0]
            nc.vector.tensor_tensor(gate_bias[:, :], col[:, at_ih:at_ih + 2 * KD], col[:, at_hh:at_hh + 2 * KD],
                                    ALU.add).then_inc(gate_bias_ready, 1)
            at_var = COLS["run_var"][0]
            nc.vector.tensor_scalar(bn_scale[:, :], col[:, at_var:at_var + KD], EPS, None, ALU.add).then_inc(var_ready, 1)
            rstd_now()
            a = {name: COLS[name][0] for name in ("gamma", "beta", "run_mean")}
            link(nc.vector.tensor_tensor(bn_scale[:, :], bn_scale[:, :], col[:, a["gamma"]:a["gamma"] + KD], ALU.mult))
            link(nc.vector.tensor_tensor(bn_bias[:, :], bn_scale[:, :], col[:, a["run_mean"]:a["run_mean"] + KD], ALU.mult))
            link(nc.vector.tensor_tensor(bn_bias[:, :], col[:, a["beta"]:a["beta"] + KD], bn_bias[:, :], ALU.subtract))
            n = 0
            for m in range(KD):
                for q, (a, w) in enumerate(NODE_CHUNKS):
                    four = bank[4 * (n % 2):4 * (n % 2) + 4]
                    gr, gz, gn, gd = g_r[:, n % 2, 0:w], g_z[:, n % 2, 0:w], g_n[:, 0:w], g_d[:, 0:w]
                    dve.wait_ge(r_done, n + 1)
                    dve.wait_ge(gate_mm, 4 * n + 3)
                    link(nc.vector.scalar_tensor_tensor(gr, four[1][:, 0:w], vec("b_hh", 2 * KD + m), gr, ALU.add, ALU.mult))
                    nc.vector.tensor_tensor(gr, gr, four[2][:, 0:w], ALU.add).then_inc(n_in, 1)
                    dve.wait_ge(n_done, n + 1)
                    link(nc.vector.tensor_tensor(gd, x1_hi[:, m, a:a + w].bitcast(F32), gn, ALU.subtract))
                    link(nc.vector.tensor_tensor(gd, gd, x1_lo[:, m, a:a + w].bitcast(F32), ALU.add))
                    dve.wait_ge(z_done, n + 1)
                    link(nc.vector.tensor_tensor(gd, gd, gz, ALU.mult))
                    link(nc.vector.tensor_tensor(gd, gd, gn, ALU.add))
                    nc.vector.tensor_scalar(bn_t[:, m, a:a + w], gd, bn_scale[:, m:m + 1], bn_bias[:, m:m + 1],
                                            ALU.mult, ALU.add).then_inc(gru_done, 1)
                    n += 1
                    if q == 0 and m + 1 < KD:
                        split_gates(m + 1)
            for t in range(BLOCKS + 1):
                if t < BLOCKS:
                    r = rows_in(t)
                    dve.wait_ge(fin_turned, t + 1)
                    if t >= 2:
                        dve.wait_ge(fin_ready, t - 1)
                    nc.vector.scalar_tensor_tensor(lnx[0:r, t % 2, :], rows[0:r, t, :], 2.0, bank[t % 2][0:r, :], ALU.mult,
                                                   ALU.add).then_inc(fin_added, 1)
                    dve.wait_ge(fin_added, t + 1)
                    variance(t % 2, r, [lnx[0:r, t % 2, :]])
                b = t - 1
                if b >= 0:
                    r = rows_in(b)
                    if b >= 2:
                        dve.wait_ge(fin_out[b % 2], 16 * (b // 2))
                    normalize(fin[0:r, b % 2, :], r, b % 2).then_inc(fin_ready, 1)


def kernel(**inputs):
    import numpy as np
    import concourse.bacc as bacc
    from concourse.bass_utils import run_bass_kernel_spmd

    a = {k: np.asarray(v) for k, v in inputs.items()}

    def by_tile(index, fill):
        full = np.full(TILES * P, fill, index.dtype)
        full[:E] = index
        return full.reshape(TILES, P).T

    def turned(attr):
        full = np.zeros((attr.shape[1], TILES * P), attr.dtype)
        full[:, :E] = attr.T
        return full

    x = np.zeros((BLOCKS * P, D), a["x"].dtype)
    x[:N] = a["x"]
    vectors = {"b1": a["L0_gnn_b1"], "g1": a["L0_gnn_g1"], "beta1": a["L0_gnn_beta1"], "b2": a["L0_gnn_b2"],
               "g2": a["L0_gnn_g2"], "beta2": a["L0_gnn_beta2"], "b_ih": a["L1_gnn_b_ih"], "b_hh": a["L1_gnn_b_hh"],
               "gamma": a["L1_gnn_gamma"], "beta": a["L1_gnn_beta"], "run_mean": a["L1_gnn_run_mean"],
               "run_var": a["L1_gnn_run_var"], "eps": np.full(P, a["L0_gnn_eps"])}
    gates = np.stack([a["L1_gnn_W_ih"], a["L1_gnn_W_hh"]]).reshape(2, 3, KD, P, KD, P)
    arrays = {
        "x": x,
        "src": by_tile(a["src"], 0),
        "dst": by_tile(a["dst"], -1),
        "attr0": turned(a["edge_attr_64"]),
        "attr1": turned(a["edge_attr_128"]),
        "W_e": a["L0_gnn_W_e"],
        "b_e": a["L0_gnn_b_e"].reshape(1, D),
        "W1": a["L0_gnn_W1"],
        "W2": a["L0_gnn_W2"],
        "V1h": a["L1_gnn_W1"][:, :D].T,
        "V1e": a["L1_gnn_W1"][:, D:].T,
        "v_b1": a["L1_gnn_b1"].reshape(1, D),
        "V2": a["L1_gnn_W2"].T,
        "v_b2": a["L1_gnn_b2"].reshape(1, D),
        "Wg": gates.transpose(2, 5, 0, 4, 1, 3).reshape(KD, P, 2 * KD * 3 * P),
        "cols": np.concatenate([vectors[n].reshape(k, P).T for n, (_, k) in COLS.items()], axis=1),
    }
    arrays = {f"in_{k}": np.ascontiguousarray(v) for k, v in arrays.items()}
    nc = bacc.Bacc("TRN2", target_bir_lowering=False, num_devices=1)
    args = [nc.dram_tensor(k, v.shape, mybir.dt.from_np(v.dtype), kind="ExternalInput").ap() for k, v in arrays.items()]
    args.append(nc.dram_tensor("out", (N, D), F32, kind="ExternalOutput").ap())
    gnn_program(nc, *args)
    r = run_bass_kernel_spmd(nc, [arrays], core_ids=[0])
    return r.results[0]["out"]
```

```python
from contextlib import ExitStack

import concourse.bass as bass
from concourse import mybir

F32 = mybir.dt.float32
F32R = mybir.dt.float32r
I32 = mybir.dt.int32
ALU = mybir.AluOpType
ACT = mybir.ActivationFunctionType

P = 128
N, E, D = 1250, 21250, 512
ED0, ED1 = 64, 128
H0 = 2 * D
EPS = 1e-5
KD = D // P
KH = H0 // P

GROUP = 12
TILES = -(-E // (P * 2 * GROUP)) * 2 * GROUP
GROUPS = TILES // GROUP
STEP = 2 * GROUP
STEPS = TILES // STEP
CHUNK = 4
ROWS = (-(-N // P) + 1) * P
BLOCKS = -(-N // P)

RAW, EDGE_BANKS, MSG, HOT, RING = 8, 4, 4, 3, 3
RELU_LAG, SUM_LAG = 6, 8

XB = 2
XQ = BLOCKS // XB
NODE_CHUNKS = [(0, 418), (418, 416), (834, 416)]
COLS = {}
for _name, _k in (("b1", KH), ("g1", KH), ("beta1", KH), ("b2", KD), ("g2", KD), ("beta2", KD),
                  ("b_ih", 3 * KD), ("b_hh", 3 * KD), ("gamma", KD), ("beta", KD),
                  ("run_mean", KD), ("run_var", KD), ("eps", 1)):
    COLS[_name] = (sum(w for _, w in COLS.values()), _k)
NCOLS = sum(w for _, w in COLS.values())

KB = 1024


def rows_in(block):
    return min(P, N - block * P)


def gnn_program(nc, x, src, dst, attr0, attr1, W_e, b_e, W1, W2, V1h, V1e, v_b1, V2, v_b2, Wg, cols, out):
    with ExitStack() as ctx:
        base = -(-nc.sbuf_base // 64) * 64
        A0 = base + 10 * KB + KB // 2
        B0 = A0 + 64 * KB

        def at(name, shape, dt, offset):
            return nc.alloc_sbuf_tensor_at(name, shape, dt, offset=offset)

        def sem(name):
            return ctx.enter_context(nc.semaphore(name))

        def psum(name, shape):
            return ctx.enter_context(nc.psum_tensor(name, shape, F32))

        small = [base]

        def keep(name, width, dt=F32, parts=P):
            t = at(name, [parts, width], dt, small[0])
            small[0] += -(-width * 4 // 64) * 64
            assert small[0] <= A0, name
            return t

        src_sb = keep("src_sb", TILES, I32)
        dst_i = keep("dst_i", TILES, I32)
        dst_f = keep("dst_f", TILES)
        in_window = keep("in_window", TILES)
        dst_left = keep("dst_left", TILES)
        iota_f = keep("iota_f", P)
        ident = keep("ident", P)
        ones = keep("ones", P)
        ones_r = keep("ones_r", 2, F32R)
        col = keep("col", NCOLS)
        stats = keep("stats", 2 * 18)
        moments = keep("moments", 2 * 4)
        minus_half = keep("minus_half", KD)
        one_eps = keep("one_eps", 1)
        gate_bias = keep("gate_bias", 2 * KD)
        bn_scale = keep("bn_scale", KD)
        bn_bias = keep("bn_bias", KD)
        base_sb = keep("base_sb", GROUPS)
        left_n = keep("left_n", 4)
        any_left = keep("any_left", 1, I32)
        idx_now = keep("idx_now", STEP, I32)
        lf_idx = keep("lf_idx", 1, I32)
        lf_dst = keep("lf_dst", 1)
        degree = keep("degree", 2 * BLOCKS)
        v_b2_hi = keep("v_b2_hi", D, F32R, 1)
        v_b2_lo = keep("v_b2_lo", D, F32R, 1)

        def vec(name, k=0):
            return col[:, COLS[name][0] + k:COLS[name][0] + k + 1]

        W1_hi = at("W1_hi", [P, KD, H0], F32R, A0)
        W1_lo = at("W1_lo", [P, KD, H0], F32R, A0 + 16 * KB)
        W2_hi = at("W2_hi", [P, KH, D], F32R, A0 + 32 * KB)
        W2_lo = at("W2_lo", [P, KH, D], F32R, A0 + 48 * KB)
        W1_raw = at("W1_raw", [P, KD, H0], F32, A0 + 16 * KB)
        W2_raw = at("W2_raw", [P, KH, D], F32, A0 + 48 * KB)
        x_in = at("x_in", [P, BLOCKS, D], F32, B0 + 84 * KB)
        xb = at("xb", [P, BLOCKS, D], F32, B0 + 104 * KB)
        zero_rows = at("zero_rows", [P, D + 2], F32, B0 + 124 * KB)
        be_bc = at("be_bc", [P, D], F32, B0 + 127 * KB)
        iota_i = at("iota_i", [P, P], I32, B0 + 130 * KB)

        raw = [at("raw0", [P, RAW, D], F32, B0), at("raw1", [P, RAW, D], F32, B0 + 80 * KB)]
        attr = [at("attr0_sb", [P, RING, CHUNK * P], F32, B0 + 42 * KB),
                at("attr1_sb", [P, RING, CHUNK * P], F32, B0 + 12 * KB)]
        attr_hl = at("attr_hl", [P, RING, CHUNK * P], F32R, B0 + 48 * KB)
        attr_hi = at("attr_hi", [P, RING, CHUNK * P], F32R, B0)
        attr_lo = at("attr_lo", [P, RING, CHUNK * P], F32R, B0 + 6 * KB)
        E0, E1 = B0 + 20 * KB, A0 + 40 * KB
        msg_hi = [at("msg_hi0", [P, MSG, D], F32R, E0), at("msg_hi1", [P, MSG, D], F32R, E1)]
        msg_lo = [at("msg_lo0", [P, MSG, D], F32R, E0 + 8 * KB), at("msg_lo1", [P, MSG, D], F32R, E1 + 8 * KB)]
        hot = [at("hot0", [P, HOT, CHUNK, P], F32R, B0 + 36 * KB), at("hot1", [P, HOT, CHUNK, P], F32R, A0 + 34 * KB)]
        sums = [at("sums0", [P, 2, D + 4], F32, B0 + 54 * KB), at("sums1", [P, 2, D + 4], F32, E1 + 16 * KB)]
        lf_msg = [at("lf_msg0", [P, D], F32, B0 + 60 * KB), at("lf_msg1", [P, D], F32, A0 + 62 * KB)]
        lf_hot = [at("lf_hot0", [P, P], F32, B0 + 18 * KB), at("lf_hot1", [P, P], F32, A0 + 61 * KB)]
        We_raw = at("We_raw", [P, D], F32, B0 + 62 * KB)
        We_hi = at("We_hi", [P, D], F32R, B0 + 64 * KB)
        We_lo = at("We_lo", [P, D], F32R, B0 + 66 * KB)
        V1e_sb = at("V1e_sb", [P, D], F32, A0 + 28 * KB)
        V1e_hi = at("V1e_hi", [P, D], F32R, A0 + 30 * KB)
        V1e_lo = at("V1e_lo", [P, D], F32R, A0 + 32 * KB)

        h_hi = at("h_hi", [P, KD, N], F32R, B0)
        h_lo = at("h_lo", [P, KD, N], F32R, B0 + 20 * KB)
        stage0 = at("stage0", [P, 4, D], F32, B0 + 40 * KB)
        s_hi = at("s_hi", [P, KH, N], F32R, B0 + 40 * KB)
        s_lo = at("s_lo", [P, KH, N], F32R, B0 + 80 * KB)
        pre = at("pre", [P, 2, N], F32, B0 + 120 * KB)
        y_t = at("y_t", [P, KD, N], F32, B0)

        rows = at("rows", [P, BLOCKS, D], F32, A0)
        V1h_raw = at("V1h_raw", [P, KD, D], F32, A0 + 20 * KB)
        V1h_hi = at("V1h_hi", [P, KD, D], F32R, B0 + 20 * KB)
        V1h_lo = at("V1h_lo", [P, KD, D], F32R, B0 + 28 * KB)
        x1_hi = at("x1_hi", [P, KD, N], F32R, B0 + 40 * KB)
        x1_lo = at("x1_lo", [P, KD, N], F32R, B0 + 60 * KB)
        table_sb = at("table_sb", [P, 2, D], F32, B0 + 120 * KB)
        vb1_bc = at("vb1_bc", [P, D], F32, B0 + 36 * KB)
        lnx = at("lnx", [P, 2, D], F32, B0 + 126 * KB)

        stage1 = at("stage1", [P, 2, D], F32, A0 + 20 * KB)
        V2_raw = at("V2_raw", [P, KD, D], F32, A0 + 20 * KB)
        V2_hi = at("V2_hi", [P, KD, D], F32R, B0 + 100 * KB)
        V2_lo = at("V2_lo", [P, KD, D], F32R, B0 + 108 * KB)
        r_hi = at("r_hi", [P, KD, N], F32R, B0 + 80 * KB)
        r_lo = at("r_lo", [P, KD, N], F32R, B0 + 20 * KB)
        deg_r = at("deg_r", [2, N], F32R, B0 + 128 * KB)
        v_b2_raw = at("v_b2_raw", [1, D], F32, B0 + 38 * KB)
        m_hi = at("m_hi", [P, KD, N], F32R, A0 + 32 * KB)
        m_lo = at("m_lo", [P, KD, N], F32R, A0 + 52 * KB)
        Wg_raw = at("Wg_raw", [P, 2 * KD * 3 * P], F32, A0 + 20 * KB)
        Wg_hi = [at("Wg_hi0", [P, 2, KD, 3, P], F32R, B0 + 8 * KB), at("Wg_hi1", [P, 2, KD, 3, P], F32R, B0 + 20 * KB)]
        Wg_lo = [at("Wg_lo0", [P, 2, KD, 3, P], F32R, B0 + 116 * KB), at("Wg_lo1", [P, 2, KD, 3, P], F32R, B0 + 80 * KB)]
        g_r = at("g_r", [P, 2, 418], F32, B0 + 32 * KB)
        g_z = at("g_z", [P, 2, 418], F32, B0 + 36 * KB)
        g_n = at("g_n", [P, 418], F32, B0 + 112 * KB)
        g_d = at("g_d", [P, 418], F32, B0 + 114 * KB)
        bn_t = at("bn_t", [P, KD, N], F32, B0 + 92 * KB)
        fin = at("fin", [P, 2, D], F32, A0 + 20 * KB)
        assert B0 + 128 * KB + 4 * N <= nc.sbuf_usable_end

        xb_dram = nc.dram_tensor("xb_dram", [BLOCKS * P, D], F32).ap()
        table_dram = nc.dram_tensor("table_dram", [N, D], F32).ap()
        sum_dram = [nc.dram_tensor("sum0_dram", [ROWS, D + 2], F32).ap(),
                    nc.dram_tensor("sum1_dram", [ROWS, D], F32).ap()]
        tables = [xb_dram, table_dram]

        bank = [psum(f"bank{b}", [P, 512]) for b in range(8)]
        e_bank = bank[0:EDGE_BANKS]
        sum_bank = bank[4:6]
        degree_bank = bank[6:8]
        misc = bank[6]
        lf_bank = bank[7]

        idx_in, cols_in, be_in, we_in, w1_in, w2_in = map(sem, ("idx_in", "cols_in", "be_in", "we_in", "w1_in", "w2_in"))
        x_in_done = [sem(f"x_in_done{q}") for q in range(XQ)]
        pool_consts, ident_ready, dst_ready, window_ready, base_ready = map(
            sem, ("pool_consts", "ident_ready", "dst_ready", "window_ready", "base_ready"))
        left_ready, left_counted, flag_ready = map(sem, ("left_ready", "left_counted", "flag_ready"))
        eps_ready, xb_ready, start_ready, zero_ready, xb_out = map(
            sem, ("eps_ready", "xb_ready", "start_ready", "zero_ready", "xb_out"))
        start_out = [sem("start_out0"), sem("start_out1")]
        we_split, w1_split, w2_split = map(sem, ("we_split", "w1_split", "w2_split"))
        stage_in = [[sem(f"stage_in0_{i}") for i in range(4)], [sem(f"stage_in1_{i}") for i in range(2)]]
        turned, turned_high, turned_low = ([sem(f"{n}{L}") for L in range(2)] for n in ("turned", "turned_high", "turned_low"))
        mlp_mm, mlp_out, silu_done, s_split = map(sem, ("mlp_mm", "mlp_out", "silu_done", "s_split"))
        var_ready, rstd_ready, bn_ready = map(sem, ("var_ready", "rstd_ready", "bn_ready"))
        rows_in_done, v1h_in, v1e_in, vb1_in, vb2_in, v2_in, wg_in = map(
            sem, ("rows_in_done", "v1h_in", "v1e_in", "vb1_in", "vb2_in", "v2_in", "wg_in"))
        v1h_split, v1e_split, vb2_split, v2_split, wg_split = map(
            sem, ("v1h_split", "v1e_split", "vb2_split", "v2_split", "wg_split"))
        degree_in = sem("degree_in")
        back_turned, back_added, x1_ready, x1_turned, x1_high, x1_low = map(
            sem, ("back_turned", "back_added", "x1_ready", "x1_turned", "x1_high", "x1_low"))
        table_mm, table_ready = map(sem, ("table_mm", "table_ready"))
        table_out = [sem(f"table_out{i}") for i in range(2)]
        m_mm, m_high, m_low = map(sem, ("m_mm", "m_high", "m_low"))
        gate_mm, r_done, z_done, n_in, n_done, gru_done = map(
            sem, ("gate_mm", "r_done", "z_done", "n_in", "n_done", "gru_done"))
        fin_turned, fin_added, fin_ready = map(sem, ("fin_turned", "fin_added", "fin_ready"))
        fin_out = [sem(f"fin_out{i}") for i in range(2)]
        gate_bias_ready = sem("gate_bias_ready")
        dve_step = sem("dve_step")
        (idx_copied, idx_read, edge_mm, edge_out, relued_act, relued_dve, low, hot_ready, summed, sum_out, accumulated,
         attr_high, attr_split) = ([sem(f"{n}{L}") for L in range(2)] for n in (
             "idx_copied", "idx_read", "edge_mm", "edge_out", "relued_act", "relued_dve", "low", "hot_ready", "summed",
             "sum_out", "accumulated", "attr_high", "attr_split"))
        gathered = [[sem(f"gathered{L}_{i}") for i in range(RAW)] for L in range(2)]
        attr_in = [[sem(f"attr_in{L}_{i}") for i in range(RING)] for L in range(2)]
        lf_free, lf_idx_ready, lf_gathered, lf_attr_in, lf_mm, lf_msg_steps, lf_hot_ready, lf_summed, lf_copied, lf_added = (
            [sem(f"{n}{L}") for L in range(2)] for n in (
                "lf_free", "lf_idx_ready", "lf_gathered", "lf_attr_in", "lf_mm", "lf_msg_steps", "lf_hot_ready",
                "lf_summed", "lf_copied", "lf_added"))

        attr_dram, attr_parts = [attr0, attr1], [ED0, ED1]
        width = [D + 2, D]
        CPS = STEP // CHUNK
        left_value = any_left[0:1, 0:1]
        LF_ALL = 16 * TILES * BLOCKS

        def wait(engine, semaphore, value):
            if not isinstance(value, int) or value > 0:
                engine.wait_ge(semaphore, value)

        def relu_on_dve(t):
            return t % 3 == 0

        def wait_gathered(engine, L, it, t):
            engine.wait_ge(gathered[L][t % RAW], it * (STEP // RAW * 16) + (t // RAW + 1) * 16)

        def feature_major(b):
            return b[:, :].rearrange("p (k n) -> p k n", k=KD)

        block = ctx.enter_context(nc.Block())

        @block.sync
        def _(sp):
            def load_chunk(L, it, c):
                rows_of = attr_parts[L]
                wait(sp, attr_split[L], it * CPS + c - RING + 1)
                for h in range(P // rows_of):
                    sp.dma_start(attr[L][h * rows_of:(h + 1) * rows_of, c % RING, :],
                                 attr_dram[L][:, bass.ds(it * (STEP * P) + c * CHUNK * P, CHUNK * P)]
                                 ).then_inc(attr_in[L][c % RING], 16)

            def load_leftover_attr(L):
                sp.wait_ge(flag_ready, 1)
                left = sp.value_load(left_value, min_val=0, max_val=1)
                with sp.If(left > 0):
                    with sp.Fori(0, TILES) as t:
                        sp.wait_ge(lf_free[L], t + 1)
                        sp.dma_start(attr[L][0:attr_parts[L], 0, 0:P],
                                     attr_dram[L][:, bass.ds(t * P, P)]).then_inc(lf_attr_in[L], 16)
                    sp.wait_ge(lf_added[L], LF_ALL)

            def load_sums(L, stage, slots):
                sp.wait_ge(accumulated[L], 16 * GROUPS)
                for b in range(BLOCKS):
                    if b >= slots:
                        sp.wait_ge(turned[L], b - slots + 1)
                    sp.dma_start(stage[:, b % slots, :], sum_dram[L][b * P:(b + 1) * P, 0:D]
                                 ).then_inc(stage_in[L][b % slots], 16)

            by_block = x.rearrange("(t p) d -> p t d", p=P)
            xb_rows = xb_dram.rearrange("(t p) d -> p t d", p=P)
            sp.dma_start(be_bc[:, :], b_e.partition_broadcast(P)).then_inc(be_in, 16)
            for q in range(XQ):
                sp.dma_start(x_in[:, q * XB:(q + 1) * XB, :], by_block[:, q * XB:(q + 1) * XB, :]).then_inc(x_in_done[q], 16)
                if q == 1:
                    sp.dma_start(dst_i[:, :], dst).then_inc(idx_in, 16)
                    sp.dma_start(src_sb[:, :], src).then_inc(idx_in, 16)
                    sp.dma_start(col[:, :], cols).then_inc(cols_in, 16)
                    for h in range(2):
                        sp.dma_start(We_raw[h * ED0:(h + 1) * ED0, :], W_e).then_inc(we_in, 16)
            load_chunk(0, 0, 0)
            for q in range(XQ):
                sp.wait_ge(xb_ready, q + 1)
                sp.dma_start(xb_rows[:, q * XB:(q + 1) * XB, :], xb[:, q * XB:(q + 1) * XB, :]).then_inc(xb_out, 16)
            load_chunk(0, 0, 1)
            load_chunk(0, 0, 2)
            sp.dma_start(W1_raw[:, :, :], W1.rearrange("(k p) n -> p k n", p=P)).then_inc(w1_in, 16)
            sp.wait_ge(zero_ready, 1)
            sp.dma_start(sum_dram[0][BLOCKS * P:ROWS, :], zero_rows[:, :]).then_inc(start_out[0], 16)
            sp.dma_start(sum_dram[0][0:BLOCKS * P, D:D + 2].rearrange("(t p) d -> p t d", p=P),
                         zero_rows[:, 0:2 * BLOCKS].rearrange("p (t d) -> p t d", d=2)).then_inc(start_out[0], 16)
            sp.wait_ge(start_ready, 1)
            sp.dma_start(sum_dram[0][0:BLOCKS * P, 0:D].rearrange("(t p) d -> p t d", p=P),
                         x_in[:, :, :]).then_inc(start_out[0], 16)
            for c in range(2, CPS):
                load_chunk(0, 0, c + 1)
            sp.dma_start(W2_raw[:, :, :], W2.rearrange("(k p) n -> p k n", p=P)).then_inc(w2_in, 16)
            with sp.Fori(1, STEPS) as it:
                for c in range(CPS):
                    load_chunk(0, it, c + 1)
            for b in range(ROWS // P):
                sp.dma_start(sum_dram[1][b * P:(b + 1) * P, :], zero_rows[:, 0:D]).then_inc(start_out[1], 16)
            load_leftover_attr(0)
            sp.wait_ge(start_out[1], 16 * (ROWS // P))
            load_sums(0, stage0, 4)
            sp.dma_start(degree[:, :].rearrange("p (t d) -> p t d", d=2),
                         sum_dram[0][0:BLOCKS * P, D:D + 2].rearrange("(t p) d -> p t d", p=P)).then_inc(degree_in, 16)
            sp.wait_ge(mlp_mm, KH * 3)
            sp.dma_start(V1h_raw[:, :, :], V1h.rearrange("(k p) n -> p k n", p=P)).then_inc(v1h_in, 16)
            sp.dma_start(rows[:, :, :], by_block).then_inc(rows_in_done, 16)
            sp.dma_start(V1e_sb[:, :], V1e).then_inc(v1e_in, 16)
            sp.dma_start(vb1_bc[:, :], v_b1.partition_broadcast(P)).then_inc(vb1_in, 16)
            sp.dma_start(v_b2_raw[:, :], v_b2).then_inc(vb2_in, 16)
            for b in range(BLOCKS):
                sp.wait_ge(table_ready, b + 1)
                sp.dma_start(table_dram[b * P:b * P + rows_in(b), :], table_sb[0:rows_in(b), b % 2, :]
                             ).then_inc(table_out[b % 2], 16)
                if b == BLOCKS // 2:
                    sp.wait_ge(back_turned, BLOCKS)
                    for c in range(RING):
                        load_chunk(1, 0, c)
            sp.wait_ge(v1h_split, 1)
            sp.dma_start(V2_raw[:, :, :], V2.rearrange("(k p) n -> p k n", p=P)).then_inc(v2_in, 16)
            for c in range(RING, CPS + 1):
                load_chunk(1, 0, c)
            with sp.Fori(1, STEPS) as it:
                for c in range(CPS):
                    load_chunk(1, it, c + 1)
            load_leftover_attr(1)
            sp.wait_ge(v2_split, 1)
            load_sums(1, stage1, 2)
            sp.wait_ge(turned[1], BLOCKS)
            for m in range(KD):
                if m:
                    sp.wait_ge(wg_split, m)
                sp.dma_start(Wg_raw[:, :], Wg[m]).then_inc(wg_in, 16)
            for b in range(BLOCKS):
                sp.wait_ge(fin_ready, b + 1)
                sp.dma_start(out[b * P:b * P + rows_in(b), :], fin[0:rows_in(b), b % 2, :]).then_inc(fin_out[b % 2], 16)
            for i in range(2):
                sp.wait_ge(fin_out[i], 16 * (BLOCKS // 2))

        @block.gpsimd
        def _(pool):
            def in_register(name, value):
                if isinstance(value, int):
                    return value
                pool.reg_mov(counts[name], pool.to_reg(value))
                return counts[name]

            counts = {name: pool.alloc_register(f"count_{name}") for name in ("one", "other")}

            def accumulate(L, g, slot, very_first):
                first_node = pool.value_load(dst_i[0:1, bass.ds((g - 1) * GROUP, 1)], min_val=0, max_val=ROWS - P)
                summed_there = in_register("one", g)
                landed = in_register("other", 16 * (g - 1))
                pool.wait_ge(start_out[L], 16 * (3, ROWS // P)[L])
                pool.wait_ge(sum_out[L], summed_there)
                if not very_first:
                    pool.wait_ge(accumulated[L], landed)
                pool.dma_start(sum_dram[L][bass.ds(first_node, P), :], sums[L][:, slot, 0:width[L]],
                               accum_op=ALU.add).then_inc(accumulated[L], 16)

            def wait_table(L):
                if L == 0:
                    pool.wait_ge(xb_out, 16 * XQ)
                else:
                    for i in range(2):
                        pool.wait_ge(table_out[i], 16 * (BLOCKS // 2))

            def gather_step(L, it, first):
                for j in range(STEP):
                    i, half = it * STEP + j, j // GROUP
                    if j % GROUP == 0:
                        if not first:
                            pool.wait_ge(idx_read[L], i - GROUP)
                        nc.gpsimd.tensor_copy(idx_now[:, half * GROUP:(half + 1) * GROUP],
                                              src_sb[:, bass.ds(i, GROUP)]).then_inc(idx_copied[L], 1)
                    copied, out_there = in_register("one", it * 2 + half + 1), in_register("other", i + 1)
                    wait_table(L)
                    if j % GROUP == 0:
                        pool.wait_ge(idx_copied[L], copied)
                    pool.wait_ge(edge_out[L], out_there)
                    pool.indirect_dma_start(raw[L][:, j % RAW, :], None, tables[L],
                                            bass.IndirectOffsetOnAxis(ap=idx_now[:, j:j + 1], axis=0),
                                            compute_op=ALU.add, engine_sem=idx_read[L]).then_inc(gathered[L][j % RAW], 16)
                    if j % GROUP == GROUP - 2 and (not first or half):
                        accumulate(L, it * 2 + half, 1 - half, first)

            def gather_leftover(L):
                pool.wait_ge(flag_ready, 1)
                left = pool.value_load(left_value, min_val=0, max_val=1)
                with pool.If(left > 0):
                    with pool.Fori(0, TILES) as t:
                        pool.wait_ge(lf_free[L], t + 1)
                        nc.gpsimd.tensor_copy(lf_idx[:, :], src_sb[:, bass.ds(t, 1)]).then_inc(lf_idx_ready[L], 1)
                        copied = in_register("one", t + 1)
                        wait_table(L)
                        pool.wait_ge(lf_idx_ready[L], copied)
                        pool.indirect_dma_start(raw[L][:, 0, :], None, tables[L],
                                                bass.IndirectOffsetOnAxis(ap=lf_idx[:, :], axis=0)
                                                ).then_inc(lf_gathered[L], 16)
                        for b in range(BLOCKS):
                            copied = in_register("one", t * BLOCKS + b + 1)
                            pool.wait_ge(start_out[L], 16 * (3, ROWS // P)[L])
                            pool.wait_ge(lf_copied[L], copied)
                            pool.dma_start(sum_dram[L][b * P:(b + 1) * P, :], sums[L][:, 0, 0:width[L]],
                                           accum_op=ALU.add).then_inc(lf_added[L], 16)
                            pool.wait_ge(lf_added[L], t * (16 * BLOCKS) + 16 * (b + 1))

            def rstd(n, slot):
                pool.wait_ge(var_ready, n)
                nc.gpsimd.tensor_tensor(moments[:, slot * 4 + 2:slot * 4 + 3], moments[:, slot * 4 + 1:slot * 4 + 2],
                                        minus_half[:, 0:1], ALU.pow).then_inc(rstd_ready, 1)

            nc.gpsimd.iota(iota_i[:, :], [[1, P]], base=0, channel_multiplier=0).then_inc(pool_consts, 1)
            nc.gpsimd.memset(minus_half[:, :], -0.5).then_inc(pool_consts, 1)
            nc.gpsimd.memset(ones[:, :], 1.0).then_inc(pool_consts, 1)
            nc.gpsimd.memset(ident[:, :], 0.0).then_inc(pool_consts, 1)
            pool.wait_ge(pool_consts, 4)
            nc.gpsimd.affine_select(out=ident[:, :], in_=ident[:, :], compare_op=ALU.not_equal, fill=1.0, base=0,
                                    pattern=[[-1, P]], channel_multiplier=1).then_inc(ident_ready, 1)
            pool.wait_ge(idx_in, 32)
            n = 0
            for L in range(2):
                wait_table(L)
                gather_step(L, 0, True)
                with pool.Fori(1, STEPS) as it:
                    gather_step(L, it, False)
                accumulate(L, GROUPS, 1, False)
                gather_leftover(L)
                if L == 0:
                    for c in range(KH + KD):
                        n += 1
                        rstd(n, c % 2)
                else:
                    n += 1
                    pool.wait_ge(var_ready, n)
                    nc.gpsimd.tensor_tensor(bn_scale[:, :], bn_scale[:, :], minus_half[:, :],
                                            ALU.pow).then_inc(rstd_ready, 1)
                for b in range(BLOCKS):
                    n += 1
                    rstd(n, b % 2)

        @block.tensor
        def _(pe):
            def product(acc, terms, start=True):
                passes = [(a, b) for a_hi, a_lo, b_hi, b_lo in terms for a, b in ((a_hi, b_hi), (a_hi, b_lo), (a_lo, b_hi))]
                for i, (a, b) in enumerate(passes):
                    mm = nc.tensor.matmul(acc, a, b, start=start and i == 0, stop=i == len(passes) - 1)
                return mm

            def edge_product(L, it, j):
                c, ks = j // CHUNK, slice(j % CHUNK * P, (j % CHUNK + 1) * P)
                if j % CHUNK == 0:
                    pe.wait_ge(attr_split[L], it * CPS + c + 1)
                wait(pe, edge_out[L], it * STEP + j - EDGE_BANKS + 1)
                acc = e_bank[j % EDGE_BANKS][:, :]
                if L == 0:
                    passes = [(attr_hl, We_hi), (attr_hl, We_lo)]
                else:
                    passes = [(attr_hi, V1e_hi), (attr_hi, V1e_lo), (attr_lo, V1e_hi)]
                for n, (features, W) in enumerate(passes):
                    mm = nc.tensor.matmul(acc, features[:, c % RING, ks], W[:, :], start=n == 0, stop=n == len(passes) - 1)
                mm.then_inc(edge_mm[L], 1)

            def sum_product(L, it, t):
                start, stop, half = t % GROUP == 0, t % GROUP == GROUP - 1, t // GROUP % 2
                pe.wait_ge(low[L], it * STEP + t + 1)
                pe.wait_ge(hot_ready[L], it * CPS + t // CHUNK + 1)
                if start:
                    wait(pe, sum_out[L], it * 2 + t // GROUP - 1)
                acc, h = sum_bank[half][:, :], hot[L][:, t // CHUNK % HOT, t % CHUNK, :]
                nc.tensor.matmul(acc, h, msg_hi[L][:, t % MSG, :], start=start, stop=False)
                mm = nc.tensor.matmul(acc, h, msg_lo[L][:, t % MSG, :], start=False, stop=stop)
                if L == 0:
                    mm = nc.tensor.matmul(degree_bank[half][:, 0:2], h, ones_r[:, :], start=start, stop=stop)
                mm.then_inc(summed[L], 1)

            def edges(L):
                for j in range(STEP):
                    edge_product(L, 0, j)
                    if j >= SUM_LAG:
                        sum_product(L, 0, j - SUM_LAG)
                with pe.Fori(1, STEPS) as it:
                    for j in range(STEP):
                        edge_product(L, it, j)
                        sum_product(L, it, j - SUM_LAG)
                for t in range(STEP - SUM_LAG, STEP):
                    sum_product(L, STEPS - 1, t)

            def leftover(L):
                pe.wait_ge(flag_ready, 1)
                left = pe.value_load(left_value, min_val=0, max_val=1)
                with pe.If(left > 0):
                    K, W = attr_parts[L], (We_raw, V1e_sb)[L]
                    with pe.Fori(0, TILES) as t:
                        pe.wait_ge(lf_attr_in[L], t * 16 + 16)
                        pe.wait_ge(lf_free[L], t + 1)
                        nc.tensor.matmul(lf_bank[:, :], attr[L][0:K, 0, 0:P], W[0:K, :], start=True,
                                         stop=True).then_inc(lf_mm[L], 1)
                        for b in range(BLOCKS):
                            pe.wait_ge(lf_hot_ready[L], t * BLOCKS + b + 1)
                            mm = nc.tensor.matmul(sum_bank[0][:, :], lf_hot[L][:, :], lf_msg[L][:, :], start=True, stop=True)
                            if L == 0:
                                mm = nc.tensor.matmul(misc[:, 0:2], lf_hot[L][:, :], ones[:, 0:2], start=True, stop=True)
                            mm.then_inc(lf_summed[L], 1)
                    pe.wait_ge(lf_added[L], LF_ALL)

            def turn_sums(L, stage, slots):
                if L == 1:
                    pe.wait_ge(degree_in, 16)
                for b in range(BLOCKS):
                    pe.wait_ge(stage_in[L][b % slots], 16 * (b // slots + 1))
                    if b >= 2:
                        pe.wait_ge(turned_low[L], b - 1)
                    for k in range(KD):
                        tr = nc.tensor.transpose(bank[b % 2][:, k * P:(k + 1) * P], stage[:, b % slots, k * P:(k + 1) * P],
                                                 ident[:, :])
                    if L == 1:
                        tr = nc.tensor.transpose(bank[2 + b % 2][0:2, 0:P], degree[:, 2 * b:2 * b + 2], ident[:, :])
                    tr.then_inc(turned[L], 1)

            pe.wait_ge(pool_consts, 4)
            pe.wait_ge(dst_ready, 1)
            nc.tensor.matmul(misc[:, 0:GROUPS], ones[0:1, :], dst_f[0:1, 0:TILES:GROUP], start=True,
                             stop=True).then_inc(base_ready, 1)
            pe.wait_ge(left_ready, 1)
            nc.tensor.matmul(misc[0:1, 16:17], left_n[:, 0:1], ones[:, 0:1], start=True, stop=True).then_inc(left_counted, 1)
            pe.wait_ge(we_split, 1)
            edges(0)
            leftover(0)
            pe.wait_ge(ident_ready, 1)
            turn_sums(0, stage0, 4)

            pe.wait_ge(turned_low[0], BLOCKS)
            pe.wait_ge(w1_split, 1)
            n = 0
            for W_hi, W_lo, X_hi, X_lo, K, M in ((W1_hi, W1_lo, h_hi, h_lo, KD, KH), (W2_hi, W2_lo, s_hi, s_lo, KH, KD)):
                if K == KH:
                    pe.wait_ge(s_split, KH)
                    pe.wait_ge(w2_split, 1)
                for m in range(M):
                    ms = slice(m * P, (m + 1) * P)
                    for a, w in NODE_CHUNKS:
                        if n >= 6:
                            pe.wait_ge(mlp_out, n - 5)
                        product(bank[2 + n % 6][:, 0:w],
                                [(W_hi[:, k, ms], W_lo[:, k, ms], X_hi[:, k, a:a + w], X_lo[:, k, a:a + w]) for k in range(K)]
                                ).then_inc(mlp_mm, 1)
                        n += 1

            pe.wait_ge(silu_done, KH + KD)
            pe.wait_ge(mlp_out, 3 * (KH + KD))
            for t in range(BLOCKS + 3):
                if t < BLOCKS:
                    r = rows_in(t)
                    if t >= 2:
                        pe.wait_ge(back_added, t - 1)
                    for k in range(KD):
                        tr = nc.tensor.transpose(bank[t % 2][0:r, k * P:(k + 1) * P], y_t[:, k, t * P:t * P + r], ident[:, :])
                    tr.then_inc(back_turned, 1)
                b = t - 2
                if 0 <= b < BLOCKS:
                    r = rows_in(b)
                    pe.wait_ge(x1_ready, b + 1)
                    if b >= 2:
                        pe.wait_ge(x1_low, b - 1)
                    for k in range(KD):
                        tr = nc.tensor.transpose(bank[2 + b % 2][:, k * P:k * P + r], rows[0:r, b, k * P:(k + 1) * P],
                                                 ident[0:r, 0:r])
                    tr.then_inc(x1_turned, 1)
                b = t - 3
                if b >= 0:
                    r = rows_in(b)
                    pe.wait_ge(x1_low, b + 1)
                    if b == 0:
                        pe.wait_ge(v1h_split, 1)
                    if b >= 2:
                        pe.wait_ge(table_ready, b - 1)
                    product(bank[4 + b % 2][0:r, :],
                            [(x1_hi[:, k, b * P:b * P + r], x1_lo[:, k, b * P:b * P + r], V1h_hi[:, k, :], V1h_lo[:, k, :])
                             for k in range(KD)]).then_inc(table_mm, 1)
            pe.wait_ge(table_ready, BLOCKS)
            pe.wait_ge(v1e_split, 1)
            edges(1)
            leftover(1)
            turn_sums(1, stage1, 2)

            pe.wait_ge(turned_low[1], BLOCKS)
            pe.wait_ge(v2_split, 1)
            pe.wait_ge(vb2_split, 1)
            n = 0
            for m in range(KD):
                ms = slice(m * P, (m + 1) * P)
                for a, w in NODE_CHUNKS:
                    if n >= 4:
                        pe.wait_ge(m_low, n - 3)
                    acc = bank[4 + n % 4][:, 0:w]
                    nc.tensor.matmul(acc, v_b2_hi[0:1, ms], deg_r[0:1, a:a + w], start=True, stop=False)
                    nc.tensor.matmul(acc, v_b2_lo[0:1, ms], deg_r[0:1, a:a + w], start=False, stop=False)
                    product(acc, [(V2_hi[:, k, ms], V2_lo[:, k, ms], r_hi[:, k, a:a + w], r_lo[:, k, a:a + w])
                                  for k in range(KD)], start=False).then_inc(m_mm, 1)
                    n += 1

            pe.wait_ge(m_low, n)
            n = 0
            for m in range(KD):
                pe.wait_ge(wg_split, m + 1)
                for a, w in NODE_CHUNKS:
                    def gate(source, g):
                        X_hi, X_lo = ((m_hi, m_lo), (x1_hi, x1_lo))[source]
                        return [(Wg_hi[m % 2][:, source, k, g, :], Wg_lo[m % 2][:, source, k, g, :],
                                 X_hi[:, k, a:a + w], X_lo[:, k, a:a + w]) for k in range(KD)]
                    if n >= 2:
                        pe.wait_ge(z_done, n - 1)
                        pe.wait_ge(n_in, n - 1)
                    four = bank[4 * (n % 2):4 * (n % 2) + 4]
                    product(four[0][:, 0:w], gate(0, 0) + gate(1, 0)).then_inc(gate_mm, 1)
                    product(four[1][:, 0:w], gate(1, 2)).then_inc(gate_mm, 1)
                    product(four[2][:, 0:w], gate(0, 2)).then_inc(gate_mm, 1)
                    product(four[3][:, 0:w], gate(0, 1) + gate(1, 1)).then_inc(gate_mm, 1)
                    n += 1
            pe.wait_ge(gru_done, n)
            for b in range(BLOCKS):
                r = rows_in(b)
                if b >= 2:
                    pe.wait_ge(fin_added, b - 1)
                for k in range(KD):
                    tr = nc.tensor.transpose(bank[b % 2][0:r, k * P:(k + 1) * P], bn_t[:, k, b * P:b * P + r], ident[:, :])
                tr.then_inc(fin_turned, 1)

        @block.scalar
        def _(act):
            def copy(to, of):
                return nc.scalar.activation(to, of, ACT.Copy)

            def window_out(L, g, slot, first):
                act.wait_ge(summed[L], g * GROUP)
                if not first:
                    act.wait_ge(accumulated[L], 16 * (g - 2))
                if L == 0:
                    copy(sums[0][:, slot, D:D + 2], degree_bank[slot][:, 0:2])
                copy(sums[L][:, slot, 0:D], sum_bank[slot][:, :]).then_inc(sum_out[L], 1)

            def high_features(L, it, c):
                act.wait_ge(attr_in[L][c % RING], (it * (CPS // RING) + c // RING + 1) * (32, 16)[L])
                wait(act, edge_mm[L], it * STEP + (c - RING + 1) * CHUNK)
                copy((attr_hl, attr_hi)[L][:, c % RING, :], attr[L][:, c % RING, :]).then_inc(attr_high[L], 1)

            def message_high(L, it, t):
                if relu_on_dve(t):
                    return
                wait_gathered(act, L, it, t)
                wait(act, summed[L], it * STEP + t - MSG + 1)
                nc.scalar.activation(msg_hi[L][:, t % MSG, :], raw[L][:, t % RAW, :], ACT.Relu).then_inc(relued_act[L], 1)

            def edge_step(L, it, first):
                for j in range(STEP):
                    if j % CHUNK == 0:
                        high_features(L, it, j // CHUNK + 1)
                    act.wait_ge(edge_mm[L], it * STEP + j + 1)
                    wait(act, low[L], it * STEP + j - RAW + 1)
                    copy(raw[L][:, j % RAW, :], e_bank[j % EDGE_BANKS][:, :]).then_inc(edge_out[L], 1)
                    if not first or j >= RELU_LAG:
                        message_high(L, it, j - RELU_LAG)
                    if j % GROUP == SUM_LAG and (not first or j > GROUP):
                        window_out(L, it * 2 + j // GROUP, 1 - j // GROUP, first)

            def edges(L):
                high_features(L, 0, 0)
                edge_step(L, 0, True)
                with act.Fori(1, STEPS) as it:
                    edge_step(L, it, False)
                for t in range(STEP - RELU_LAG, STEP):
                    message_high(L, STEPS - 1, t)
                window_out(L, GROUPS, 1, False)
                act.wait_ge(flag_ready, 1)
                left = act.value_load(left_value, min_val=0, max_val=1)
                with act.If(left > 0):
                    act.wait_ge(lf_added[L], LF_ALL)

            def high_of_turned(L, hi):
                for b in range(BLOCKS):
                    r = rows_in(b)
                    act.wait_ge(turned[L], b + 1)
                    if L == 1:
                        copy(deg_r[:, b * P:b * P + r], bank[2 + b % 2][0:2, 0:r])
                    copy(hi[:, :, b * P:b * P + r], feature_major(bank[b % 2])[:, :, 0:r]).then_inc(turned_high[L], 1)

            act.wait_ge(eps_ready, 1)
            act.wait_ge(xb_ready, XQ)
            nc.scalar.activation(x_in[:, :, :], x_in[:, :, :], ACT.Identity, scale=one_eps[:, :]).then_inc(start_ready, 1)
            edges(0)
            high_of_turned(0, h_hi)

            def silu(c):
                act.wait_ge(bn_ready, c + 1)
                to = pre[:, c % 2, :] if c < KH else y_t[:, c - KH, :]
                at4 = 4 * (c % 2)
                nc.scalar.activation(to, pre[:, c % 2, :], ACT.Silu, scale=moments[:, at4 + 2:at4 + 3],
                                     bias=moments[:, at4 + 3:at4 + 4]).then_inc(silu_done, 1)

            n = 0
            for c in range(KH + KD):
                if c == KH:
                    silu(c - 1)
                for q, (a, w) in enumerate(NODE_CHUNKS):
                    act.wait_ge(mlp_mm, n + 1)
                    if c >= 2 and q == 0:
                        act.wait_ge(s_split, min(c - 1, KH))
                        act.wait_ge(silu_done, c - 1)
                    nc.scalar.activation(pre[:, c % 2, a:a + w], bank[2 + n % 6][:, 0:w], ACT.Identity,
                                         bias=vec("b1", c) if c < KH else vec("b2", c - KH)).then_inc(mlp_out, 1)
                    n += 1
                    if q == 0 and c not in (0, KH):
                        silu(c - 1)
            silu(KH + KD - 1)
            for b in range(BLOCKS):
                r = rows_in(b)
                act.wait_ge(x1_turned, b + 1)
                copy(x1_hi[:, :, b * P:b * P + r], feature_major(bank[2 + b % 2])[:, :, 0:r]).then_inc(x1_high, 1)
            edges(1)
            high_of_turned(1, r_hi)
            n = 0
            for m in range(KD):
                for a, w in NODE_CHUNKS:
                    act.wait_ge(m_mm, n + 1)
                    copy(m_hi[:, m, a:a + w], bank[4 + n % 4][:, 0:w]).then_inc(m_high, 1)
                    n += 1
            act.wait_ge(gate_bias_ready, 1)
            n = 0
            for m in range(KD):
                for a, w in NODE_CHUNKS:
                    four = bank[4 * (n % 2):4 * (n % 2) + 4]
                    act.wait_ge(gate_mm, 4 * n + 1)
                    if n >= 2:
                        act.wait_ge(gru_done, n - 1)
                    nc.scalar.activation(g_r[:, n % 2, 0:w], four[0][:, 0:w], ACT.Sigmoid,
                                         bias=gate_bias[:, m:m + 1]).then_inc(r_done, 1)
                    act.wait_ge(n_in, n + 1)
                    if n:
                        act.wait_ge(gru_done, n)
                    nc.scalar.activation(g_n[:, 0:w], g_r[:, n % 2, 0:w], ACT.Tanh,
                                         bias=vec("b_ih", 2 * KD + m)).then_inc(n_done, 1)
                    act.wait_ge(gate_mm, 4 * n + 4)
                    nc.scalar.activation(g_z[:, n % 2, 0:w], four[3][:, 0:w], ACT.Sigmoid,
                                         bias=gate_bias[:, KD + m:KD + m + 1]).then_inc(z_done, 1)
                    n += 1

        @block.vector
        def _(dve):
            steps = [0]

            def link(ins):
                steps[0] += 1
                ins.then_inc(dve_step, 1)
                dve.wait_ge(dve_step, steps[0])

            def low_part(to, value, high):
                return nc.vector.tensor_tensor(to, value, high.bitcast(F32), ALU.subtract)

            def split(hi, lo, raw):
                link(nc.vector.tensor_copy(hi, raw))
                return low_part(lo, raw, hi)

            dve.wait_ge(cols_in, 16)
            nc.vector.tensor_scalar(one_eps[:, :], vec("eps"), 1.0, None, ALU.add).then_inc(eps_ready, 1)
            dve.wait_ge(idx_in, 32)
            nc.vector.tensor_copy(dst_f[:, :], dst_i[:, :]).then_inc(dst_ready, 1)
            dve.wait_ge(pool_consts, 4)
            nc.vector.tensor_copy(iota_f[:, :], iota_i[:, :])
            nc.vector.tensor_copy(ones_r[:, :], ones[:, 0:2])
            dve.wait_ge(base_ready, 1)
            link(nc.vector.tensor_copy(base_sb[:, :], misc[:, 0:GROUPS]))
            for g in range(GROUPS):
                gs = slice(g * GROUP, (g + 1) * GROUP)
                i = nc.vector.tensor_scalar(in_window[:, gs], dst_f[:, gs], base_sb[:, g:g + 1], None, ALU.subtract)
            link(i)
            link(nc.vector.tensor_scalar(dst_left[:, :], in_window[:, :], 0.0, None, ALU.is_lt))
            link(nc.vector.scalar_tensor_tensor(dst_left[:, :], in_window[:, :], float(P - 1), dst_left[:, :],
                                                ALU.is_gt, ALU.add))
            link(nc.vector.scalar_tensor_tensor(dst_left[:, :], dst_f[:, :], 0.0, dst_left[:, :], ALU.is_ge, ALU.mult))
            link(nc.vector.tensor_reduce(left_n[:, 0:1], dst_left[:, :], mybir.AxisListType.X, ALU.add))
            link(nc.vector.scalar_tensor_tensor(dst_left[:, :], dst_f[:, :], 1.0, dst_left[:, :], ALU.add, ALU.mult))
            link(nc.vector.tensor_scalar(dst_left[:, :], dst_left[:, :], -1.0, None, ALU.add))
            nc.vector.nop().then_inc(window_ready, 1)
            nc.vector.nop().then_inc(left_ready, 1)
            dve.wait_ge(left_counted, 1)
            nc.vector.tensor_scalar(any_left[0:1, :], misc[0:1, 16:17], 0.0, None, ALU.is_gt).then_inc(flag_ready, 1)
            dve.wait_ge(we_in, 32)
            split(We_hi[:, :], We_lo[:, :], We_raw[:, :]).then_inc(we_split, 1)
            dve.wait_ge(be_in, 16)
            for q in range(XQ):
                dve.wait_ge(x_in_done[q], 16)
                xs = slice(q * XB, (q + 1) * XB)
                nc.vector.tensor_tensor(xb[:, xs, :], x_in[:, xs, :], be_bc[:, :].unsqueeze(1).broadcast_to([P, XB, D]),
                                        ALU.add).then_inc(xb_ready, 1)
            nc.vector.memset(zero_rows[:, :], 0.0).then_inc(zero_ready, 1)

            def low_features(L, it, c):
                dve.wait_ge(attr_high[L], it * CPS + c + 1)
                s = c % RING
                if L == 0:
                    i = low_part(attr_hl[ED0:P, s, :], attr[0][ED0:P, s, :], attr_hl[ED0:P, s, :])
                else:
                    i = low_part(attr_lo[:, s, :], attr[1][:, s, :], attr_hi[:, s, :])
                i.then_inc(attr_split[L], 1)

            def one_hots(L, it, c):
                wait(dve, summed[L], it * STEP + (c - HOT + 1) * CHUNK)
                nodes = iota_f[:, :].unsqueeze(1).broadcast_to([P, CHUNK, P])
                own = in_window[:, bass.ds(it * STEP + c * CHUNK, CHUNK)].unsqueeze(2).broadcast_to([P, CHUNK, P])
                nc.vector.tensor_tensor(hot[L][:, c % HOT, :, :], nodes, own, ALU.is_equal).then_inc(hot_ready[L], 1)

            def message_parts(L, it, t):
                wait_gathered(dve, L, it, t)
                wait(dve, summed[L], it * STEP + t - MSG + 1)
                if relu_on_dve(t):
                    nc.vector.tensor_scalar(msg_hi[L][:, t % MSG, :], raw[L][:, t % RAW, :], 0.0, None,
                                            ALU.max).then_inc(relued_dve[L], 1)
                    dve.wait_ge(relued_dve[L], it * (STEP // 3) + t // 3 + 1)
                else:
                    dve.wait_ge(relued_act[L], it * (STEP - STEP // 3) + t - t // 3)
                nc.vector.scalar_tensor_tensor(msg_lo[L][:, t % MSG, :], raw[L][:, t % RAW, :], 0.0,
                                               msg_hi[L][:, t % MSG, :].bitcast(F32), ALU.max,
                                               ALU.subtract).then_inc(low[L], 1)

            def edge_step(L, it, first):
                for j in range(STEP):
                    c = j // CHUNK
                    if j % CHUNK == 0:
                        low_features(L, it, c + 1)
                    if not first or j >= RELU_LAG:
                        message_parts(L, it, j - RELU_LAG)
                    if j % CHUNK == 2:
                        one_hots(L, it, c)

            def edges(L):
                low_features(L, 0, 0)
                if L == 0:
                    dve.wait_ge(w1_in, 16)
                    for k in range(KD):
                        i = split(W1_hi[:, k, :], W1_lo[:, k, :], W1_raw[:, k, :])
                    i.then_inc(w1_split, 1)
                edge_step(L, 0, True)
                if L == 1:
                    dve.wait_ge(v2_in, 16)
                    i = split(V2_hi[:, :, :], V2_lo[:, :, :], V2_raw[:, :, :])
                    i.then_inc(v2_split, 1)
                    dve.wait_ge(vb2_in, 16)
                    split(v_b2_hi[:, :], v_b2_lo[:, :], v_b2_raw[:, :]).then_inc(vb2_split, 1)
                with dve.Fori(1, STEPS) as it:
                    edge_step(L, it, False)
                for t in range(STEP - RELU_LAG, STEP):
                    message_parts(L, STEPS - 1, t)
                leftover(L)

            def leftover(L):
                dve.wait_ge(flag_ready, 1)
                left = dve.value_load(left_value, min_val=0, max_val=1)
                with dve.If(left > 0):
                    dve.wait_ge(accumulated[L], 16 * GROUPS)
                    nc.vector.nop().then_inc(lf_free[L], 1)
                    with dve.Fori(0, TILES) as t:
                        dve.wait_ge(lf_gathered[L], t * 16 + 16)
                        dve.wait_ge(lf_mm[L], t + 1)
                        nc.vector.tensor_copy(lf_dst[:, :], dst_left[:, bass.ds(t, 1)]).then_inc(lf_msg_steps[L], 1)
                        nc.vector.tensor_tensor(lf_msg[L][:, :], lf_bank[:, :], raw[L][:, 0, :],
                                                ALU.add).then_inc(lf_msg_steps[L], 1)
                        dve.wait_ge(lf_msg_steps[L], t * 3 + 2)
                        nc.vector.tensor_scalar(lf_msg[L][:, :], lf_msg[L][:, :], 0.0, None,
                                                ALU.max).then_inc(lf_msg_steps[L], 1)
                        dve.wait_ge(lf_msg_steps[L], t * 3 + 3)
                        for b in range(BLOCKS):
                            nc.vector.tensor_scalar(lf_hot[L][:, :], iota_f[:, :], float(b * P), lf_dst[:, 0:1], ALU.add,
                                                    ALU.is_equal).then_inc(lf_hot_ready[L], 1)
                            dve.wait_ge(lf_summed[L], t * BLOCKS + b + 1)
                            if b:
                                dve.wait_ge(lf_added[L], t * (16 * BLOCKS) + 16 * b)
                            if L == 0:
                                nc.vector.tensor_copy(sums[0][:, 0, D:D + 2], misc[:, 0:2])
                            nc.vector.tensor_copy(sums[L][:, 0, 0:D], sum_bank[0][:, :]).then_inc(lf_copied[L], 1)
                        dve.wait_ge(lf_added[L], t * (16 * BLOCKS) + 16 * BLOCKS)
                        nc.vector.nop().then_inc(lf_free[L], 1)

            def low_of_turned(L, hi, lo):
                for b in range(BLOCKS):
                    r = rows_in(b)
                    dve.wait_ge(turned_high[L], b + 1)
                    low_part(lo[:, :, b * P:b * P + r], feature_major(bank[b % 2])[:, :, 0:r],
                             hi[:, :, b * P:b * P + r]).then_inc(turned_low[L], 1)

            def variance(slot, parts, value):
                n = len(value)
                for q, v in enumerate(value):
                    i = nc.vector.bn_stats(stats[0:parts, slot * 18 + q * 6:slot * 18 + q * 6 + 6], v)
                link(i)
                link(nc.vector.bn_aggr(moments[0:parts, slot * 4:slot * 4 + 2], stats[0:parts, slot * 18:slot * 18 + 6 * n]))
                at4 = slot * 4 + 1
                nc.vector.tensor_scalar(moments[0:parts, at4:at4 + 1], moments[0:parts, at4:at4 + 1], EPS, None,
                                        ALU.add).then_inc(var_ready, 1)

            edges(0)
            low_of_turned(0, h_hi, h_lo)

            rstds = [0]

            def rstd_now():
                rstds[0] += 1
                dve.wait_ge(rstd_ready, rstds[0])

            def split_hidden(c):
                dve.wait_ge(silu_done, c + 1)
                split(s_hi[:, c, :], s_lo[:, c, :], pre[:, c % 2, :]).then_inc(s_split, 1)

            for c in range(KH + KD):
                dve.wait_ge(mlp_out, 3 * c + 3)
                variance(c % 2, P, [pre[:, c % 2, a:a + w] for a, w in NODE_CHUNKS])
                rstd_now()
                at4 = 4 * (c % 2)
                g, beta = (vec("g1", c), vec("beta1", c)) if c < KH else (vec("g2", c - KH), vec("beta2", c - KH))
                link(nc.vector.tensor_tensor(moments[:, at4 + 2:at4 + 3], moments[:, at4 + 2:at4 + 3], g, ALU.mult))
                link(nc.vector.tensor_tensor(moments[:, at4 + 3:at4 + 4], moments[:, at4:at4 + 1], moments[:, at4 + 2:at4 + 3],
                                             ALU.mult))
                nc.vector.tensor_tensor(moments[:, at4 + 3:at4 + 4], beta, moments[:, at4 + 3:at4 + 4],
                                        ALU.subtract).then_inc(bn_ready, 1)
                if c < KH:
                    if c == 0:
                        dve.wait_ge(w2_in, 16)
                    i = split(W2_hi[:, c, :], W2_lo[:, c, :], W2_raw[:, c, :])
                    if c == KH - 1:
                        i.then_inc(w2_split, 1)
                    split_hidden(c)
                if c == KH:
                    dve.wait_ge(v1h_in, 16)
                    split(V1h_hi[:, :, :], V1h_lo[:, :, :], V1h_raw[:, :, :]).then_inc(v1h_split, 1)

            def normalize(to, parts, slot):
                rstd_now()
                return nc.vector.tensor_scalar(to, lnx[0:parts, slot, :], moments[0:parts, slot * 4:slot * 4 + 1],
                                               moments[0:parts, slot * 4 + 2:slot * 4 + 3], ALU.subtract, ALU.mult)

            dve.wait_ge(rows_in_done, 16)
            dve.wait_ge(vb1_in, 16)
            for t in range(BLOCKS + 3):
                if t < BLOCKS:
                    r = rows_in(t)
                    dve.wait_ge(back_turned, t + 1)
                    if t >= 2:
                        dve.wait_ge(x1_ready, t - 1)
                    i = nc.vector.tensor_tensor(lnx[0:r, t % 2, :], bank[t % 2][0:r, :], rows[0:r, t, :], ALU.add)
                    i.then_inc(back_added, 1)
                    dve.wait_ge(back_added, t + 1)
                    variance(t % 2, r, [lnx[0:r, t % 2, :]])
                b = t - 1
                if 0 <= b < BLOCKS:
                    r = rows_in(b)
                    normalize(rows[0:r, b, :], r, b % 2).then_inc(x1_ready, 1)
                b = t - 2
                if 0 <= b < BLOCKS:
                    r = rows_in(b)
                    dve.wait_ge(x1_high, b + 1)
                    low_part(x1_lo[:, :, b * P:b * P + r], feature_major(bank[2 + b % 2])[:, :, 0:r],
                             x1_hi[:, :, b * P:b * P + r]).then_inc(x1_low, 1)
                b = t - 3
                if b >= 0:
                    r = rows_in(b)
                    dve.wait_ge(table_mm, b + 1)
                    if b >= 2:
                        dve.wait_ge(table_out[b % 2], 16 * (b // 2))
                    nc.vector.tensor_tensor(table_sb[0:r, b % 2, :], bank[4 + b % 2][0:r, :], vb1_bc[0:r, :],
                                            ALU.add).then_inc(table_ready, 1)
            dve.wait_ge(v1e_in, 16)
            split(V1e_hi[:, :], V1e_lo[:, :], V1e_sb[:, :]).then_inc(v1e_split, 1)
            edges(1)
            low_of_turned(1, r_hi, r_lo)

            def split_gates(m):
                dve.wait_ge(wg_in, 16 * (m + 1))
                flat = (t[:, :, :, :, :].rearrange("p a k g n -> p (a k g n)") for t in (Wg_hi[m % 2], Wg_lo[m % 2]))
                split(*flat, Wg_raw[:, :]).then_inc(wg_split, 1)

            n = 0
            for m in range(KD):
                for a, w in NODE_CHUNKS:
                    dve.wait_ge(m_high, n + 1)
                    low_part(m_lo[:, m, a:a + w], bank[4 + n % 4][:, 0:w], m_hi[:, m, a:a + w]).then_inc(m_low, 1)
                    n += 1
                    if n == 6:
                        split_gates(0)
            at_ih, at_hh = COLS["b_ih"][0], COLS["b_hh"][0]
            nc.vector.tensor_tensor(gate_bias[:, :], col[:, at_ih:at_ih + 2 * KD], col[:, at_hh:at_hh + 2 * KD],
                                    ALU.add).then_inc(gate_bias_ready, 1)
            at_var = COLS["run_var"][0]
            nc.vector.tensor_scalar(bn_scale[:, :], col[:, at_var:at_var + KD], EPS, None, ALU.add).then_inc(var_ready, 1)
            rstd_now()
            a = {name: COLS[name][0] for name in ("gamma", "beta", "run_mean")}
            link(nc.vector.tensor_tensor(bn_scale[:, :], bn_scale[:, :], col[:, a["gamma"]:a["gamma"] + KD], ALU.mult))
            link(nc.vector.tensor_tensor(bn_bias[:, :], bn_scale[:, :], col[:, a["run_mean"]:a["run_mean"] + KD], ALU.mult))
            link(nc.vector.tensor_tensor(bn_bias[:, :], col[:, a["beta"]:a["beta"] + KD], bn_bias[:, :], ALU.subtract))
            n = 0
            for m in range(KD):
                for q, (a, w) in enumerate(NODE_CHUNKS):
                    four = bank[4 * (n % 2):4 * (n % 2) + 4]
                    gr, gz, gn, gd = g_r[:, n % 2, 0:w], g_z[:, n % 2, 0:w], g_n[:, 0:w], g_d[:, 0:w]
                    dve.wait_ge(r_done, n + 1)
                    dve.wait_ge(gate_mm, 4 * n + 3)
                    link(nc.vector.scalar_tensor_tensor(gr, four[1][:, 0:w], vec("b_hh", 2 * KD + m), gr, ALU.add, ALU.mult))
                    nc.vector.tensor_tensor(gr, gr, four[2][:, 0:w], ALU.add).then_inc(n_in, 1)
                    dve.wait_ge(n_done, n + 1)
                    link(nc.vector.tensor_tensor(gd, x1_hi[:, m, a:a + w].bitcast(F32), gn, ALU.subtract))
                    link(nc.vector.tensor_tensor(gd, gd, x1_lo[:, m, a:a + w].bitcast(F32), ALU.add))
                    dve.wait_ge(z_done, n + 1)
                    link(nc.vector.tensor_tensor(gd, gd, gz, ALU.mult))
                    link(nc.vector.tensor_tensor(gd, gd, gn, ALU.add))
                    nc.vector.tensor_scalar(bn_t[:, m, a:a + w], gd, bn_scale[:, m:m + 1], bn_bias[:, m:m + 1],
                                            ALU.mult, ALU.add).then_inc(gru_done, 1)
                    n += 1
                    if q == 0 and m + 1 < KD:
                        split_gates(m + 1)
            for t in range(BLOCKS + 1):
                if t < BLOCKS:
                    r = rows_in(t)
                    dve.wait_ge(fin_turned, t + 1)
                    if t >= 2:
                        dve.wait_ge(fin_ready, t - 1)
                    nc.vector.scalar_tensor_tensor(lnx[0:r, t % 2, :], rows[0:r, t, :], 2.0, bank[t % 2][0:r, :], ALU.mult,
                                                   ALU.add).then_inc(fin_added, 1)
                    dve.wait_ge(fin_added, t + 1)
                    variance(t % 2, r, [lnx[0:r, t % 2, :]])
                b = t - 1
                if b >= 0:
                    r = rows_in(b)
                    if b >= 2:
                        dve.wait_ge(fin_out[b % 2], 16 * (b // 2))
                    normalize(fin[0:r, b % 2, :], r, b % 2).then_inc(fin_ready, 1)


def kernel(**inputs):
    import numpy as np
    import concourse.bacc as bacc
    from concourse.bass_utils import run_bass_kernel_spmd

    a = {k: np.asarray(v) for k, v in inputs.items()}

    def by_tile(index, fill):
        full = np.full(TILES * P, fill, index.dtype)
        full[:E] = index
        return full.reshape(TILES, P).T

    def turned(attr):
        full = np.zeros((attr.shape[1], (TILES + CHUNK) * P), attr.dtype)
        full[:, :E] = attr.T
        return full

    x = np.zeros((BLOCKS * P, D), a["x"].dtype)
    x[:N] = a["x"]
    vectors = {"b1": a["L0_gnn_b1"], "g1": a["L0_gnn_g1"], "beta1": a["L0_gnn_beta1"], "b2": a["L0_gnn_b2"],
               "g2": a["L0_gnn_g2"], "beta2": a["L0_gnn_beta2"], "b_ih": a["L1_gnn_b_ih"], "b_hh": a["L1_gnn_b_hh"],
               "gamma": a["L1_gnn_gamma"], "beta": a["L1_gnn_beta"], "run_mean": a["L1_gnn_run_mean"],
               "run_var": a["L1_gnn_run_var"], "eps": np.full(P, a["L0_gnn_eps"])}
    gates = np.stack([a["L1_gnn_W_ih"], a["L1_gnn_W_hh"]]).reshape(2, 3, KD, P, KD, P)
    arrays = {
        "x": x,
        "src": by_tile(a["src"], 0),
        "dst": by_tile(a["dst"], -1),
        "attr0": turned(a["edge_attr_64"]),
        "attr1": turned(a["edge_attr_128"]),
        "W_e": a["L0_gnn_W_e"],
        "b_e": a["L0_gnn_b_e"].reshape(1, D),
        "W1": a["L0_gnn_W1"],
        "W2": a["L0_gnn_W2"],
        "V1h": a["L1_gnn_W1"][:, :D].T,
        "V1e": a["L1_gnn_W1"][:, D:].T,
        "v_b1": a["L1_gnn_b1"].reshape(1, D),
        "V2": a["L1_gnn_W2"].T,
        "v_b2": a["L1_gnn_b2"].reshape(1, D),
        "Wg": gates.transpose(2, 5, 0, 4, 1, 3).reshape(KD, P, 2 * KD * 3 * P),
        "cols": np.concatenate([vectors[n].reshape(k, P).T for n, (_, k) in COLS.items()], axis=1),
    }
    arrays = {f"in_{k}": np.ascontiguousarray(v) for k, v in arrays.items()}
    nc = bacc.Bacc("TRN2", target_bir_lowering=False, num_devices=1)
    args = [nc.dram_tensor(k, v.shape, mybir.dt.from_np(v.dtype), kind="ExternalInput").ap() for k, v in arrays.items()]
    args.append(nc.dram_tensor("out", (N, D), F32, kind="ExternalOutput").ap())
    gnn_program(nc, *args)
    r = run_bass_kernel_spmd(nc, [arrays], core_ids=[0])
    return r.results[0]["out"]
```

```python
from contextlib import ExitStack

import concourse.bass as bass
from concourse import mybir

F32 = mybir.dt.float32
F32R = mybir.dt.float32r
I32 = mybir.dt.int32
ALU = mybir.AluOpType
ACT = mybir.ActivationFunctionType

P = 128
N, E, D = 1250, 21250, 512
ED0, ED1 = 64, 128
H0 = 2 * D
EPS = 1e-5
KD = D // P
KH = H0 // P

GROUP = 12
TILES = -(-E // (P * 2 * GROUP)) * 2 * GROUP
GROUPS = TILES // GROUP
STEP = 2 * GROUP
STEPS = TILES // STEP
CHUNK = 4
ROWS = (-(-N // P) + 1) * P
BLOCKS = -(-N // P)

RAW, EDGE_BANKS, MSG, HOT, RING = 8, 4, 4, 3, 3
RELU_LAG, SUM_LAG = 6, 8

XB = 2
XQ = BLOCKS // XB
SB = 2
NODE_CHUNKS = [(0, 4 * P), (4 * P, 3 * P), (7 * P, N - 7 * P)]
COLS = {}
for _name, _k in (("b1", KH), ("g1", KH), ("beta1", KH), ("b2", KD), ("g2", KD), ("beta2", KD),
                  ("b_ih", 3 * KD), ("b_hh", 3 * KD), ("gamma", KD), ("beta", KD),
                  ("run_mean", KD), ("run_var", KD), ("eps", 1)):
    COLS[_name] = (sum(w for _, w in COLS.values()), _k)
NCOLS = sum(w for _, w in COLS.values())

KB = 1024


def rows_in(block):
    return min(P, N - block * P)


def blocks_of(q):
    at, w = NODE_CHUNKS[q]
    return range(at // P, -(-(at + w) // P))


def gnn_program(nc, x, src, dst, attr0, attr1, W_e, b_e, W1, W2, V1h, V1e, v_b1, V2, v_b2, Wg, cols, out):
    with ExitStack() as ctx:
        base = -(-nc.sbuf_base // 64) * 64
        A0 = base + 10 * KB + KB // 2
        B0 = A0 + 64 * KB

        def at(name, shape, dt, offset):
            return nc.alloc_sbuf_tensor_at(name, shape, dt, offset=offset)

        def sem(name):
            return ctx.enter_context(nc.semaphore(name))

        def psum(name, shape):
            return ctx.enter_context(nc.psum_tensor(name, shape, F32))

        small = [base]

        def keep(name, width, dt=F32, parts=P):
            t = at(name, [parts, width], dt, small[0])
            small[0] += -(-width * 4 // 64) * 64
            assert small[0] <= A0, name
            return t

        src_sb = keep("src_sb", TILES + GROUP, I32)
        dst_i = keep("dst_i", TILES, I32)
        dst_f = keep("dst_f", TILES)
        in_window = keep("in_window", TILES)
        dst_left = keep("dst_left", TILES)
        iota_f = keep("iota_f", P)
        ident = keep("ident", P)
        ones = keep("ones", P)
        ones_r = keep("ones_r", 2, F32R)
        col = keep("col", NCOLS)
        stats = keep("stats", 2 * 18)
        moments = keep("moments", 2 * 4)
        minus_half = keep("minus_half", KD)
        one_eps = keep("one_eps", 1)
        gate_bias = keep("gate_bias", 2 * KD)
        bn_scale = keep("bn_scale", KD)
        bn_bias = keep("bn_bias", KD)
        base_sb = keep("base_sb", GROUPS)
        left_n = keep("left_n", 4)
        any_left = keep("any_left", 1, I32)
        idx_now = keep("idx_now", STEP, I32)
        lf_idx = keep("lf_idx", 1, I32)
        lf_dst = keep("lf_dst", 1)
        degree = keep("degree", 2 * BLOCKS)
        v_b2_hi = keep("v_b2_hi", D, F32R, 1)
        v_b2_lo = keep("v_b2_lo", D, F32R, 1)

        def vec(name, k=0):
            return col[:, COLS[name][0] + k:COLS[name][0] + k + 1]

        W1_hi = at("W1_hi", [P, KD, H0], F32R, A0)
        W1_lo = at("W1_lo", [P, KD, H0], F32R, A0 + 16 * KB)
        W2_hi = at("W2_hi", [P, KH, D], F32R, A0 + 32 * KB)
        W2_lo = at("W2_lo", [P, KH, D], F32R, A0 + 48 * KB)
        W1_raw = at("W1_raw", [P, KD, H0], F32, A0 + 16 * KB)
        W2_raw = at("W2_raw", [P, KH, D], F32, A0 + 48 * KB)
        x_in = at("x_in", [P, BLOCKS, D], F32, B0 + 84 * KB)
        xb = at("xb", [P, BLOCKS, D], F32, B0 + 104 * KB)
        zero_rows = at("zero_rows", [P, D + 2], F32, B0 + 131 * KB)
        be_bc = at("be_bc", [P, D], F32, B0 + 127 * KB)
        iota_i = at("iota_i", [P, P], I32, B0 + 130 * KB)

        raw = [at("raw0", [P, RAW, D], F32, B0), at("raw1", [P, RAW, D], F32, B0 + 80 * KB)]
        attr = [at("attr0_sb", [P, RING, CHUNK * P], F32, B0 + 42 * KB),
                at("attr1_sb", [P, RING, CHUNK * P], F32, A0 + 20 * KB)]
        attr_hl = at("attr_hl", [P, RING, CHUNK * P], F32R, B0 + 48 * KB)
        attr_hi = at("attr_hi", [P, RING, CHUNK * P], F32R, B0)
        attr_lo = at("attr_lo", [P, RING, CHUNK * P], F32R, B0 + 6 * KB)
        E0, E1 = B0 + 20 * KB, A0 + 40 * KB
        msg_hi = [at("msg_hi0", [P, MSG, D], F32R, E0), at("msg_hi1", [P, MSG, D], F32R, E1)]
        msg_lo = [at("msg_lo0", [P, MSG, D], F32R, E0 + 8 * KB), at("msg_lo1", [P, MSG, D], F32R, E1 + 8 * KB)]
        hot = [at("hot0", [P, HOT, CHUNK, P], F32R, B0 + 36 * KB), at("hot1", [P, HOT, CHUNK, P], F32R, A0 + 34 * KB)]
        sums = [at("sums0", [P, 2, D + 4], F32, B0 + 54 * KB), at("sums1", [P, 2, D + 4], F32, E1 + 16 * KB)]
        lf_msg = [at("lf_msg0", [P, D], F32, B0 + 60 * KB), at("lf_msg1", [P, D], F32, A0 + 62 * KB)]
        lf_hot = [at("lf_hot0", [P, P], F32, B0 + 18 * KB), at("lf_hot1", [P, P], F32, A0 + 61 * KB)]
        We_raw = at("We_raw", [P, D], F32, B0 + 62 * KB)
        We_hi = at("We_hi", [P, D], F32R, B0 + 64 * KB)
        We_lo = at("We_lo", [P, D], F32R, B0 + 66 * KB)
        V1e_sb = at("V1e_sb", [P, D], F32, A0 + 28 * KB)
        V1e_hi = at("V1e_hi", [P, D], F32R, A0 + 30 * KB)
        V1e_lo = at("V1e_lo", [P, D], F32R, A0 + 32 * KB)

        h_hi = at("h_hi", [P, KD, N], F32R, B0)
        h_lo = at("h_lo", [P, KD, N], F32R, B0 + 20 * KB)
        stage0 = at("stage0", [P, BLOCKS, D], F32, B0 + 40 * KB)
        s_hi = at("s_hi", [P, KH, N], F32R, B0 + 40 * KB)
        s_lo = at("s_lo", [P, KH, N], F32R, B0 + 80 * KB)
        pre = at("pre", [P, 2, N], F32, B0 + 120 * KB)
        y_t = at("y_t", [P, KD, N], F32, B0)

        rows = at("rows", [P, BLOCKS, D], F32, A0)
        V1h_raw = at("V1h_raw", [P, KD, D], F32, A0 + 20 * KB)
        V1h_hi = at("V1h_hi", [P, KD, D], F32R, B0 + 20 * KB)
        V1h_lo = at("V1h_lo", [P, KD, D], F32R, B0 + 28 * KB)
        x1_hi = at("x1_hi", [P, KD, N], F32R, B0 + 40 * KB)
        x1_lo = at("x1_lo", [P, KD, N], F32R, B0 + 60 * KB)
        table_sb = at("table_sb", [P, 2, D], F32, B0 + 100 * KB)
        vb1_bc = at("vb1_bc", [P, D], F32, B0 + 36 * KB)
        lnx = at("lnx", [P, 2, D], F32, B0 + 96 * KB)

        stage1 = at("stage1", [P, BLOCKS, D], F32, A0 + 20 * KB)
        V2_raw = at("V2_raw", [P, KD, D], F32, B0 + 108 * KB)
        V2_hi = at("V2_hi", [P, KD, D], F32R, B0 + 100 * KB)
        V2_lo = at("V2_lo", [P, KD, D], F32R, B0 + 108 * KB)
        r_hi = at("r_hi", [P, KD, N], F32R, B0 + 80 * KB)
        r_lo = at("r_lo", [P, KD, N], F32R, B0 + 20 * KB)
        deg_r = at("deg_r", [2, N], F32R, B0 + 128 * KB)
        v_b2_raw = at("v_b2_raw", [1, D], F32, B0 + 38 * KB)
        m_hi = at("m_hi", [P, KD, N], F32R, A0 + 32 * KB)
        m_lo = at("m_lo", [P, KD, N], F32R, A0 + 52 * KB)
        Wg_raw = at("Wg_raw", [P, 2 * KD * 3 * P], F32, A0 + 20 * KB)
        Wg_hi = [at("Wg_hi0", [P, 2, KD, 3, P], F32R, B0 + 8 * KB), at("Wg_hi1", [P, 2, KD, 3, P], F32R, B0 + 20 * KB)]
        Wg_lo = [at("Wg_lo0", [P, 2, KD, 3, P], F32R, B0 + 116 * KB), at("Wg_lo1", [P, 2, KD, 3, P], F32R, B0 + 80 * KB)]
        Wh_raw = at("Wh_raw", [P, KD * 3 * P], F32, B0 + 122 * KB)
        g_r = at("g_r", [P, 2, 512], F32, B0 + 32 * KB)
        g_z = at("g_z", [P, 2, 512], F32, B0 + 36 * KB)
        g_n = at("g_n", [P, 512], F32, B0 + 112 * KB)
        g_d = at("g_d", [P, 512], F32, B0 + 114 * KB)
        bn_t = at("bn_t", [P, KD, N], F32, B0 + 92 * KB)
        fin = at("fin", [P, 2, D], F32, A0 + 20 * KB)
        last = at("last", [P, 2, D], F32, A0 + 24 * KB)
        assert B0 + 128 * KB + 4 * N <= nc.sbuf_usable_end

        xb_dram = nc.dram_tensor("xb_dram", [BLOCKS * P, D], F32).ap()
        table_dram = nc.dram_tensor("table_dram", [N, D], F32).ap()
        sum_dram = [nc.dram_tensor("sum0_dram", [ROWS, D + 2], F32).ap(),
                    nc.dram_tensor("sum1_dram", [ROWS, D], F32).ap()]
        tables = [xb_dram, table_dram]

        bank = [psum(f"bank{b}", [P, 512]) for b in range(8)]
        e_bank = bank[0:EDGE_BANKS]
        sum_bank = bank[4:6]
        degree_bank = bank[6:8]
        turn_bank = [[bank[b] for b in (0, 1, 5, 6)], [bank[b] for b in (2, 7)]]
        last_bank = [bank[b] for b in (5, 4, 6, 7, 0, 1, 2, 3, 0, 1)]
        misc = bank[6]
        lf_bank = bank[7]

        idx_in, cols_in, be_in, we_in, w1_in, w2_in = map(sem, ("idx_in", "cols_in", "be_in", "we_in", "w1_in", "w2_in"))
        x_in_done = [sem(f"x_in_done{q}") for q in range(XQ)]
        pool_consts, dst_ready, base_ready = map(sem, ("pool_consts", "dst_ready", "base_ready"))
        left_ready, left_counted, flag_ready = map(sem, ("left_ready", "left_counted", "flag_ready"))
        eps_ready, xb_ready, start_ready, zero_ready, xb_out = map(
            sem, ("eps_ready", "xb_ready", "start_ready", "zero_ready", "xb_out"))
        start_out = [sem("start_out0"), sem("start_out1")]
        we_split, w1_split, w2_split = map(sem, ("we_split", "w1_split", "w2_split"))
        stage_in = [[sem(f"stage_in{L}_{q}") for q in range(3)] for L in range(2)]
        turned, turned_high, turned_low = ([sem(f"{n}{L}") for L in range(2)] for n in ("turned", "turned_high", "turned_low"))
        mlp_mm, mlp_out, silu_done, s_split = map(sem, ("mlp_mm", "mlp_out", "silu_done", "s_split"))
        var_ready, rstd_ready, bn_ready = map(sem, ("var_ready", "rstd_ready", "bn_ready"))
        rows_in_done, v1h_in, v1e_in, vb1_in, vb2_in, v2_in, wg_in = map(
            sem, ("rows_in_done", "v1h_in", "v1e_in", "vb1_in", "vb2_in", "v2_in", "wg_in"))
        v1h_split, v1e_split, vb2_split, v2_split, wg_split = map(
            sem, ("v1h_split", "v1e_split", "vb2_split", "v2_split", "wg_split"))
        wh_in, wh_split = map(sem, ("wh_in", "wh_split"))
        degree_in, degree_mm, degree_turned = map(sem, ("degree_in", "degree_mm", "degree_turned"))
        back_turned, back_added, x1_ready, x1_turned, x1_high, x1_low = map(
            sem, ("back_turned", "back_added", "x1_ready", "x1_turned", "x1_high", "x1_low"))
        table_mm, table_ready = map(sem, ("table_mm", "table_ready"))
        table_out = [sem(f"table_out{i}") for i in range(2)]
        m_mm, m_high, m_low = map(sem, ("m_mm", "m_high", "m_low"))
        gate_mm, r_done, z_done, n_in, n_done, gru_done = map(
            sem, ("gate_mm", "r_done", "z_done", "n_in", "n_done", "gru_done"))
        fin_turned, fin_added, fin_bias, fin_ready = map(sem, ("fin_turned", "fin_added", "fin_bias", "fin_ready"))
        fin_out = [sem(f"fin_out{i}") for i in range(2)]
        gate_bias_ready = sem("gate_bias_ready")
        dve_step = sem("dve_step")
        (idx_copied, edge_mm, edge_out, relued_act, relued_dve, low, hot_ready, summed, sum_out, accumulated,
         attr_high, attr_split) = ([sem(f"{n}{L}") for L in range(2)] for n in (
             "idx_copied", "edge_mm", "edge_out", "relued_act", "relued_dve", "low", "hot_ready", "summed",
             "sum_out", "accumulated", "attr_high", "attr_split"))
        gathered = [[sem(f"gathered{L}_{i}") for i in range(RAW)] for L in range(2)]
        attr_in = [[sem(f"attr_in{L}_{i}") for i in range(RING)] for L in range(2)]
        lf_free, lf_idx_ready, lf_gathered, lf_attr_in, lf_mm, lf_msg_steps, lf_hot_ready, lf_summed, lf_copied, lf_added = (
            [sem(f"{n}{L}") for L in range(2)] for n in (
                "lf_free", "lf_idx_ready", "lf_gathered", "lf_attr_in", "lf_mm", "lf_msg_steps", "lf_hot_ready",
                "lf_summed", "lf_copied", "lf_added"))

        attr_dram, attr_parts = [attr0, attr1], [ED0, ED1]
        width = [D + 2, D]
        CPS = STEP // CHUNK
        left_value = any_left[0:1, 0:1]
        STARTS = 2 + CPS + 1 - RING + 1
        LF_ALL = 16 * TILES * BLOCKS

        def wait(engine, semaphore, value):
            if not isinstance(value, int) or value > 0:
                engine.wait_ge(semaphore, value)

        def relu_on_dve(t):
            return t % 3 == 0

        def wait_gathered(engine, L, it, t):
            engine.wait_ge(gathered[L][t % RAW], it * (STEP // RAW * 16) + (t // RAW + 1) * 16)

        def feature_major(b):
            return b[:, :].rearrange("p (k n) -> p k n", k=KD)

        block = ctx.enter_context(nc.Block())

        @block.sync
        def _(sp):
            def load_chunk(L, it, c):
                rows_of = attr_parts[L]
                wait(sp, attr_split[L], it * CPS + c - RING + 1)
                for h in range(P // rows_of):
                    sp.dma_start(attr[L][h * rows_of:(h + 1) * rows_of, c % RING, :],
                                 attr_dram[L][:, bass.ds(it * (STEP * P) + c * CHUNK * P, CHUNK * P)]
                                 ).then_inc(attr_in[L][c % RING], 16)

            def load_leftover_attr(L):
                sp.wait_ge(flag_ready, 1)
                left = sp.value_load(left_value, min_val=0, max_val=1)
                with sp.If(left > 0):
                    with sp.Fori(0, TILES) as t:
                        sp.wait_ge(lf_free[L], t + 1)
                        sp.dma_start(attr[L][0:attr_parts[L], 0, 0:P],
                                     attr_dram[L][:, bass.ds(t * P, P)]).then_inc(lf_attr_in[L], 16)
                    sp.wait_ge(lf_added[L], LF_ALL)

            def load_sums(L, stage):
                sp.wait_ge(accumulated[L], 16 * GROUPS)
                for q in range(3):
                    b = blocks_of(q)
                    sp.dma_start(stage[:, b.start:b.stop, :],
                                 sum_dram[L][b.start * P:b.stop * P, 0:D].rearrange("(t p) d -> p t d", p=P)
                                 ).then_inc(stage_in[L][q], 16)

            by_block = x.rearrange("(t p) d -> p t d", p=P)
            xb_rows = xb_dram.rearrange("(t p) d -> p t d", p=P)
            sp.dma_start(be_bc[:, :], b_e.partition_broadcast(P)).then_inc(be_in, 16)
            for q in range(XQ):
                sp.dma_start(x_in[:, q * XB:(q + 1) * XB, :], by_block[:, q * XB:(q + 1) * XB, :]).then_inc(x_in_done[q], 16)
                if q == 1:
                    sp.dma_start(dst_i[:, :], dst).then_inc(idx_in, 16)
                    sp.dma_start(src_sb[:, :], src).then_inc(idx_in, 16)
                    sp.dma_start(col[:, :], cols).then_inc(cols_in, 16)
                    for h in range(2):
                        sp.dma_start(We_raw[h * ED0:(h + 1) * ED0, :], W_e).then_inc(we_in, 16)
            load_chunk(0, 0, 0)
            for q in range(XQ):
                sp.wait_ge(xb_ready, q + 1)
                sp.dma_start(xb_rows[:, q * XB:(q + 1) * XB, :], xb[:, q * XB:(q + 1) * XB, :]).then_inc(xb_out, 16)
            load_chunk(0, 0, 1)
            load_chunk(0, 0, 2)
            sp.wait_ge(zero_ready, 1)
            sp.dma_start(sum_dram[0][BLOCKS * P:ROWS, :], zero_rows[:, :]).then_inc(start_out[0], 16)
            sp.dma_start(sum_dram[0][0:BLOCKS * P, D:D + 2].rearrange("(t p) d -> p t d", p=P),
                         zero_rows[:, 0:2 * BLOCKS].rearrange("p (t d) -> p t d", d=2)).then_inc(start_out[0], 16)
            sp.wait_ge(start_ready, 1)
            start_rows = sum_dram[0][0:BLOCKS * P, 0:D].rearrange("(t p) d -> p t d", p=P)
            for c in range(RING, CPS + 1):
                load_chunk(0, 0, c)
                q = c - RING
                sp.dma_start(start_rows[:, q * SB:(q + 1) * SB, :], x_in[:, q * SB:(q + 1) * SB, :]).then_inc(start_out[0], 16)
            q = CPS + 1 - RING
            sp.dma_start(start_rows[:, q * SB:, :], x_in[:, q * SB:, :]).then_inc(start_out[0], 16)
            for h, (a, b) in enumerate(((1, 3), (3, 5), (5, STEPS))):
                with sp.Fori(a, b) as it:
                    for c in range(CPS):
                        load_chunk(0, it, c + 1)
                if h < 2:
                    sp.dma_start(W1_raw[:, 2 * h:2 * h + 2, :],
                                 W1[2 * h * P:(2 * h + 2) * P, :].rearrange("(k p) n -> p k n", p=P)).then_inc(w1_in, 16)
            load_leftover_attr(0)
            load_sums(0, stage0)
            sp.dma_start(degree[:, :].rearrange("p (t d) -> p t d", d=2),
                         sum_dram[0][0:BLOCKS * P, D:D + 2].rearrange("(t p) d -> p t d", p=P)).then_inc(degree_in, 16)
            sp.dma_start(W2_raw[:, :, :], W2.rearrange("(k p) n -> p k n", p=P)).then_inc(w2_in, 16)
            for b in range(ROWS // P):
                sp.dma_start(sum_dram[1][b * P:(b + 1) * P, :], zero_rows[:, 0:D]).then_inc(start_out[1], 16)
            sp.wait_ge(mlp_mm, KH * 3)
            sp.dma_start(V1h_raw[:, :, :], V1h.rearrange("(k p) n -> p k n", p=P)).then_inc(v1h_in, 16)
            sp.dma_start(rows[:, :, :], by_block).then_inc(rows_in_done, 16)
            sp.dma_start(V1e_sb[:, :], V1e).then_inc(v1e_in, 16)
            sp.dma_start(vb1_bc[:, :], v_b1.partition_broadcast(P)).then_inc(vb1_in, 16)
            sp.dma_start(v_b2_raw[:, :], v_b2).then_inc(vb2_in, 16)
            for b in range(BLOCKS):
                sp.wait_ge(table_ready, b + 1)
                sp.dma_start(table_dram[b * P:b * P + rows_in(b), :], table_sb[0:rows_in(b), b % 2, :]
                             ).then_inc(table_out[b % 2], 16)
                if b == BLOCKS // 2:
                    sp.wait_ge(back_turned, BLOCKS)
                    sp.wait_ge(v1h_split, 1)
                    for c in range(RING):
                        load_chunk(1, 0, c)
                    sp.dma_start(Wh_raw[:, :], Wg[0][:, KD * 3 * P:2 * KD * 3 * P]).then_inc(wh_in, 16)
            sp.dma_start(V2_raw[:, :, :], V2.rearrange("(k p) n -> p k n", p=P)).then_inc(v2_in, 16)
            for c in range(RING, CPS + 1):
                load_chunk(1, 0, c)
            with sp.Fori(1, STEPS) as it:
                for c in range(CPS):
                    load_chunk(1, it, c + 1)
            load_leftover_attr(1)
            sp.wait_ge(v2_split, KD)
            load_sums(1, stage1)
            sp.wait_ge(turned[1], BLOCKS)
            for m in range(KD):
                if m:
                    sp.wait_ge(wg_split, m)
                part = slice(0, (1 if m == 0 else 2) * KD * 3 * P)
                sp.dma_start(Wg_raw[:, part], Wg[m][:, part]).then_inc(wg_in, 16)
            for b in range(BLOCKS):
                sp.wait_ge(fin_ready, b + 1)
                sp.dma_start(out[b * P:b * P + rows_in(b), :], fin[0:rows_in(b), b % 2, :]).then_inc(fin_out[b % 2], 16)
            for i in range(2):
                sp.wait_ge(fin_out[i], 16 * (BLOCKS // 2))

        @block.gpsimd
        def _(pool):
            def in_register(name, value):
                if isinstance(value, int):
                    return value
                pool.reg_mov(counts[name], pool.to_reg(value))
                return counts[name]

            counts = {name: pool.alloc_register(f"count_{name}") for name in ("one", "other")}

            def accumulate(L, g, slot, very_first):
                first_node = pool.value_load(dst_i[0:1, bass.ds((g - 1) * GROUP, 1)], min_val=0, max_val=ROWS - P)
                summed_there = in_register("one", g)
                landed = in_register("other", 16 * (g - 1))
                pool.wait_ge(start_out[L], 16 * (STARTS, ROWS // P)[L])
                pool.wait_ge(sum_out[L], summed_there)
                if not very_first:
                    pool.wait_ge(accumulated[L], landed)
                pool.dma_start(sum_dram[L][bass.ds(first_node, P), :], sums[L][:, slot, 0:width[L]],
                               accum_op=ALU.add).then_inc(accumulated[L], 16)

            def wait_table(L):
                if L == 0:
                    pool.wait_ge(xb_out, 16 * XQ)
                else:
                    for i in range(2):
                        pool.wait_ge(table_out[i], 16 * (BLOCKS // 2))

            def gather_step(L, it, first):
                for j in range(STEP):
                    i, half = it * STEP + j, j // GROUP
                    copied, out_there = in_register("one", it * 2 + half + 1), in_register("other", i + 1)
                    wait_table(L)
                    if j % GROUP == 0:
                        pool.wait_ge(idx_copied[L], copied)
                    pool.wait_ge(edge_out[L], out_there)
                    pool.indirect_dma_start(raw[L][:, j % RAW, :], None, tables[L],
                                            bass.IndirectOffsetOnAxis(ap=idx_now[:, j:j + 1], axis=0),
                                            compute_op=ALU.add).then_inc(gathered[L][j % RAW], 16)
                    if j % GROUP == GROUP - 2 and (not first or half):
                        accumulate(L, it * 2 + half, 1 - half, first)

            def gather_leftover(L):
                pool.wait_ge(flag_ready, 1)
                left = pool.value_load(left_value, min_val=0, max_val=1)
                with pool.If(left > 0):
                    with pool.Fori(0, TILES) as t:
                        pool.wait_ge(lf_free[L], t + 1)
                        nc.gpsimd.tensor_copy(lf_idx[:, :], src_sb[:, bass.ds(t, 1)]).then_inc(lf_idx_ready[L], 1)
                        copied = in_register("one", t + 1)
                        wait_table(L)
                        pool.wait_ge(lf_idx_ready[L], copied)
                        pool.indirect_dma_start(raw[L][:, 0, :], None, tables[L],
                                                bass.IndirectOffsetOnAxis(ap=lf_idx[:, :], axis=0)
                                                ).then_inc(lf_gathered[L], 16)
                        for b in range(BLOCKS):
                            copied = in_register("one", t * BLOCKS + b + 1)
                            pool.wait_ge(start_out[L], 16 * (STARTS, ROWS // P)[L])
                            pool.wait_ge(lf_copied[L], copied)
                            pool.dma_start(sum_dram[L][b * P:(b + 1) * P, :], sums[L][:, 0, 0:width[L]],
                                           accum_op=ALU.add).then_inc(lf_added[L], 16)
                            pool.wait_ge(lf_added[L], t * (16 * BLOCKS) + 16 * (b + 1))

            def rstd(n, slot):
                pool.wait_ge(var_ready, n)
                nc.gpsimd.tensor_tensor(moments[:, slot * 4 + 2:slot * 4 + 3], moments[:, slot * 4 + 1:slot * 4 + 2],
                                        minus_half[:, 0:1], ALU.pow).then_inc(rstd_ready, 1)

            nc.gpsimd.iota(iota_i[:, :], [[1, P]], base=0, channel_multiplier=0).then_inc(pool_consts, 1)
            nc.gpsimd.memset(minus_half[:, :], -0.5).then_inc(pool_consts, 1)
            nc.gpsimd.memset(ones[:, :], 1.0).then_inc(pool_consts, 1)
            nc.gpsimd.memset(ident[:, :], 0.0).then_inc(pool_consts, 1)
            pool.wait_ge(pool_consts, 4)
            nc.gpsimd.affine_select(out=ident[:, :], in_=ident[:, :], compare_op=ALU.not_equal, fill=1.0, base=0,
                                    pattern=[[-1, P]], channel_multiplier=1).then_inc(pool_consts, 1)
            pool.wait_ge(idx_in, 32)
            n = 0
            for L in range(2):
                wait_table(L)
                gather_step(L, 0, True)
                with pool.Fori(1, STEPS) as it:
                    gather_step(L, it, False)
                accumulate(L, GROUPS, 1, False)
                gather_leftover(L)
                if L == 0:
                    for c in range(KH + KD):
                        n += 1
                        rstd(n, c % 2)
                else:
                    n += 1
                    pool.wait_ge(var_ready, n)
                    nc.gpsimd.tensor_tensor(bn_scale[:, :], bn_scale[:, :], minus_half[:, :],
                                            ALU.pow).then_inc(rstd_ready, 1)
                for b in range(BLOCKS):
                    n += 1
                    rstd(n, b % 2)

        @block.tensor
        def _(pe):
            def product(acc, terms, start=True, stop=True):
                passes = [(a, b) for a_hi, a_lo, b_hi, b_lo in terms for a, b in ((a_hi, b_hi), (a_hi, b_lo), (a_lo, b_hi))]
                for i, (a, b) in enumerate(passes):
                    mm = nc.tensor.matmul(acc, a, b, start=start and i == 0,
                                          stop=stop and i == len(passes) - 1)
                return mm

            def edge_product(L, it, j):
                c, ks = j // CHUNK, slice(j % CHUNK * P, (j % CHUNK + 1) * P)
                if j % CHUNK == 0:
                    pe.wait_ge(attr_split[L], it * CPS + c + 1)
                wait(pe, edge_out[L], it * STEP + j - EDGE_BANKS + 1)
                acc = e_bank[j % EDGE_BANKS][:, :]
                if L == 0:
                    passes = [(attr_hl, We_hi), (attr_hl, We_lo)]
                else:
                    passes = [(attr_hi, V1e_hi), (attr_hi, V1e_lo), (attr_lo, V1e_hi)]
                for n, (features, W) in enumerate(passes):
                    mm = nc.tensor.matmul(acc, features[:, c % RING, ks], W[:, :], start=n == 0, stop=n == len(passes) - 1)
                mm.then_inc(edge_mm[L], 1)

            def sum_product(L, it, t):
                start, stop, half = t % GROUP == 0, t % GROUP == GROUP - 1, t // GROUP % 2
                pe.wait_ge(low[L], it * STEP + t + 1)
                pe.wait_ge(hot_ready[L], it * CPS + t // CHUNK + 1)
                if start:
                    wait(pe, sum_out[L], it * 2 + t // GROUP - 1)
                acc, h = sum_bank[half][:, :], hot[L][:, t // CHUNK % HOT, t % CHUNK, :]
                nc.tensor.matmul(acc, h, msg_hi[L][:, t % MSG, :], start=start, stop=False)
                mm = nc.tensor.matmul(acc, h, msg_lo[L][:, t % MSG, :], start=False, stop=stop)
                if L == 0:
                    mm = nc.tensor.matmul(degree_bank[half][:, 0:2], h, ones_r[:, :], start=start, stop=stop)
                mm.then_inc(summed[L], 1)

            def edges(L):
                for j in range(STEP):
                    edge_product(L, 0, j)
                    if j >= SUM_LAG:
                        sum_product(L, 0, j - SUM_LAG)
                with pe.Fori(1, STEPS) as it:
                    for j in range(STEP):
                        edge_product(L, it, j)
                        sum_product(L, it, j - SUM_LAG)
                for t in range(STEP - SUM_LAG, STEP):
                    sum_product(L, STEPS - 1, t)

            def leftover(L):
                pe.wait_ge(flag_ready, 1)
                left = pe.value_load(left_value, min_val=0, max_val=1)
                with pe.If(left > 0):
                    K, W = attr_parts[L], (We_raw, V1e_sb)[L]
                    with pe.Fori(0, TILES) as t:
                        pe.wait_ge(lf_attr_in[L], t * 16 + 16)
                        pe.wait_ge(lf_free[L], t + 1)
                        nc.tensor.matmul(lf_bank[:, :], attr[L][0:K, 0, 0:P], W[0:K, :], start=True,
                                         stop=True).then_inc(lf_mm[L], 1)
                        for b in range(BLOCKS):
                            pe.wait_ge(lf_hot_ready[L], t * BLOCKS + b + 1)
                            mm = nc.tensor.matmul(sum_bank[0][:, :], lf_hot[L][:, :], lf_msg[L][:, :], start=True, stop=True)
                            if L == 0:
                                mm = nc.tensor.matmul(misc[:, 0:2], lf_hot[L][:, :], ones[:, 0:2], start=True, stop=True)
                            mm.then_inc(lf_summed[L], 1)
                    pe.wait_ge(lf_added[L], LF_ALL)

            def turn_sums(L, stage, blocks):
                for b in blocks:
                    for q in range(3):
                        if b == blocks_of(q).start:
                            pe.wait_ge(stage_in[L][q], 16)
                    banks = len(turn_bank[L])
                    if b >= banks:
                        pe.wait_ge(turned_low[L], b - banks + 1)
                    for k in range(KD):
                        tr = nc.tensor.transpose(turn_bank[L][b % banks][:, k * P:(k + 1) * P], stage[:, b, k * P:(k + 1) * P],
                                                 ident[:, :])
                    tr.then_inc(turned[L], 1)

            def turning_product(L, stage, q, acc, terms, start):
                later = list(range(BLOCKS - len(terms), BLOCKS)) if q == 0 else []
                if q == 0:
                    turn_sums(L, stage, range(BLOCKS - len(terms)))
                pe.wait_ge(turned_low[L], blocks_of(q).stop)
                for k, term in enumerate(terms):
                    mm = product(acc, [term], start=start and k == 0, stop=k == len(terms) - 1)
                    turn_sums(L, stage, later[k:k + 1])
                return mm

            pe.wait_ge(pool_consts, 4)
            pe.wait_ge(dst_ready, 1)
            nc.tensor.matmul(misc[:, 0:GROUPS], ones[0:1, :], dst_f[0:1, 0:TILES:GROUP], start=True,
                             stop=True).then_inc(base_ready, 1)
            pe.wait_ge(left_ready, 1)
            nc.tensor.matmul(misc[0:1, 16:17], left_n[:, 0:1], ones[:, 0:1], start=True, stop=True).then_inc(left_counted, 1)
            pe.wait_ge(we_split, 1)
            edges(0)
            leftover(0)
            pe.wait_ge(pool_consts, 5)

            n = 0
            for W_hi, W_lo, X_hi, X_lo, K, M in ((W1_hi, W1_lo, h_hi, h_lo, KD, KH), (W2_hi, W2_lo, s_hi, s_lo, KH, KD)):
                def terms(m, q, chunks):
                    ms, (a, w) = slice(m * P, (m + 1) * P), NODE_CHUNKS[q]
                    return [(W_hi[:, k, ms], W_lo[:, k, ms], X_hi[:, k, a:a + w], X_lo[:, k, a:a + w]) for k in chunks]

                each = [(m, q) for m in range(M) for q in range(3)]
                early = 6 if K == KH else 0
                if early:
                    pe.wait_ge(w2_split, KH)
                    pe.wait_ge(s_split, KH - 2)
                    for i, (m, q) in enumerate(each[:early]):
                        pe.wait_ge(mlp_out, n + i - 5)
                        product(bank[2 + (n + i) % 6][:, 0:NODE_CHUNKS[q][1]], terms(m, q, range(K - 2)), stop=False)
                    pe.wait_ge(s_split, KH)
                for i, (m, q) in enumerate(each):
                    if K == KD and q == 0:
                        pe.wait_ge(w1_split, m + 1)
                    if n >= 6 and i >= early:
                        pe.wait_ge(mlp_out, n - 5)
                    acc = bank[2 + n % 6][:, 0:NODE_CHUNKS[q][1]]
                    if K == KD and m == 0:
                        turning_product(0, stage0, q, acc, terms(m, q, range(K)), True).then_inc(mlp_mm, 1)
                    elif i < early:
                        product(acc, terms(m, q, [K - 2, K - 1]), start=False).then_inc(mlp_mm, 1)
                    else:
                        product(acc, terms(m, q, range(K))).then_inc(mlp_mm, 1)
                    n += 1

            pe.wait_ge(mlp_out, 3 * (KH + KD))
            for t in range(BLOCKS + 3):
                if t < BLOCKS:
                    r = rows_in(t)
                    for q in range(3):
                        if t == blocks_of(q).start:
                            pe.wait_ge(silu_done, KH + KD + q)
                    if t >= 2:
                        pe.wait_ge(back_added, t - 1)
                    for k in range(KD):
                        tr = nc.tensor.transpose(bank[t % 2][0:r, k * P:(k + 1) * P], y_t[:, k, t * P:t * P + r], ident[:, :])
                    tr.then_inc(back_turned, 1)
                b = t - 2
                if 0 <= b < BLOCKS:
                    r = rows_in(b)
                    pe.wait_ge(x1_ready, b + 1)
                    if b >= 2:
                        pe.wait_ge(x1_low, b - 1)
                    for k in range(KD):
                        tr = nc.tensor.transpose(bank[2 + b % 2][:, k * P:k * P + r], rows[0:r, b, k * P:(k + 1) * P],
                                                 ident[0:r, 0:r])
                    tr.then_inc(x1_turned, 1)
                b = t - 3
                if b >= 0:
                    r = rows_in(b)
                    pe.wait_ge(x1_low, b + 1)
                    if b == 0:
                        pe.wait_ge(v1h_split, 1)
                    if b >= 2:
                        pe.wait_ge(table_ready, b - 1)
                    product(bank[4 + b % 2][0:r, :],
                            [(x1_hi[:, k, b * P:b * P + r], x1_lo[:, k, b * P:b * P + r], V1h_hi[:, k, :], V1h_lo[:, k, :])
                             for k in range(KD)]).then_inc(table_mm, 1)
            pe.wait_ge(table_ready, BLOCKS)
            pe.wait_ge(degree_in, 16)
            for i in range(0, BLOCKS, KD):
                if i == 2 * KD:
                    pe.wait_ge(degree_turned, 1)
                for b in range(i, min(i + KD, BLOCKS)):
                    tr = nc.tensor.transpose(degree_bank[i // KD % 2][0:2, (b - i) * P:(b - i + 1) * P],
                                             degree[:, 2 * b:2 * b + 2], ident[:, :])
                tr.then_inc(degree_mm, 1)
            pe.wait_ge(v1e_split, 1)
            edges(1)
            leftover(1)

            def gate(m, q, source, g):
                X_hi, X_lo = ((m_hi, m_lo), (x1_hi, x1_lo))[source]
                a, w = NODE_CHUNKS[q]
                return [(Wg_hi[m % 2][:, source, k, g, :], Wg_lo[m % 2][:, source, k, g, :],
                         X_hi[:, k, a:a + w], X_lo[:, k, a:a + w]) for k in range(KD)]

            pe.wait_ge(edge_out[1], TILES)
            pe.wait_ge(wh_split, 1)
            w = NODE_CHUNKS[0][1]
            product(bank[1][:, 0:w], gate(0, 0, 1, 2)).then_inc(gate_mm, 1)
            product(bank[0][:, 0:w], gate(0, 0, 1, 0), stop=False)
            product(bank[3][:, 0:w], gate(0, 0, 1, 1), stop=False)

            n = 0
            for m in range(KD):
                ms = slice(m * P, (m + 1) * P)
                pe.wait_ge(v2_split, m + 1)
                for q, (a, w) in enumerate(NODE_CHUNKS):
                    if m == 0:
                        pe.wait_ge(vb2_split, 1)
                    if n >= 3:
                        pe.wait_ge(m_low, n - 2)
                    acc = bank[4 + n % 3][:, 0:w]
                    nc.tensor.matmul(acc, v_b2_hi[0:1, ms], deg_r[0:1, a:a + w], start=True, stop=False)
                    nc.tensor.matmul(acc, v_b2_lo[0:1, ms], deg_r[0:1, a:a + w], start=False, stop=False)
                    terms = [(V2_hi[:, k, ms], V2_lo[:, k, ms], r_hi[:, k, a:a + w], r_lo[:, k, a:a + w]) for k in range(KD)]
                    mm = turning_product(1, stage1, q, acc, terms, False) if m == 0 else product(acc, terms, start=False)
                    mm.then_inc(m_mm, 1)
                    n += 1

            def turn_back(blocks):
                for b in blocks:
                    r = rows_in(b)
                    if b >= 8:
                        pe.wait_ge(fin_added, b - 3)
                    for k in range(KD):
                        tr = nc.tensor.transpose(last_bank[b][0:r, k * P:(k + 1) * P], bn_t[:, k, b * P:b * P + r], ident[:, :])
                    tr.then_inc(fin_turned, 1)

            n = 0
            for m in range(KD):
                pe.wait_ge(wg_split, m + 1)
                for a, w in NODE_CHUNKS:
                    if n >= 2:
                        pe.wait_ge(z_done, n - 1)
                        pe.wait_ge(n_in, n - 1)
                    four = bank[4 * (n % 2):4 * (n % 2) + 4]
                    q = n % 3
                    if n == 1:
                        pe.wait_ge(m_low, 3 * KD - 1)
                    if n == 3 * KD - 1:
                        pe.wait_ge(fin_added, 1)
                    if n:
                        product(four[1][:, 0:w], gate(m, q, 1, 2)).then_inc(gate_mm, 1)
                    if n == 3 * KD - 1:
                        pe.wait_ge(fin_added, 2)
                    if n:
                        product(four[0][:, 0:w], gate(m, q, 1, 0), stop=False)
                    if m == 0:
                        pe.wait_ge(m_low, 3 * (KD - 1) + q + 1)
                    product(four[0][:, 0:w], gate(m, q, 0, 0), start=False).then_inc(gate_mm, 1)
                    if n >= 3 * KD - 2:
                        pe.wait_ge(gru_done, n)
                        turn_back(blocks_of(q - 1))
                    if n == 3 * KD - 1:
                        pe.wait_ge(fin_added, 3)
                    if n == 1:
                        pe.wait_ge(m_low, 3 * KD)
                    product(four[2][:, 0:w], gate(m, q, 0, 2)).then_inc(gate_mm, 1)
                    if n == 3 * KD - 1:
                        pe.wait_ge(fin_added, 4)
                    if n:
                        product(four[3][:, 0:w], gate(m, q, 1, 1), stop=False)
                    product(four[3][:, 0:w], gate(m, q, 0, 1), start=False).then_inc(gate_mm, 1)
                    n += 1
            pe.wait_ge(gru_done, n)
            turn_back(blocks_of(2))

        @block.scalar
        def _(act):
            def copy(to, of):
                return nc.scalar.activation(to, of, ACT.Copy)

            def window_out(L, g, slot, first):
                act.wait_ge(summed[L], g * GROUP)
                if not first:
                    act.wait_ge(accumulated[L], 16 * (g - 2))
                if L == 0:
                    copy(sums[0][:, slot, D:D + 2], degree_bank[slot][:, 0:2])
                copy(sums[L][:, slot, 0:D], sum_bank[slot][:, :]).then_inc(sum_out[L], 1)

            def high_features(L, it, c):
                act.wait_ge(attr_in[L][c % RING], (it * (CPS // RING) + c // RING + 1) * (32, 16)[L])
                wait(act, edge_mm[L], it * STEP + (c - RING + 1) * CHUNK)
                copy((attr_hl, attr_hi)[L][:, c % RING, :], attr[L][:, c % RING, :]).then_inc(attr_high[L], 1)

            def message_high(L, it, t):
                if relu_on_dve(t):
                    return
                wait_gathered(act, L, it, t)
                wait(act, summed[L], it * STEP + t - MSG + 1)
                nc.scalar.activation(msg_hi[L][:, t % MSG, :], raw[L][:, t % RAW, :], ACT.Relu).then_inc(relued_act[L], 1)

            def edge_step(L, it, first):
                for j in range(STEP):
                    if j % CHUNK == 0:
                        high_features(L, it, j // CHUNK + 1)
                    act.wait_ge(edge_mm[L], it * STEP + j + 1)
                    wait(act, low[L], it * STEP + j - RAW + 1)
                    copy(raw[L][:, j % RAW, :], e_bank[j % EDGE_BANKS][:, :]).then_inc(edge_out[L], 1)
                    if not first or j >= RELU_LAG:
                        message_high(L, it, j - RELU_LAG)
                    if j % GROUP == SUM_LAG and (not first or j > GROUP):
                        window_out(L, it * 2 + j // GROUP, 1 - j // GROUP, first)

            def edges(L):
                high_features(L, 0, 0)
                edge_step(L, 0, True)
                with act.Fori(1, STEPS) as it:
                    edge_step(L, it, False)
                for t in range(STEP - RELU_LAG, STEP):
                    message_high(L, STEPS - 1, t)
                window_out(L, GROUPS, 1, False)
                act.wait_ge(flag_ready, 1)
                left = act.value_load(left_value, min_val=0, max_val=1)
                with act.If(left > 0):
                    act.wait_ge(lf_added[L], LF_ALL)

            def high_of_turned(L, hi):
                for b in range(BLOCKS):
                    r = rows_in(b)
                    act.wait_ge(turned[L], b + 1)
                    copy(hi[:, :, b * P:b * P + r], feature_major(turn_bank[L][b % len(turn_bank[L])])[:, :, 0:r]).then_inc(turned_high[L], 1)

            edges(0)
            high_of_turned(0, h_hi)

            def silu(c):
                act.wait_ge(bn_ready, c + 1)
                to = pre[:, c % 2, :] if c < KH else y_t[:, c - KH, :]
                at4 = 4 * (c % 2)
                for a, w in NODE_CHUNKS if c == KH + KD - 1 else [(0, N)]:
                    nc.scalar.activation(to[:, a:a + w], pre[:, c % 2, a:a + w], ACT.Silu, scale=moments[:, at4 + 2:at4 + 3],
                                         bias=moments[:, at4 + 3:at4 + 4]).then_inc(silu_done, 1)

            n = 0
            for c in range(KH + KD):
                if c == KH:
                    silu(c - 1)
                for q, (a, w) in enumerate(NODE_CHUNKS):
                    act.wait_ge(mlp_mm, n + 1)
                    if c >= 2 and q == 0:
                        act.wait_ge(s_split, min(c - 1, KH))
                        act.wait_ge(silu_done, c - 1)
                    nc.scalar.activation(pre[:, c % 2, a:a + w], bank[2 + n % 6][:, 0:w], ACT.Identity,
                                         bias=vec("b1", c) if c < KH else vec("b2", c - KH)).then_inc(mlp_out, 1)
                    n += 1
                    if q == 0 and c not in (0, KH):
                        silu(c - 1)
            silu(KH + KD - 1)
            for b in range(BLOCKS):
                r = rows_in(b)
                act.wait_ge(x1_turned, b + 1)
                copy(x1_hi[:, :, b * P:b * P + r], feature_major(bank[2 + b % 2])[:, :, 0:r]).then_inc(x1_high, 1)
            for i in range(0, BLOCKS, KD):
                w = min(KD * P, N - i * P)
                act.wait_ge(degree_mm, i // KD + 1)
                copy(deg_r[:, i * P:i * P + w], degree_bank[i // KD % 2][0:2, 0:w]).then_inc(degree_turned, 1)
            edges(1)
            high_of_turned(1, r_hi)
            n = 0
            for m in range(KD):
                for a, w in NODE_CHUNKS:
                    act.wait_ge(m_mm, n + 1)
                    copy(m_hi[:, m, a:a + w], bank[4 + n % 3][:, 0:w]).then_inc(m_high, 1)
                    n += 1
            act.wait_ge(gate_bias_ready, 1)

            def last_norm(blocks):
                for b in blocks:
                    r, at4 = rows_in(b), 4 * (b % 2)
                    act.wait_ge(fin_bias, b + 1)
                    if b >= 2:
                        act.wait_ge(fin_out[b % 2], 16 * (b // 2))
                    nc.scalar.activation(fin[0:r, b % 2, :], last[0:r, b % 2, :], ACT.Identity,
                                         scale=moments[0:r, at4 + 2:at4 + 3],
                                         bias=moments[0:r, at4 + 3:at4 + 4]).then_inc(fin_ready, 1)

            n = 0
            for m in range(KD):
                for a, w in NODE_CHUNKS:
                    four = bank[4 * (n % 2):4 * (n % 2) + 4]
                    act.wait_ge(gate_mm, 4 * n + 2)
                    if n >= 2:
                        act.wait_ge(gru_done, n - 1)
                    nc.scalar.activation(g_r[:, n % 2, 0:w], four[0][:, 0:w], ACT.Sigmoid,
                                         bias=gate_bias[:, m:m + 1]).then_inc(r_done, 1)
                    if n >= 3 * KD - 2:
                        last_norm(blocks_of(n % 3 - 1))
                    act.wait_ge(n_in, n + 1)
                    if n:
                        act.wait_ge(gru_done, n)
                    nc.scalar.activation(g_n[:, 0:w], g_r[:, n % 2, 0:w], ACT.Tanh,
                                         bias=vec("b_ih", 2 * KD + m)).then_inc(n_done, 1)
                    act.wait_ge(gate_mm, 4 * n + 4)
                    nc.scalar.activation(g_z[:, n % 2, 0:w], four[3][:, 0:w], ACT.Sigmoid,
                                         bias=gate_bias[:, KD + m:KD + m + 1]).then_inc(z_done, 1)
                    n += 1
            last_norm(blocks_of(2))

        @block.vector
        def _(dve):
            steps = [0]

            def link(ins):
                steps[0] += 1
                ins.then_inc(dve_step, 1)
                dve.wait_ge(dve_step, steps[0])

            def low_part(to, value, high):
                return nc.vector.tensor_tensor(to, value, high.bitcast(F32), ALU.subtract)

            def split(hi, lo, raw):
                link(nc.vector.tensor_copy(hi, raw))
                return low_part(lo, raw, hi)

            def count_left():
                link(nc.vector.tensor_scalar(dst_left[:, :], in_window[:, :], 0.0, None, ALU.is_lt))
                link(nc.vector.scalar_tensor_tensor(dst_left[:, :], in_window[:, :], float(P - 1), dst_left[:, :],
                                                    ALU.is_gt, ALU.add))
                link(nc.vector.scalar_tensor_tensor(dst_left[:, :], dst_f[:, :], 0.0, dst_left[:, :], ALU.is_ge, ALU.mult))
                link(nc.vector.tensor_reduce(left_n[:, 0:1], dst_left[:, :], mybir.AxisListType.X, ALU.add))
                link(nc.vector.scalar_tensor_tensor(dst_left[:, :], dst_f[:, :], 1.0, dst_left[:, :], ALU.add, ALU.mult))
                link(nc.vector.tensor_scalar(dst_left[:, :], dst_left[:, :], -1.0, None, ALU.add))
                nc.vector.nop().then_inc(left_ready, 1)
                dve.wait_ge(left_counted, 1)
                nc.vector.tensor_scalar(any_left[0:1, :], misc[0:1, 16:17], 0.0, None, ALU.is_gt).then_inc(flag_ready, 1)

            dve.wait_ge(cols_in, 16)
            nc.vector.tensor_scalar(one_eps[:, :], vec("eps"), 1.0, None, ALU.add).then_inc(eps_ready, 1)
            dve.wait_ge(be_in, 16)
            for q in range(XQ):
                dve.wait_ge(x_in_done[q], 16)
                xs = slice(q * XB, (q + 1) * XB)
                nc.vector.tensor_tensor(xb[:, xs, :], x_in[:, xs, :], be_bc[:, :].unsqueeze(1).broadcast_to([P, XB, D]),
                                        ALU.add).then_inc(xb_ready, 1)
                if q == 1:
                    dve.wait_ge(idx_in, 32)
                    nc.vector.tensor_copy(dst_f[:, :], dst_i[:, :]).then_inc(dst_ready, 1)
            dve.wait_ge(we_in, 32)
            split(We_hi[:, :], We_lo[:, :], We_raw[:, :]).then_inc(we_split, 1)
            dve.wait_ge(pool_consts, 4)
            nc.vector.tensor_copy(iota_f[:, :], iota_i[:, :])
            nc.vector.tensor_copy(ones_r[:, :], ones[:, 0:2])
            dve.wait_ge(base_ready, 1)
            link(nc.vector.tensor_copy(base_sb[:, :], misc[:, 0:GROUPS]))
            by_group = [t[:, :].rearrange("p (g i) -> p g i", i=GROUP) for t in (in_window, dst_f)]
            link(nc.vector.tensor_tensor(*by_group, base_sb[:, :].unsqueeze(2).broadcast_to([P, GROUPS, GROUP]), ALU.subtract))
            nc.vector.memset(zero_rows[:, :], 0.0).then_inc(zero_ready, 1)
            dve.wait_ge(eps_ready, 1)
            dve.wait_ge(xb_ready, XQ)
            count_left()
            nc.vector.tensor_scalar(x_in[:, :, :], x_in[:, :, :], one_eps[:, 0:1], None, ALU.mult).then_inc(start_ready, 1)

            def low_features(L, it, c):
                dve.wait_ge(attr_high[L], it * CPS + c + 1)
                s = c % RING
                if L == 0:
                    i = low_part(attr_hl[ED0:P, s, :], attr[0][ED0:P, s, :], attr_hl[ED0:P, s, :])
                else:
                    i = low_part(attr_lo[:, s, :], attr[1][:, s, :], attr_hi[:, s, :])
                i.then_inc(attr_split[L], 1)

            def one_hots(L, it, c):
                wait(dve, summed[L], it * STEP + (c - HOT + 1) * CHUNK)
                nodes = iota_f[:, :].unsqueeze(1).broadcast_to([P, CHUNK, P])
                own = in_window[:, bass.ds(it * STEP + c * CHUNK, CHUNK)].unsqueeze(2).broadcast_to([P, CHUNK, P])
                nc.vector.tensor_tensor(hot[L][:, c % HOT, :, :], nodes, own, ALU.is_equal).then_inc(hot_ready[L], 1)

            def message_parts(L, it, t):
                wait_gathered(dve, L, it, t)
                wait(dve, summed[L], it * STEP + t - MSG + 1)
                if relu_on_dve(t):
                    nc.vector.tensor_scalar(msg_hi[L][:, t % MSG, :], raw[L][:, t % RAW, :], 0.0, None,
                                            ALU.max).then_inc(relued_dve[L], 1)
                    dve.wait_ge(relued_dve[L], it * (STEP // 3) + t // 3 + 1)
                else:
                    dve.wait_ge(relued_act[L], it * (STEP - STEP // 3) + t - t // 3)
                nc.vector.scalar_tensor_tensor(msg_lo[L][:, t % MSG, :], raw[L][:, t % RAW, :], 0.0,
                                               msg_hi[L][:, t % MSG, :].bitcast(F32), ALU.max,
                                               ALU.subtract).then_inc(low[L], 1)

            W1_FIRST = KH - 2

            def split_w1(m):
                ms = slice(m * P, (m + 1) * P)
                split(W1_hi[:, :, ms], W1_lo[:, :, ms], W1_raw[:, :, ms]).then_inc(w1_split, 1)

            def split_w2(k):
                split(W2_hi[:, k, :], W2_lo[:, k, :], W2_raw[:, k, :]).then_inc(w2_split, 1)

            def split_v2(m):
                ms = slice(m * P, (m + 1) * P)
                split(V2_hi[:, :, ms], V2_lo[:, :, ms], V2_raw[:, :, ms]).then_inc(v2_split, 1)

            def indices(L, it, group):
                first_tile = it * STEP + group * GROUP
                half = group % 2 * GROUP
                nc.vector.tensor_copy(idx_now[:, half:half + GROUP],
                                      src_sb[:, bass.ds(first_tile, GROUP)]).then_inc(idx_copied[L], 1)

            def edge_step(L, it, first):
                for j in range(STEP):
                    c = j // CHUNK
                    if j % CHUNK == 0:
                        low_features(L, it, c + 1)
                    if not first or j >= RELU_LAG:
                        message_parts(L, it, j - RELU_LAG)
                    if j % GROUP == RELU_LAG:
                        indices(L, it, j // GROUP + 1)
                    if j % CHUNK == 2:
                        one_hots(L, it, c)

            def edges(L):
                indices(L, 0, 0)
                low_features(L, 0, 0)
                edge_step(L, 0, True)
                with dve.Fori(1, STEPS) as it:
                    edge_step(L, it, False)
                for t in range(STEP - RELU_LAG, STEP):
                    message_parts(L, STEPS - 1, t)
                leftover(L)

            def leftover(L):
                dve.wait_ge(flag_ready, 1)
                left = dve.value_load(left_value, min_val=0, max_val=1)
                with dve.If(left > 0):
                    dve.wait_ge(accumulated[L], 16 * GROUPS)
                    nc.vector.nop().then_inc(lf_free[L], 1)
                    with dve.Fori(0, TILES) as t:
                        dve.wait_ge(lf_gathered[L], t * 16 + 16)
                        dve.wait_ge(lf_mm[L], t + 1)
                        nc.vector.tensor_copy(lf_dst[:, :], dst_left[:, bass.ds(t, 1)]).then_inc(lf_msg_steps[L], 1)
                        nc.vector.tensor_tensor(lf_msg[L][:, :], lf_bank[:, :], raw[L][:, 0, :],
                                                ALU.add).then_inc(lf_msg_steps[L], 1)
                        dve.wait_ge(lf_msg_steps[L], t * 3 + 2)
                        nc.vector.tensor_scalar(lf_msg[L][:, :], lf_msg[L][:, :], 0.0, None,
                                                ALU.max).then_inc(lf_msg_steps[L], 1)
                        dve.wait_ge(lf_msg_steps[L], t * 3 + 3)
                        for b in range(BLOCKS):
                            nc.vector.tensor_scalar(lf_hot[L][:, :], iota_f[:, :], float(b * P), lf_dst[:, 0:1], ALU.add,
                                                    ALU.is_equal).then_inc(lf_hot_ready[L], 1)
                            dve.wait_ge(lf_summed[L], t * BLOCKS + b + 1)
                            if b:
                                dve.wait_ge(lf_added[L], t * (16 * BLOCKS) + 16 * b)
                            if L == 0:
                                nc.vector.tensor_copy(sums[0][:, 0, D:D + 2], misc[:, 0:2])
                            nc.vector.tensor_copy(sums[L][:, 0, 0:D], sum_bank[0][:, :]).then_inc(lf_copied[L], 1)
                        dve.wait_ge(lf_added[L], t * (16 * BLOCKS) + 16 * BLOCKS)
                        nc.vector.nop().then_inc(lf_free[L], 1)

            def low_of_turned(L, hi, lo):
                for b in range(BLOCKS):
                    r = rows_in(b)
                    dve.wait_ge(turned_high[L], b + 1)
                    low_part(lo[:, :, b * P:b * P + r], feature_major(turn_bank[L][b % len(turn_bank[L])])[:, :, 0:r],
                             hi[:, :, b * P:b * P + r]).then_inc(turned_low[L], 1)

            def add_stats(slot, parts, q, value):
                at = slot * 18 + q * 6
                return nc.vector.bn_stats(stats[0:parts, at:at + 6], value)

            def variance(slot, parts, n):
                link(nc.vector.bn_aggr(moments[0:parts, slot * 4:slot * 4 + 2], stats[0:parts, slot * 18:slot * 18 + 6 * n]))
                at4 = slot * 4 + 1
                nc.vector.tensor_scalar(moments[0:parts, at4:at4 + 1], moments[0:parts, at4:at4 + 1], EPS, None,
                                        ALU.add).then_inc(var_ready, 1)

            edges(0)
            dve.wait_ge(w1_in, 32)
            for m in range(W1_FIRST):
                split_w1(m)
            low_of_turned(0, h_hi, h_lo)

            rstds = [0]

            def rstd_now():
                rstds[0] += 1
                dve.wait_ge(rstd_ready, rstds[0])

            def node_stats(c, q):
                a, w = NODE_CHUNKS[q]
                dve.wait_ge(mlp_out, 3 * c + q + 1)
                return add_stats(c % 2, P, q, pre[:, c % 2, a:a + w])

            def split_hidden(c):
                dve.wait_ge(silu_done, c + 1)
                split(s_hi[:, c, :], s_lo[:, c, :], pre[:, c % 2, :]).then_inc(s_split, 1)

            for c in range(KH + KD):
                for q in range(3):
                    if q or not 0 < c < KH:
                        i = node_stats(c, q)
                link(i)
                variance(c % 2, P, 3)
                if c == 0:
                    split_w1(W1_FIRST)
                elif c < 5:
                    if c == 1:
                        dve.wait_ge(w2_in, 16)
                    split_w2(2 * c - 2)
                rstd_now()
                at4 = 4 * (c % 2)
                g, beta = (vec("g1", c), vec("beta1", c)) if c < KH else (vec("g2", c - KH), vec("beta2", c - KH))
                link(nc.vector.tensor_tensor(moments[:, at4 + 2:at4 + 3], moments[:, at4 + 2:at4 + 3], g, ALU.mult))
                link(nc.vector.tensor_tensor(moments[:, at4 + 3:at4 + 4], moments[:, at4:at4 + 1], moments[:, at4 + 2:at4 + 3],
                                             ALU.mult))
                nc.vector.tensor_tensor(moments[:, at4 + 3:at4 + 4], beta, moments[:, at4 + 3:at4 + 4],
                                        ALU.subtract).then_inc(bn_ready, 1)
                if c < KH:
                    if c == 0:
                        split_w1(W1_FIRST + 1)
                    elif c < 5:
                        split_w2(2 * c - 1)
                    if c < KH - 1:
                        node_stats(c + 1, 0)
                    split_hidden(c)
                if c == KH:
                    dve.wait_ge(v1h_in, 16)
                    split(V1h_hi[:, :, :], V1h_lo[:, :, :], V1h_raw[:, :, :]).then_inc(v1h_split, 1)

            def normalize(to, parts, slot):
                rstd_now()
                return nc.vector.tensor_scalar(to, lnx[0:parts, slot, :], moments[0:parts, slot * 4:slot * 4 + 1],
                                               moments[0:parts, slot * 4 + 2:slot * 4 + 3], ALU.subtract, ALU.mult)

            dve.wait_ge(rows_in_done, 16)
            dve.wait_ge(vb1_in, 16)
            for t in range(BLOCKS + 3):
                if t < BLOCKS:
                    r = rows_in(t)
                    dve.wait_ge(back_turned, t + 1)
                    if t == 1:
                        dve.wait_ge(silu_done, KH + KD + 2)
                    if t >= 2:
                        dve.wait_ge(x1_ready, t - 1)
                    i = nc.vector.tensor_tensor(lnx[0:r, t % 2, :], bank[t % 2][0:r, :], rows[0:r, t, :], ALU.add)
                    i.then_inc(back_added, 1)
                    dve.wait_ge(back_added, t + 1)
                    link(add_stats(t % 2, r, 0, lnx[0:r, t % 2, :]))
                    variance(t % 2, r, 1)
                b = t - 1
                if 0 <= b < BLOCKS:
                    r = rows_in(b)
                    normalize(rows[0:r, b, :], r, b % 2).then_inc(x1_ready, 1)
                b = t - 2
                if 0 <= b < BLOCKS:
                    r = rows_in(b)
                    dve.wait_ge(x1_high, b + 1)
                    low_part(x1_lo[:, :, b * P:b * P + r], feature_major(bank[2 + b % 2])[:, :, 0:r],
                             x1_hi[:, :, b * P:b * P + r]).then_inc(x1_low, 1)
                b = t - 3
                if b >= 0:
                    r = rows_in(b)
                    dve.wait_ge(table_mm, b + 1)
                    if b >= 2:
                        dve.wait_ge(table_out[b % 2], 16 * (b // 2))
                    nc.vector.tensor_tensor(table_sb[0:r, b % 2, :], bank[4 + b % 2][0:r, :], vb1_bc[0:r, :],
                                            ALU.add).then_inc(table_ready, 1)
            dve.wait_ge(wh_in, 16)
            wh = [t[:, 1, :, :, :].rearrange("p k g n -> p (k g n)") for t in (Wg_hi[0], Wg_lo[0])]
            split(*wh, Wh_raw[:, :]).then_inc(wh_split, 1)
            dve.wait_ge(v1e_in, 16)
            split(V1e_hi[:, :], V1e_lo[:, :], V1e_sb[:, :]).then_inc(v1e_split, 1)
            edges(1)
            dve.wait_ge(v2_in, 16)
            for m in range(KD):
                split_v2(m)
            dve.wait_ge(vb2_in, 16)
            split(v_b2_hi[:, :], v_b2_lo[:, :], v_b2_raw[:, :]).then_inc(vb2_split, 1)
            low_of_turned(1, r_hi, r_lo)

            def split_gates(m):
                dve.wait_ge(wg_in, 16 * (m + 1))
                parts = 1 if m == 0 else 2
                flat = (t[:, 0:parts, :, :, :].rearrange("p a k g n -> p (a k g n)") for t in (Wg_hi[m % 2], Wg_lo[m % 2]))
                split(*flat, Wg_raw[:, 0:parts * KD * 3 * P]).then_inc(wg_split, 1)

            n = 0
            for m in range(KD):
                for a, w in NODE_CHUNKS:
                    dve.wait_ge(m_high, n + 1)
                    low_part(m_lo[:, m, a:a + w], bank[4 + n % 3][:, 0:w], m_hi[:, m, a:a + w]).then_inc(m_low, 1)
                    n += 1
                    if n == 6:
                        split_gates(0)
            at_ih, at_hh = COLS["b_ih"][0], COLS["b_hh"][0]
            nc.vector.tensor_tensor(gate_bias[:, :], col[:, at_ih:at_ih + 2 * KD], col[:, at_hh:at_hh + 2 * KD],
                                    ALU.add).then_inc(gate_bias_ready, 1)
            at_var = COLS["run_var"][0]
            nc.vector.tensor_scalar(bn_scale[:, :], col[:, at_var:at_var + KD], EPS, None, ALU.add).then_inc(var_ready, 1)
            rstd_now()
            a = {name: COLS[name][0] for name in ("gamma", "beta", "run_mean")}
            link(nc.vector.tensor_tensor(bn_scale[:, :], bn_scale[:, :], col[:, a["gamma"]:a["gamma"] + KD], ALU.mult))
            link(nc.vector.tensor_tensor(bn_bias[:, :], bn_scale[:, :], col[:, a["run_mean"]:a["run_mean"] + KD], ALU.mult))
            link(nc.vector.tensor_tensor(bn_bias[:, :], col[:, a["beta"]:a["beta"] + KD], bn_bias[:, :], ALU.subtract))
            def last_blocks(blocks):
                def last_bias(b):
                    r, at4 = rows_in(b), 4 * (b % 2)
                    rstd_now()
                    nc.vector.scalar_tensor_tensor(moments[0:r, at4 + 3:at4 + 4], moments[0:r, at4:at4 + 1], -1.0,
                                                   moments[0:r, at4 + 2:at4 + 3], ALU.mult, ALU.mult).then_inc(fin_bias, 1)

                for b in blocks:
                    r = rows_in(b)
                    dve.wait_ge(fin_turned, b + 1)
                    if b >= 2:
                        dve.wait_ge(fin_ready, b - 1)
                    nc.vector.scalar_tensor_tensor(last[0:r, b % 2, :], rows[0:r, b, :], 2.0, last_bank[b][0:r, :], ALU.mult,
                                                   ALU.add).then_inc(fin_added, 1)
                    dve.wait_ge(fin_added, b + 1)
                    link(add_stats(b % 2, r, 0, last[0:r, b % 2, :]))
                    variance(b % 2, r, 1)
                    if b > blocks.start:
                        last_bias(b - 1)
                last_bias(blocks.stop - 1)

            n = 0
            for m in range(KD):
                for q, (a, w) in enumerate(NODE_CHUNKS):
                    if n >= 3 * KD - 2:
                        last_blocks(blocks_of(q - 1))
                    four = bank[4 * (n % 2):4 * (n % 2) + 4]
                    gr, gz, gn, gd = g_r[:, n % 2, 0:w], g_z[:, n % 2, 0:w], g_n[:, 0:w], g_d[:, 0:w]
                    dve.wait_ge(r_done, n + 1)
                    dve.wait_ge(gate_mm, 4 * n + 3)
                    link(nc.vector.scalar_tensor_tensor(gr, four[1][:, 0:w], vec("b_hh", 2 * KD + m), gr, ALU.add, ALU.mult))
                    nc.vector.tensor_tensor(gr, gr, four[2][:, 0:w], ALU.add).then_inc(n_in, 1)
                    dve.wait_ge(n_done, n + 1)
                    link(nc.vector.tensor_tensor(gd, x1_hi[:, m, a:a + w].bitcast(F32), gn, ALU.subtract))
                    link(nc.vector.tensor_tensor(gd, gd, x1_lo[:, m, a:a + w].bitcast(F32), ALU.add))
                    dve.wait_ge(z_done, n + 1)
                    link(nc.vector.tensor_tensor(gd, gd, gz, ALU.mult))
                    link(nc.vector.tensor_tensor(gd, gd, gn, ALU.add))
                    nc.vector.tensor_scalar(bn_t[:, m, a:a + w], gd, bn_scale[:, m:m + 1], bn_bias[:, m:m + 1],
                                            ALU.mult, ALU.add).then_inc(gru_done, 1)
                    n += 1
                    if q == 0 and m + 1 < KD:
                        split_gates(m + 1)
            last_blocks(blocks_of(2))


def kernel(**inputs):
    import numpy as np
    import concourse.bacc as bacc
    from concourse.bass_utils import run_bass_kernel_spmd

    a = {k: np.asarray(v) for k, v in inputs.items()}

    def by_tile(index, fill, tiles=TILES):
        full = np.full(tiles * P, fill, index.dtype)
        full[:E] = index
        return full.reshape(tiles, P).T

    def turned(attr):
        full = np.zeros((attr.shape[1], (TILES + CHUNK) * P), attr.dtype)
        full[:, :E] = attr.T
        return full

    x = np.zeros((BLOCKS * P, D), a["x"].dtype)
    x[:N] = a["x"]
    vectors = {"b1": a["L0_gnn_b1"], "g1": a["L0_gnn_g1"], "beta1": a["L0_gnn_beta1"], "b2": a["L0_gnn_b2"],
               "g2": a["L0_gnn_g2"], "beta2": a["L0_gnn_beta2"], "b_ih": a["L1_gnn_b_ih"], "b_hh": a["L1_gnn_b_hh"],
               "gamma": a["L1_gnn_gamma"], "beta": a["L1_gnn_beta"], "run_mean": a["L1_gnn_run_mean"],
               "run_var": a["L1_gnn_run_var"], "eps": np.full(P, a["L0_gnn_eps"])}
    gates = np.stack([a["L1_gnn_W_ih"], a["L1_gnn_W_hh"]]).reshape(2, 3, KD, P, KD, P)
    arrays = {
        "x": x,
        "src": by_tile(a["src"], 0, TILES + GROUP),
        "dst": by_tile(a["dst"], -1),
        "attr0": turned(a["edge_attr_64"]),
        "attr1": turned(a["edge_attr_128"]),
        "W_e": a["L0_gnn_W_e"],
        "b_e": a["L0_gnn_b_e"].reshape(1, D),
        "W1": a["L0_gnn_W1"],
        "W2": a["L0_gnn_W2"],
        "V1h": a["L1_gnn_W1"][:, :D].T,
        "V1e": a["L1_gnn_W1"][:, D:].T,
        "v_b1": a["L1_gnn_b1"].reshape(1, D),
        "V2": a["L1_gnn_W2"].T,
        "v_b2": a["L1_gnn_b2"].reshape(1, D),
        "Wg": gates.transpose(2, 5, 0, 4, 1, 3).reshape(KD, P, 2 * KD * 3 * P),
        "cols": np.concatenate([vectors[n].reshape(k, P).T for n, (_, k) in COLS.items()], axis=1),
    }
    arrays = {f"in_{k}": np.ascontiguousarray(v) for k, v in arrays.items()}
    nc = bacc.Bacc("TRN2", target_bir_lowering=False, num_devices=1)
    args = [nc.dram_tensor(k, v.shape, mybir.dt.from_np(v.dtype), kind="ExternalInput").ap() for k, v in arrays.items()]
    args.append(nc.dram_tensor("out", (N, D), F32, kind="ExternalOutput").ap())
    gnn_program(nc, *args)
    r = run_bass_kernel_spmd(nc, [arrays], core_ids=[0])
    return r.results[0]["out"]
```
